# Optimizing a Trainium2 kernel written in Bass

```python
import numpy as np
import jax
import jax.numpy as jnp

def _softmax(x, axis=-1):
    return jax.nn.softmax(x, axis=axis)

def _gelu(x):
    return jax.nn.gelu(x, approximate=True)

def _silu(x):
    return jax.nn.silu(x)

def _sigmoid(x):
    return jax.nn.sigmoid(x)

def _layernorm(x, axis=-1, eps=1e-05):
    m = jnp.mean(x, axis=axis, keepdims=True)
    v = jnp.var(x, axis=axis, keepdims=True)
    return (x - m) / jnp.sqrt(v + eps)

def _scatter_add(tgt, idx, src, axis=0):
    return tgt.at[idx].add(src)

def _segment_sum(src, seg, n):
    return jax.ops.segment_sum(src, seg, n)
kernel_name = 'mk_decoder_postln_d4_seqx_r4_daab03'

def setup_inputs(seed: int=0):
    np.random.seed(seed)
    _w = jnp.asarray

    def _rec_inputs():
        import jax
        import jax.numpy as jnp
        _rk = jax.random.key(seed)
        x = -0.000125 + 0.9999 * jax.random.normal(jax.random.fold_in(_rk, 1), (16, 128, 256), jnp.float32)
        _lenS = 128 - jax.random.randint(jax.random.fold_in(_rk, 7), (16,), 0, max(1, 128 // 4) + 1, jnp.int32)
        _lenS2 = 128 - jax.random.randint(jax.random.fold_in(_rk, 8), (16,), 0, max(1, 128 // 4) + 1, jnp.int32)
        _ctx_1024P = jax.random.normal(jax.random.fold_in(_rk, 11), (16, 16, 256), jnp.float32)
        _ctx_1024c = jax.random.dirichlet(jax.random.fold_in(_rk, 511), 0.3 * jnp.ones((16,), jnp.float32), (16, 128))
        _ctx_1024t = jnp.einsum('bsk,bkd->bsd', _ctx_1024c, _ctx_1024P)
        _ctx_1024t = _ctx_1024t * jax.lax.rsqrt(jnp.mean(jnp.square(_ctx_1024t)) + 1e-12) * 0.953939
        ctx_1024 = -1.52775e-05 + 0.999936 * (_ctx_1024t + 0.3 * jax.random.normal(jax.random.fold_in(_rk, 611), (16, 128, 256), jnp.float32))
        _validS = jnp.arange(128)[None, :] < _lenS[:, None]
        _validS2 = jnp.arange(128)[None, :] < _lenS2[:, None]
        _causal = jnp.tril(jnp.ones((128, 128), dtype=bool))
        mask_BxS2_bk1 = jnp.broadcast_to(_validS2[:, :], (16, 128))
        mask_BxSxS2_ff0 = jnp.where(jnp.ones((16, 128, 128), dtype=bool), 0.0, -1000000000.0).astype(jnp.float32)
        return (x, ctx_1024, mask_BxS2_bk1, mask_BxSxS2_ff0)
    x, ctx_1024, mask_BxS2_bk1, mask_BxSxS2_ff0 = _rec_inputs()

    def _L0_attn_setup():
        import jax, jax.numpy as jnp
        import numpy as np
        H, DK, DV, M = (8, 64, 64, 8)

        def _l2norm(x, eps=1e-06):
            return x * jax.lax.rsqrt(jnp.sum(x * x, axis=-1, keepdims=True) + eps)

        def _rotary(x, cos, sin):
            d = x.shape[-1] // 2
            x1, x2 = (x[..., :d], x[..., d:])
            c = cos[:, None]
            s = sin[:, None]
            return jnp.concatenate([x1 * c + x2 * s, -x1 * s + x2 * c], axis=-1)
        key = jax.random.key(seed)
        ks = jax.random.split(key, 11)
        B, T, D = (2, 512, 256)
        w = lambda k, shape, s=0.02: jax.random.normal(k, shape, jnp.float32) * s
        return {'hidden_states': jax.random.normal(ks[0], (B, T, D), jnp.float32), 'Wq': w(ks[1], (D, H * DK)), 'Wk': w(ks[2], (D, H * DK)), 'Wv': w(ks[3], (D, H * DV)), 'Wbeta': w(ks[4], (D, H * M)), 'Wtg': w(ks[5], (D, H * M)), 'mode_logits': w(ks[6], (H, M), 0.1), 'log_decay': w(ks[7], (H, M), 0.1), 'omega_log_scale': w(ks[8], (H, M), 0.1), 'Wg': w(ks[9], (D, H * DV)), 'Wo': w(ks[10], (H * DV, D))}
    _L0_attn_all = _L0_attn_setup()
    _L0_attn_in = {k: v for k, v in _L0_attn_all.items() if k in ('Wq', 'Wk', 'Wv', 'Wbeta', 'Wtg', 'mode_logits', 'log_decay', 'omega_log_scale', 'Wg', 'Wo')}
    del _L0_attn_all

    def _L0_xattn_setup():
        import jax, jax.numpy as jnp
        import numpy as np
        EPS = 1e-12

        def _l2_normalize(x, axis):
            n = jnp.sqrt(jnp.sum(x * x, axis=axis, keepdims=True))
            return x / jnp.maximum(n, EPS)
        key = jax.random.key(seed)
        ks = jax.random.split(key, 13)
        b, n, d, h = (8, 1024, 256, 16)
        scale = 0.02
        inp = {'query': jax.random.normal(ks[0], (b, n, d), jnp.float32), 'key': jax.random.normal(ks[1], (b, n, d), jnp.float32), 'value': jax.random.normal(ks[2], (b, n, d), jnp.float32), 'key_padding_mask': jax.random.randint(ks[3], (b, n), 0, 2).astype(bool), 'Wq': jax.random.normal(ks[4], (d, d), jnp.float32) * scale, 'bq': jax.random.normal(ks[5], (d,), jnp.float32) * scale, 'Wk': jax.random.normal(ks[6], (d, d), jnp.float32) * scale, 'bk': jax.random.normal(ks[7], (d,), jnp.float32) * scale, 'Wv': jax.random.normal(ks[8], (d, d), jnp.float32) * scale, 'bv': jax.random.normal(ks[9], (d,), jnp.float32) * scale, 'Wo': jax.random.normal(ks[10], (d, d), jnp.float32) * scale, 'bo': jax.random.normal(ks[11], (d,), jnp.float32) * scale}
        return inp
    _L0_xattn_all = _L0_xattn_setup()
    _L0_xattn_in = {k: v for k, v in _L0_xattn_all.items() if k in ('Wq', 'bq', 'Wk', 'bk', 'Wv', 'bv', 'Wo', 'bo')}
    del _L0_xattn_all

    def _L0_ffn_setup():
        import jax, jax.numpy as jnp
        import numpy as np
        D_MODEL = 256
        D_HIDDEN = 1024
        NUM_EXPERTS = 8
        B, T = (2, 512)
        key = jax.random.key(seed)
        ks = jax.random.split(key, 8)
        s = 0.02
        x = jax.random.normal(ks[0], (B, T, D_MODEL), dtype=jnp.float32)
        Wg = jax.random.normal(ks[1], (D_MODEL, NUM_EXPERTS), dtype=jnp.float32) * s
        bg = jnp.zeros((NUM_EXPERTS,), dtype=jnp.float32)
        W1 = jax.random.normal(ks[2], (NUM_EXPERTS, D_MODEL, D_HIDDEN), dtype=jnp.float32) * s
        b1 = jnp.zeros((NUM_EXPERTS, D_HIDDEN), dtype=jnp.float32)
        W2 = jax.random.normal(ks[3], (NUM_EXPERTS, D_HIDDEN, D_MODEL), dtype=jnp.float32) * s
        b2 = jnp.zeros((NUM_EXPERTS, D_MODEL), dtype=jnp.float32)
        return {'x': x, 'Wg': Wg, 'bg': bg, 'W1': W1, 'b1': b1, 'W2': W2, 'b2': b2}
    _L0_ffn_all = _L0_ffn_setup()
    _L0_ffn_in = {k: v for k, v in _L0_ffn_all.items() if k in ('Wg', 'bg', 'W1', 'b1', 'W2', 'b2')}
    del _L0_ffn_all

    def _L1_attn_setup():
        import jax, jax.numpy as jnp
        import numpy as np
        B, T, D, H = (2, 512, 256, 16)
        Dh = D // H

        def _rope(q, k):
            t = q.shape[2]
            dh = q.shape[3]
            inv_freq = 1.0 / 10000.0 ** (jnp.arange(0, dh, 2, dtype=jnp.float32) / dh)
            pos = jnp.arange(t, dtype=jnp.float32)
            freqs = pos[:, None] * inv_freq[None, :]
            sin = jnp.sin(freqs)[None, None]
            cos = jnp.cos(freqs)[None, None]

            def rot(x):
                xe, xo = (x[..., ::2], x[..., 1::2])
                re = xe * cos - xo * sin
                ro = xe * sin + xo * cos
                return jnp.stack([re, ro], axis=-1).reshape(x.shape)
            return (rot(q), rot(k))
        key = jax.random.key(seed)
        k1, k2, k3 = jax.random.split(key, 3)
        s = 1.0 / np.sqrt(D)
        return {'x': jax.random.normal(k1, (B, T, D), dtype=jnp.float32), 'w_qkv': jax.random.normal(k2, (3 * D, D), dtype=jnp.float32) * s, 'b_qkv': jnp.zeros((3 * D,), dtype=jnp.float32), 'w_out': jax.random.normal(k3, (D, D), dtype=jnp.float32) * s, 'b_out': jnp.zeros((D,), dtype=jnp.float32)}
    _L1_attn_all = _L1_attn_setup()
    _L1_attn_in = {k: v for k, v in _L1_attn_all.items() if k in ('w_qkv', 'b_qkv', 'w_out', 'b_out')}
    del _L1_attn_all

    def _L1_xattn_setup():
        import jax, jax.numpy as jnp
        import numpy as np
        NUM_HEADS = 16
        DIM = 256
        key = jax.random.key(seed)
        ks = jax.random.split(key, 12)
        B, N, T, C = (4, 1024, 77, DIM)
        s = 1.0 / np.sqrt(C)
        return {'hidden_states': jax.random.normal(ks[0], (B, N, C), jnp.float32), 'encoder_hidden_states': jax.random.normal(ks[1], (B, T, C), jnp.float32), 'attention_mask': jnp.zeros((B, N, T), jnp.float32), 'Wq': jax.random.normal(ks[2], (C, C), jnp.float32) * s, 'bq': jnp.zeros((C,), jnp.float32), 'Wk': jax.random.normal(ks[3], (C, C), jnp.float32) * s, 'bk': jnp.zeros((C,), jnp.float32), 'Wv': jax.random.normal(ks[4], (C, C), jnp.float32) * s, 'bv': jnp.zeros((C,), jnp.float32), 'Wo': jax.random.normal(ks[5], (C, C), jnp.float32) * s, 'bo': jnp.zeros((C,), jnp.float32)}
    _L1_xattn_all = _L1_xattn_setup()
    _L1_xattn_in = {k: v for k, v in _L1_xattn_all.items() if k in ('Wq', 'bq', 'Wk', 'bk', 'Wv', 'bv', 'Wo', 'bo')}
    del _L1_xattn_all

    def _L1_ffn_setup():
        import jax, jax.numpy as jnp
        import numpy as np
        QMAX = 127.0

        def _ste_round(v):
            return v + jax.lax.stop_gradient(jnp.round(v) - v)

        def _act_fake_quant(x, clip_factor):
            scale = jax.nn.sigmoid(clip_factor) * jnp.max(jnp.abs(x)) / QMAX
            return jnp.clip(_ste_round(x / scale), -QMAX - 1.0, QMAX) * scale

        def _weight_fake_quant(w):
            scale = jnp.max(jnp.abs(w), axis=1, keepdims=True) / QMAX
            return jnp.clip(_ste_round(w / scale), -QMAX - 1.0, QMAX) * scale
        key = jax.random.key(seed)
        k1, k2, k3, k4 = jax.random.split(key, 4)
        B, S, H, I = (8, 2048, 256, 704)
        return {'x': jax.random.normal(k1, (B, S, H), dtype=jnp.float32), 'clip_x': jnp.full((1,), 4.0, dtype=jnp.float32), 'clip_down': jnp.full((1,), 4.0, dtype=jnp.float32), 'w_gate': jax.random.normal(k2, (I, H), dtype=jnp.float32) * 0.02, 'w_up': jax.random.normal(k3, (I, H), dtype=jnp.float32) * 0.02, 'w_down': jax.random.normal(k4, (H, I), dtype=jnp.float32) * 0.02}
    _L1_ffn_all = _L1_ffn_setup()
    _L1_ffn_in = {k: v for k, v in _L1_ffn_all.items() if k in ('clip_x', 'clip_down', 'w_gate', 'w_up', 'w_down')}
    del _L1_ffn_all

    def _L2_attn_setup():
        import jax, jax.numpy as jnp
        import numpy as np
        from jax import lax
        D_MODEL = 256
        N_HEADS = 16
        FACTOR = 1
        key = jax.random.key(seed)
        ks = jax.random.split(key, 9)
        B, S, D = (8, 512, D_MODEL)
        x = jax.random.normal(ks[0], (B, S, D), dtype=jnp.float32)
        scale = 1.0 / np.sqrt(D)
        Wq = jax.random.normal(ks[1], (D, D), dtype=jnp.float32) * scale
        Wk = jax.random.normal(ks[2], (D, D), dtype=jnp.float32) * scale
        Wv = jax.random.normal(ks[3], (D, D), dtype=jnp.float32) * scale
        Wo = jax.random.normal(ks[4], (D, D), dtype=jnp.float32) * scale
        bq = jax.random.normal(ks[5], (D,), dtype=jnp.float32) * scale
        bk = jax.random.normal(ks[6], (D,), dtype=jnp.float32) * scale
        bv = jax.random.normal(ks[7], (D,), dtype=jnp.float32) * scale
        bo = jax.random.normal(ks[8], (D,), dtype=jnp.float32) * scale
        return {'x': x, 'Wq': Wq, 'bq': bq, 'Wk': Wk, 'bk': bk, 'Wv': Wv, 'bv': bv, 'Wo': Wo, 'bo': bo}
    _L2_attn_all = _L2_attn_setup()
    _L2_attn_in = {k: v for k, v in _L2_attn_all.items() if k in ('Wq', 'bq', 'Wk', 'bk', 'Wv', 'bv', 'Wo', 'bo')}
    del _L2_attn_all

    def _L2_xattn_setup():
        import jax, jax.numpy as jnp
        import numpy as np
        N_HEAD = 16
        key = jax.random.key(seed)
        ks = jax.random.split(key, 5)
        b, l, d = (4, 512, 256)
        dh = d // N_HEAD
        return {'q': jax.random.normal(ks[0], (b, l, d), dtype=jnp.float32), 'kv': jax.random.normal(ks[1], (b, l, d), dtype=jnp.float32), 'Wq': jax.random.normal(ks[2], (d, d), dtype=jnp.float32) * 0.02, 'Wkv': jax.random.normal(ks[3], (2 * dh, d), dtype=jnp.float32) * 0.02, 'Wc': jax.random.normal(ks[4], (d, d), dtype=jnp.float32) * 0.02}
    _L2_xattn_all = _L2_xattn_setup()
    _L2_xattn_in = {k: v for k, v in _L2_xattn_all.items() if k in ('Wq', 'Wkv', 'Wc')}
    del _L2_xattn_all

    def _L2_ffn_setup():
        import jax, jax.numpy as jnp
        import numpy as np
        HIDDEN = 256
        INNER = 1024

        def _weight_quant(w):
            scale = 1.0 / jnp.clip(jnp.mean(jnp.abs(w)), 1e-05)
            wq = jnp.clip(jnp.round(w * scale), -1.0, 1.0) / scale
            return w + jax.lax.stop_gradient(wq - w)

        def _act_quant(x):
            scale = 127.0 / jnp.clip(jnp.max(jnp.abs(x), axis=-1, keepdims=True), 1e-05)
            xq = jnp.clip(jnp.round(x * scale), -128.0, 127.0) / scale
            return x + jax.lax.stop_gradient(xq - x)

        def _bitlinear(x, w):
            return jnp.einsum('bsi,oi->bso', _act_quant(x), _weight_quant(w))
        key = jax.random.key(seed)
        k0, k1, k2, k3 = jax.random.split(key, 4)
        x = jax.random.normal(k0, (4, 512, HIDDEN), dtype=jnp.float32)
        w_gate = jax.random.normal(k1, (INNER, HIDDEN), dtype=jnp.float32) / np.sqrt(HIDDEN)
        w_up = jax.random.normal(k2, (INNER, HIDDEN), dtype=jnp.float32) / np.sqrt(HIDDEN)
        w_down = jax.random.normal(k3, (HIDDEN, INNER), dtype=jnp.float32) / np.sqrt(INNER)
        return {'x': x, 'w_gate': w_gate, 'w_up': w_up, 'w_down': w_down}
    _L2_ffn_all = _L2_ffn_setup()
    _L2_ffn_in = {k: v for k, v in _L2_ffn_all.items() if k in ('w_gate', 'w_up', 'w_down')}
    del _L2_ffn_all

    def _L3_attn_setup():
        import jax, jax.numpy as jnp
        import numpy as np
        B, T, D = (4, 512, 256)
        key = jax.random.key(seed)
        kx, kq, kk, kv = jax.random.split(key, 4)
        scale = 1.0 / np.sqrt(D)
        return {'x': jax.random.normal(kx, (B, T, D), dtype=jnp.float32), 'Wq': jax.random.normal(kq, (D, D), dtype=jnp.float32) * scale, 'Wk': jax.random.normal(kk, (D, D), dtype=jnp.float32) * scale, 'Wv': jax.random.normal(kv, (D, D), dtype=jnp.float32) * scale}
    _L3_attn_all = _L3_attn_setup()
    _L3_attn_in = {k: v for k, v in _L3_attn_all.items() if k in ('Wq', 'Wk', 'Wv')}
    del _L3_attn_all

    def _L3_xattn_setup():
        import jax, jax.numpy as jnp
        import numpy as np
        B, S, D, H = (1, 512, 256, 16)
        DH = D // H
        HID = 4 * D
        EPS = 1e-05
        NEG = -1000000000.0

        def _layernorm(x, g, b):
            mu = jnp.mean(x, axis=-1, keepdims=True)
            var = jnp.mean((x - mu) ** 2, axis=-1, keepdims=True)
            return (x - mu) * jax.lax.rsqrt(var + EPS) * g + b

        def _mha(x_q, x_kv, W, bias, causal):
            q = jnp.einsum('bsd,hde->bhse', x_q, W) + bias[None, :, None, :]
            k = jnp.einsum('bsd,hde->bhse', x_kv, W) + bias[None, :, None, :]
            v = jnp.einsum('bsd,hde->bhse', x_kv, W) + bias[None, :, None, :]
            scores = jnp.einsum('bhse,bhte->bhst', q, k) / jnp.sqrt(jnp.float32(DH))
            if causal:
                sq, sk = (scores.shape[-2], scores.shape[-1])
                mask = jnp.triu(jnp.ones((sq, sk), bool), k=1)
                scores = jnp.where(mask, NEG, scores)
            p = jax.nn.softmax(scores, axis=-1)
            out = jnp.einsum('bhst,bhte->bhse', p, v)
            b, h, s, e = out.shape
            return out.transpose(0, 2, 1, 3).reshape(b, s, h * e)
        key = jax.random.key(seed)
        ks = jax.random.split(key, 12)
        s = 0.02
        return {'y': jax.random.normal(ks[0], (B, S, D), jnp.float32), 'encoder_output': jax.random.normal(ks[1], (B, S, D), jnp.float32), 'Wq_self': jax.random.normal(ks[2], (H, D, DH), jnp.float32) * s, 'bq_self': jax.random.normal(ks[3], (H, DH), jnp.float32) * s, 'Wq_cross': jax.random.normal(ks[4], (H, D, DH), jnp.float32) * s, 'bq_cross': jax.random.normal(ks[5], (H, DH), jnp.float32) * s, 'g1': jnp.ones((D,), jnp.float32), 'beta1': jnp.zeros((D,), jnp.float32), 'g2': jnp.ones((D,), jnp.float32), 'beta2': jnp.zeros((D,), jnp.float32), 'g3': jnp.ones((D,), jnp.float32), 'beta3': jnp.zeros((D,), jnp.float32), 'w1': jax.random.normal(ks[6], (D, HID), jnp.float32) * s, 'b1': jax.random.normal(ks[7], (HID,), jnp.float32) * s, 'w2': jax.random.normal(ks[8], (HID, D), jnp.float32) * s, 'b2': jax.random.normal(ks[9], (D,), jnp.float32) * s}
    _L3_xattn_all = _L3_xattn_setup()
    _L3_xattn_in = {k: v for k, v in _L3_xattn_all.items() if k in ('Wq_self', 'bq_self', 'Wq_cross', 'bq_cross', 'g1', 'beta1', 'g2', 'beta2', 'g3', 'beta3', 'w1', 'b1', 'w2', 'b2')}
    del _L3_xattn_all

    def _L3_ffn_setup():
        import jax, jax.numpy as jnp
        import numpy as np
        B, S, H = (2, 256, 256)
        E, F = (16, 128)
        G, TOPK_G, TOPK = (4, 2, 4)
        N_SHARED = 2
        ROUTE_SCALE = 1.0
        FS = N_SHARED * F

        def _gate(x, w_gate):
            T = x.shape[0]
            scores = jax.nn.sigmoid(x @ w_gate.T)
            sv = scores.reshape(T, G, E // G)
            group_scores = jax.lax.top_k(sv, 2)[0].sum(-1)
            top_groups = jax.lax.top_k(group_scores, TOPK_G)[1]
            allowed = jnp.zeros((T, G), dtype=bool).at[jnp.arange(T)[:, None], top_groups].set(True)
            masked = jnp.where(allowed[:, :, None], sv, -jnp.inf).reshape(T, E)
            _, idx = jax.lax.top_k(masked, TOPK)
            w = jnp.take_along_axis(scores, idx, axis=1)
            w = w / (w.sum(-1, keepdims=True) + 1e-06) * ROUTE_SCALE
            return (w, idx)

        def _swiglu(x, w1, w3, w2):
            return jax.nn.silu(x @ w1.T) * (x @ w3.T) @ w2.T
        key = jax.random.key(seed)
        ks = jax.random.split(key, 8)
        scale = 0.02
        return {'hidden_states': jax.random.normal(ks[0], (B, S, H), dtype=jnp.float32), 'w_gate': jax.random.normal(ks[1], (E, H), dtype=jnp.float32) * scale, 'w1_e': jax.random.normal(ks[2], (E, F, H), dtype=jnp.float32) * scale, 'w3_e': jax.random.normal(ks[3], (E, F, H), dtype=jnp.float32) * scale, 'w2_e': jax.random.normal(ks[4], (E, H, F), dtype=jnp.float32) * scale, 'w1_s': jax.random.normal(ks[5], (FS, H), dtype=jnp.float32) * scale, 'w3_s': jax.random.normal(ks[6], (FS, H), dtype=jnp.float32) * scale, 'w2_s': jax.random.normal(ks[7], (H, FS), dtype=jnp.float32) * scale}
    _L3_ffn_all = _L3_ffn_setup()
    _L3_ffn_in = {k: v for k, v in _L3_ffn_all.items() if k in ('w_gate', 'w1_e', 'w3_e', 'w2_e', 'w1_s', 'w3_s', 'w2_s')}
    del _L3_ffn_all
    return {'x': x, 'ctx_1024': ctx_1024, 'mask_BxS2_bk1': mask_BxS2_bk1, 'mask_BxSxS2_ff0': mask_BxSxS2_ff0, 'L0_attn_Wq': _L0_attn_in['Wq'], 'L0_attn_Wk': _L0_attn_in['Wk'], 'L0_attn_Wv': _L0_attn_in['Wv'], 'L0_attn_Wbeta': _L0_attn_in['Wbeta'], 'L0_attn_Wtg': _L0_attn_in['Wtg'], 'L0_attn_mode_logits': _L0_attn_in['mode_logits'], 'L0_attn_log_decay': _L0_attn_in['log_decay'], 'L0_attn_omega_log_scale': _L0_attn_in['omega_log_scale'], 'L0_attn_Wg': _L0_attn_in['Wg'], 'L0_attn_Wo': _L0_attn_in['Wo'], 'L0_xattn_Wq': _L0_xattn_in['Wq'], 'L0_xattn_bq': _L0_xattn_in['bq'], 'L0_xattn_Wk': _L0_xattn_in['Wk'], 'L0_xattn_bk': _L0_xattn_in['bk'], 'L0_xattn_Wv': _L0_xattn_in['Wv'], 'L0_xattn_bv': _L0_xattn_in['bv'], 'L0_xattn_Wo': _L0_xattn_in['Wo'], 'L0_xattn_bo': _L0_xattn_in['bo'], 'L0_ffn_Wg': _L0_ffn_in['Wg'], 'L0_ffn_bg': _L0_ffn_in['bg'], 'L0_ffn_W1': _L0_ffn_in['W1'], 'L0_ffn_b1': _L0_ffn_in['b1'], 'L0_ffn_W2': _L0_ffn_in['W2'], 'L0_ffn_b2': _L0_ffn_in['b2'], 'L1_attn_w_qkv': _L1_attn_in['w_qkv'], 'L1_attn_b_qkv': _L1_attn_in['b_qkv'], 'L1_attn_w_out': _L1_attn_in['w_out'], 'L1_attn_b_out': _L1_attn_in['b_out'], 'L1_xattn_Wq': _L1_xattn_in['Wq'], 'L1_xattn_bq': _L1_xattn_in['bq'], 'L1_xattn_Wk': _L1_xattn_in['Wk'], 'L1_xattn_bk': _L1_xattn_in['bk'], 'L1_xattn_Wv': _L1_xattn_in['Wv'], 'L1_xattn_bv': _L1_xattn_in['bv'], 'L1_xattn_Wo': _L1_xattn_in['Wo'], 'L1_xattn_bo': _L1_xattn_in['bo'], 'L1_ffn_clip_x': _L1_ffn_in['clip_x'], 'L1_ffn_clip_down': _L1_ffn_in['clip_down'], 'L1_ffn_w_gate': _L1_ffn_in['w_gate'], 'L1_ffn_w_up': _L1_ffn_in['w_up'], 'L1_ffn_w_down': _L1_ffn_in['w_down'], 'L2_attn_Wq': _L2_attn_in['Wq'], 'L2_attn_bq': _L2_attn_in['bq'], 'L2_attn_Wk': _L2_attn_in['Wk'], 'L2_attn_bk': _L2_attn_in['bk'], 'L2_attn_Wv': _L2_attn_in['Wv'], 'L2_attn_bv': _L2_attn_in['bv'], 'L2_attn_Wo': _L2_attn_in['Wo'], 'L2_attn_bo': _L2_attn_in['bo'], 'L2_xattn_Wq': _L2_xattn_in['Wq'], 'L2_xattn_Wkv': _L2_xattn_in['Wkv'], 'L2_xattn_Wc': _L2_xattn_in['Wc'], 'L2_ffn_w_gate': _L2_ffn_in['w_gate'], 'L2_ffn_w_up': _L2_ffn_in['w_up'], 'L2_ffn_w_down': _L2_ffn_in['w_down'], 'L3_attn_Wq': _L3_attn_in['Wq'], 'L3_attn_Wk': _L3_attn_in['Wk'], 'L3_attn_Wv': _L3_attn_in['Wv'], 'L3_xattn_Wq_self': _L3_xattn_in['Wq_self'], 'L3_xattn_bq_self': _L3_xattn_in['bq_self'], 'L3_xattn_Wq_cross': _L3_xattn_in['Wq_cross'], 'L3_xattn_bq_cross': _L3_xattn_in['bq_cross'], 'L3_xattn_g1': _L3_xattn_in['g1'], 'L3_xattn_beta1': _L3_xattn_in['beta1'], 'L3_xattn_g2': _L3_xattn_in['g2'], 'L3_xattn_beta2': _L3_xattn_in['beta2'], 'L3_xattn_g3': _L3_xattn_in['g3'], 'L3_xattn_beta3': _L3_xattn_in['beta3'], 'L3_xattn_w1': _L3_xattn_in['w1'], 'L3_xattn_b1': _L3_xattn_in['b1'], 'L3_xattn_w2': _L3_xattn_in['w2'], 'L3_xattn_b2': _L3_xattn_in['b2'], 'L3_ffn_w_gate': _L3_ffn_in['w_gate'], 'L3_ffn_w1_e': _L3_ffn_in['w1_e'], 'L3_ffn_w3_e': _L3_ffn_in['w3_e'], 'L3_ffn_w2_e': _L3_ffn_in['w2_e'], 'L3_ffn_w1_s': _L3_ffn_in['w1_s'], 'L3_ffn_w3_s': _L3_ffn_in['w3_s'], 'L3_ffn_w2_s': _L3_ffn_in['w2_s']}

def reference(x, ctx_1024, mask_BxS2_bk1, mask_BxSxS2_ff0, L0_attn_Wq, L0_attn_Wk, L0_attn_Wv, L0_attn_Wbeta, L0_attn_Wtg, L0_attn_mode_logits, L0_attn_log_decay, L0_attn_omega_log_scale, L0_attn_Wg, L0_attn_Wo, L0_xattn_Wq, L0_xattn_bq, L0_xattn_Wk, L0_xattn_bk, L0_xattn_Wv, L0_xattn_bv, L0_xattn_Wo, L0_xattn_bo, L0_ffn_Wg, L0_ffn_bg, L0_ffn_W1, L0_ffn_b1, L0_ffn_W2, L0_ffn_b2, L1_attn_w_qkv, L1_attn_b_qkv, L1_attn_w_out, L1_attn_b_out, L1_xattn_Wq, L1_xattn_bq, L1_xattn_Wk, L1_xattn_bk, L1_xattn_Wv, L1_xattn_bv, L1_xattn_Wo, L1_xattn_bo, L1_ffn_clip_x, L1_ffn_clip_down, L1_ffn_w_gate, L1_ffn_w_up, L1_ffn_w_down, L2_attn_Wq, L2_attn_bq, L2_attn_Wk, L2_attn_bk, L2_attn_Wv, L2_attn_bv, L2_attn_Wo, L2_attn_bo, L2_xattn_Wq, L2_xattn_Wkv, L2_xattn_Wc, L2_ffn_w_gate, L2_ffn_w_up, L2_ffn_w_down, L3_attn_Wq, L3_attn_Wk, L3_attn_Wv, L3_xattn_Wq_self, L3_xattn_bq_self, L3_xattn_Wq_cross, L3_xattn_bq_cross, L3_xattn_g1, L3_xattn_beta1, L3_xattn_g2, L3_xattn_beta2, L3_xattn_g3, L3_xattn_beta3, L3_xattn_w1, L3_xattn_b1, L3_xattn_w2, L3_xattn_b2, L3_ffn_w_gate, L3_ffn_w1_e, L3_ffn_w3_e, L3_ffn_w2_e, L3_ffn_w1_s, L3_ffn_w3_s, L3_ffn_w2_s):
    import jax
    import jax.numpy as jnp

    def _L0_attn_ref(hidden_states, Wq, Wk, Wv, Wbeta, Wtg, mode_logits, log_decay, omega_log_scale, Wg, Wo):
        import jax, jax.numpy as jnp
        import numpy as np
        H, DK, DV, M = (8, 64, 64, 8)

        def _l2norm(x, eps=1e-06):
            return x * jax.lax.rsqrt(jnp.sum(x * x, axis=-1, keepdims=True) + eps)

        def _rotary(x, cos, sin):
            d = x.shape[-1] // 2
            x1, x2 = (x[..., :d], x[..., d:])
            c = cos[:, None]
            s = sin[:, None]
            return jnp.concatenate([x1 * c + x2 * s, -x1 * s + x2 * c], axis=-1)
        x = hidden_states
        B, T, D = x.shape
        q = (x @ Wq).reshape(B, T, H, DK)
        k = (x @ Wk).reshape(B, T, H, DK)
        v = (x @ Wv).reshape(B, T, H, DV)
        beta = jax.nn.sigmoid((x @ Wbeta).reshape(B, T, H, M))
        tg = jax.nn.sigmoid((x @ Wtg).reshape(B, T, H, M))
        pair = jnp.arange(0, DK, 2, dtype=jnp.float32)
        inv_freq = 1.0 / 10000.0 ** (pair / DK)
        omega_scale = jnp.exp(omega_log_scale)
        pos = jnp.arange(T, dtype=jnp.float32)
        angles = pos[:, None, None, None] * omega_scale[None, :, :, None] * inv_freq
        cos = jnp.transpose(jnp.cos(angles), (2, 0, 1, 3))
        sin = jnp.transpose(jnp.sin(angles), (2, 0, 1, 3))
        scale = DK ** (-0.5)
        qr = _l2norm(_rotary(q, cos, sin)) * scale
        kr = _l2norm(_rotary(k, cos, sin))
        rho = jnp.exp(-jax.nn.softplus(log_decay))
        g = jnp.log(jnp.clip(tg * rho, 1e-06))
        qt = jnp.transpose(qr, (2, 0, 1, 3, 4))
        kt = jnp.transpose(kr, (2, 0, 1, 3, 4))
        vt = jnp.transpose(v, (1, 0, 2, 3))
        gt = jnp.transpose(g, (1, 3, 0, 2))
        bt = jnp.transpose(beta, (1, 3, 0, 2))

        def step(S, inp):
            q_t, k_t, v_t, b_g, b_beta = inp
            S = S * jnp.exp(b_g)[..., None, None]
            kv = jnp.einsum('mbhk,mbhkv->mbhv', k_t, S)
            dv = (v_t[None] - kv) * b_beta[..., None]
            S = S + k_t[..., :, None] * dv[..., None, :]
            o_t = jnp.einsum('mbhk,mbhkv->mbhv', q_t, S)
            return (S, o_t)
        S0 = jnp.zeros((M, B, H, DK, DV), jnp.float32)
        _, ys = jax.lax.scan(step, S0, (qt, kt, vt, gt, bt))
        mode_w = jax.nn.softmax(mode_logits, axis=-1)
        o = jnp.einsum('tmbhv,hm->bthv', ys, mode_w)
        gate = jax.nn.sigmoid((x @ Wg).reshape(B, T, H, DV))
        o = o * gate
        return o.reshape(B, T, H * DV) @ Wo

    def _L0_xattn_ref(query, key, value, key_padding_mask, Wq, bq, Wk, bk, Wv, bv, Wo, bo):
        import jax, jax.numpy as jnp
        import numpy as np
        EPS = 1e-12

        def _l2_normalize(x, axis):
            n = jnp.sqrt(jnp.sum(x * x, axis=axis, keepdims=True))
            return x / jnp.maximum(n, EPS)
        b, n, d = query.shape
        h = 16
        dh = d // h
        q = query @ Wq.T + bq
        k = key @ Wk.T + bk
        v = value @ Wv.T + bv
        q = 1.0 + jax.nn.elu(q)
        k = 1.0 + jax.nn.elu(k)
        k = jnp.where(key_padding_mask[:, :, None], 0.0, k)
        q = q.reshape(b, n, h, dh).transpose(0, 2, 1, 3)
        k = k.reshape(b, n, h, dh).transpose(0, 2, 1, 3)
        v = v.reshape(b, n, h, dh).transpose(0, 2, 1, 3)
        q = _l2_normalize(q, axis=2)
        k = _l2_normalize(k, axis=3)
        kv = jnp.einsum('bhnd,bhne->bhde', k, v)
        out = jnp.einsum('bhnd,bhde->bhne', q, kv)
        out = out.transpose(0, 2, 1, 3).reshape(b, n, d)
        return out @ Wo.T + bo

    def _L0_ffn_ref(x, Wg, bg, W1, b1, W2, b2):
        import jax, jax.numpy as jnp
        import numpy as np
        D_MODEL = 256
        D_HIDDEN = 1024
        NUM_EXPERTS = 8
        B, T = (2, 512)
        gate_logits = jnp.einsum('btd,de->bte', x, Wg) + bg
        gate_scores = jax.nn.softmax(gate_logits, axis=-1)
        top1_idx = jnp.argmax(gate_scores, axis=-1)
        top1_mask = jax.nn.one_hot(top1_idx, NUM_EXPERTS, dtype=x.dtype)
        top1_weight = jnp.sum(gate_scores * top1_mask, axis=-1, keepdims=True)
        h = jax.nn.silu(jnp.einsum('btd,edh->bteh', x, W1) + b1)
        o = jnp.einsum('bteh,ehd->bted', h, W2) + b2
        y = jnp.sum(o * top1_mask[..., None], axis=2) * top1_weight
        return y

    def _L1_attn_ref(x, w_qkv, b_qkv, w_out, b_out):
        import jax, jax.numpy as jnp
        import numpy as np
        B, T, D, H = (2, 512, 256, 16)
        Dh = D // H

        def _rope(q, k):
            t = q.shape[2]
            dh = q.shape[3]
            inv_freq = 1.0 / 10000.0 ** (jnp.arange(0, dh, 2, dtype=jnp.float32) / dh)
            pos = jnp.arange(t, dtype=jnp.float32)
            freqs = pos[:, None] * inv_freq[None, :]
            sin = jnp.sin(freqs)[None, None]
            cos = jnp.cos(freqs)[None, None]

            def rot(x):
                xe, xo = (x[..., ::2], x[..., 1::2])
                re = xe * cos - xo * sin
                ro = xe * sin + xo * cos
                return jnp.stack([re, ro], axis=-1).reshape(x.shape)
            return (rot(q), rot(k))
        b, t, d = x.shape
        qkv = x @ w_qkv.T + b_qkv
        q, k, v = jnp.split(qkv, 3, axis=-1)
        q = q.reshape(b, t, H, Dh).transpose(0, 2, 1, 3)
        k = k.reshape(b, t, H, Dh).transpose(0, 2, 1, 3)
        v = v.reshape(b, t, H, Dh).transpose(0, 2, 1, 3)
        q, k = _rope(q, k)
        scores = jnp.einsum('bhtd,bhsd->bhts', q, k) / jnp.sqrt(jnp.float32(Dh))
        causal = jnp.tril(jnp.ones((t, t), dtype=bool))[None, None]
        scores = jnp.where(causal, scores, -jnp.inf)
        probs = jax.nn.softmax(scores, axis=-1)
        out = jnp.einsum('bhts,bhsd->bhtd', probs, v)
        out = out.transpose(0, 2, 1, 3).reshape(b, t, d)
        return out @ w_out.T + b_out

    def _L1_xattn_ref(hidden_states, encoder_hidden_states, attention_mask, Wq, bq, Wk, bk, Wv, bv, Wo, bo):
        import jax, jax.numpy as jnp
        import numpy as np
        NUM_HEADS = 16
        DIM = 256
        B, N, C = hidden_states.shape
        T = encoder_hidden_states.shape[1]
        H = NUM_HEADS
        D = C // H
        q = (hidden_states @ Wq.T + bq).reshape(B, N, H, D).transpose(0, 2, 1, 3)
        k = (encoder_hidden_states @ Wk.T + bk).reshape(B, T, H, D).transpose(0, 2, 1, 3)
        v = (encoder_hidden_states @ Wv.T + bv).reshape(B, T, H, D).transpose(0, 2, 1, 3)
        scale = 1.0 / jnp.sqrt(jnp.asarray(D, q.dtype))
        scores = jnp.einsum('bhnd,bhtd->bhnt', q, k) * scale + attention_mask[:, None, :, :]
        attn = jax.nn.softmax(scores, axis=-1)
        out = jnp.einsum('bhnt,bhtd->bhnd', attn, v)
        out = out.transpose(0, 2, 1, 3).reshape(B, N, C)
        return out @ Wo.T + bo

    def _L1_ffn_ref(x, clip_x, clip_down, w_gate, w_up, w_down):
        import jax, jax.numpy as jnp
        import numpy as np
        QMAX = 127.0

        def _ste_round(v):
            return v + jax.lax.stop_gradient(jnp.round(v) - v)

        def _act_fake_quant(x, clip_factor):
            scale = jax.nn.sigmoid(clip_factor) * jnp.max(jnp.abs(x)) / QMAX
            return jnp.clip(_ste_round(x / scale), -QMAX - 1.0, QMAX) * scale

        def _weight_fake_quant(w):
            scale = jnp.max(jnp.abs(w), axis=1, keepdims=True) / QMAX
            return jnp.clip(_ste_round(w / scale), -QMAX - 1.0, QMAX) * scale
        xq = _act_fake_quant(x, clip_x[0])
        gate = jnp.einsum('bsh,ih->bsi', xq, _weight_fake_quant(w_gate))
        up = jnp.einsum('bsh,ih->bsi', xq, _weight_fake_quant(w_up))
        h = _act_fake_quant(jax.nn.silu(gate) * up, clip_down[0])
        return jnp.einsum('bsi,hi->bsh', h, _weight_fake_quant(w_down))

    def _L2_attn_ref(x, Wq, bq, Wk, bk, Wv, bv, Wo, bo):
        import jax, jax.numpy as jnp
        import numpy as np
        from jax import lax
        D_MODEL = 256
        N_HEADS = 16
        FACTOR = 1
        B, S, D = x.shape
        H = N_HEADS
        dk = D // H
        topk = S * FACTOR

        def proj(W, b):
            y = x @ W + b
            return y.reshape(B, S, H, dk).transpose(0, 2, 1, 3)
        Q = proj(Wq, bq)
        K = proj(Wk, bk)
        V = proj(Wv, bv)
        qf = jnp.fft.rfft(Q, axis=-2)
        kf = jnp.fft.rfft(K, axis=-2)
        corr = jnp.fft.irfft(qf * jnp.conj(kf), n=S, axis=-2)
        w = lax.top_k(corr.transpose(0, 1, 3, 2), topk)[0]
        w = w.transpose(0, 1, 3, 2)
        w = jax.nn.softmax(w, axis=-2)
        out = jnp.einsum('bhti,bhij->bhtj', w, V[:, :, :dk, :])
        ctx = out.transpose(0, 2, 1, 3).reshape(B, topk, D)
        return ctx @ Wo + bo

    def _L2_xattn_ref(q, kv, Wq, Wkv, Wc):
        import jax, jax.numpy as jnp
        import numpy as np
        N_HEAD = 16
        b, l, d = q.shape
        h = N_HEAD
        dh = d // h
        qp = jnp.einsum('bld,ed->ble', q, Wq)
        scores = jnp.einsum('bld,bmd->blm', qp, kv)
        idx = jnp.argmax(scores, axis=-1)
        mem = jnp.take_along_axis(kv, idx[..., None], axis=1)
        mkv = jnp.einsum('bld,ed->ble', mem, Wkv)
        mk, mv = jnp.split(mkv, 2, axis=-1)
        qh = qp.reshape(b, l, h, dh).transpose(0, 2, 1, 3)
        scale = 1.0 / np.sqrt(dh).astype(np.float32)
        logits = jnp.einsum('bhld,bmd->bhlm', qh, mk) * scale
        attn = jax.nn.softmax(logits, axis=-1)
        out = jnp.einsum('bhlm,bmd->bhld', attn, mv)
        out = out.transpose(0, 2, 1, 3).reshape(b, l, d)
        return jnp.einsum('bld,ed->ble', out, Wc)

    def _L2_ffn_ref(x, w_gate, w_up, w_down):
        import jax, jax.numpy as jnp
        import numpy as np
        HIDDEN = 256
        INNER = 1024

        def _weight_quant(w):
            scale = 1.0 / jnp.clip(jnp.mean(jnp.abs(w)), 1e-05)
            wq = jnp.clip(jnp.round(w * scale), -1.0, 1.0) / scale
            return w + jax.lax.stop_gradient(wq - w)

        def _act_quant(x):
            scale = 127.0 / jnp.clip(jnp.max(jnp.abs(x), axis=-1, keepdims=True), 1e-05)
            xq = jnp.clip(jnp.round(x * scale), -128.0, 127.0) / scale
            return x + jax.lax.stop_gradient(xq - x)

        def _bitlinear(x, w):
            return jnp.einsum('bsi,oi->bso', _act_quant(x), _weight_quant(w))
        gate = jax.nn.silu(_bitlinear(x, w_gate))
        up = _bitlinear(x, w_up)
        return _bitlinear(gate * up, w_down)

    def _L3_attn_ref(x, Wq, Wk, Wv):
        import jax, jax.numpy as jnp
        import numpy as np
        B, T, D = (4, 512, 256)
        q = jnp.einsum('btd,od->bto', x, Wq)
        k = jnp.einsum('btd,od->bto', x, Wk)
        v = jnp.einsum('btd,od->bto', x, Wv)
        scores = jnp.einsum('bqd,bkd->bqk', q, k)
        inv_sqrt_d = 1.0 / np.sqrt(k.shape[-1]).astype(np.float32)
        weights = jax.nn.softmax(scores * inv_sqrt_d, axis=-1)
        return jnp.einsum('bqk,bkd->bqd', weights, v)

    def _L3_xattn_ref(y, encoder_output, Wq_self, bq_self, Wq_cross, bq_cross, g1, beta1, g2, beta2, g3, beta3, w1, b1, w2, b2):
        import jax, jax.numpy as jnp
        import numpy as np
        B, S, D, H = (1, 512, 256, 16)
        DH = D // H
        HID = 4 * D
        EPS = 1e-05
        NEG = -1000000000.0

        def _layernorm(x, g, b):
            mu = jnp.mean(x, axis=-1, keepdims=True)
            var = jnp.mean((x - mu) ** 2, axis=-1, keepdims=True)
            return (x - mu) * jax.lax.rsqrt(var + EPS) * g + b

        def _mha(x_q, x_kv, W, bias, causal):
            q = jnp.einsum('bsd,hde->bhse', x_q, W) + bias[None, :, None, :]
            k = jnp.einsum('bsd,hde->bhse', x_kv, W) + bias[None, :, None, :]
            v = jnp.einsum('bsd,hde->bhse', x_kv, W) + bias[None, :, None, :]
            scores = jnp.einsum('bhse,bhte->bhst', q, k) / jnp.sqrt(jnp.float32(DH))
            if causal:
                sq, sk = (scores.shape[-2], scores.shape[-1])
                mask = jnp.triu(jnp.ones((sq, sk), bool), k=1)
                scores = jnp.where(mask, NEG, scores)
            p = jax.nn.softmax(scores, axis=-1)
            out = jnp.einsum('bhst,bhte->bhse', p, v)
            b, h, s, e = out.shape
            return out.transpose(0, 2, 1, 3).reshape(b, s, h * e)
        sa = _mha(y, y, Wq_self, bq_self, causal=True)
        y1 = _layernorm(y + sa, g1, beta1)
        ca = _mha(y1, encoder_output, Wq_cross, bq_cross, causal=False)
        y2 = _layernorm(y1 + ca, g2, beta2)
        ff = jnp.maximum(y2 @ w1 + b1, 0.0) @ w2 + b2
        return _layernorm(y2 + ff, g3, beta3)

    def _L3_ffn_ref(hidden_states, w_gate, w1_e, w3_e, w2_e, w1_s, w3_s, w2_s):
        import jax, jax.numpy as jnp
        import numpy as np
        B, S, H = (2, 256, 256)
        E, F = (16, 128)
        G, TOPK_G, TOPK = (4, 2, 4)
        N_SHARED = 2
        ROUTE_SCALE = 1.0
        FS = N_SHARED * F

        def _gate(x, w_gate):
            T = x.shape[0]
            scores = jax.nn.sigmoid(x @ w_gate.T)
            sv = scores.reshape(T, G, E // G)
            group_scores = jax.lax.top_k(sv, 2)[0].sum(-1)
            top_groups = jax.lax.top_k(group_scores, TOPK_G)[1]
            allowed = jnp.zeros((T, G), dtype=bool).at[jnp.arange(T)[:, None], top_groups].set(True)
            masked = jnp.where(allowed[:, :, None], sv, -jnp.inf).reshape(T, E)
            _, idx = jax.lax.top_k(masked, TOPK)
            w = jnp.take_along_axis(scores, idx, axis=1)
            w = w / (w.sum(-1, keepdims=True) + 1e-06) * ROUTE_SCALE
            return (w, idx)

        def _swiglu(x, w1, w3, w2):
            return jax.nn.silu(x @ w1.T) * (x @ w3.T) @ w2.T
        shape = hidden_states.shape
        x = hidden_states.reshape(-1, H)
        weights, idx = _gate(x, w_gate)
        combine = (jax.nn.one_hot(idx, E, dtype=x.dtype) * weights[..., None]).sum(1)
        g = jax.nn.silu(jnp.einsum('th,efh->tef', x, w1_e))
        u = jnp.einsum('th,efh->tef', x, w3_e)
        routed = jnp.einsum('tef,ehf,te->th', g * u, w2_e, combine)
        shared = _swiglu(x, w1_s, w3_s, w2_s)
        return (routed + shared).reshape(shape)
    x = _layernorm(x + _L0_attn_ref(x, L0_attn_Wq, L0_attn_Wk, L0_attn_Wv, L0_attn_Wbeta, L0_attn_Wtg, L0_attn_mode_logits, L0_attn_log_decay, L0_attn_omega_log_scale, L0_attn_Wg, L0_attn_Wo), axis=-1)
    x = _layernorm(x + _L0_xattn_ref(x, ctx_1024, ctx_1024, mask_BxS2_bk1, L0_xattn_Wq, L0_xattn_bq, L0_xattn_Wk, L0_xattn_bk, L0_xattn_Wv, L0_xattn_bv, L0_xattn_Wo, L0_xattn_bo), axis=-1)
    x = _layernorm(x + _L0_ffn_ref(x, L0_ffn_Wg, L0_ffn_bg, L0_ffn_W1, L0_ffn_b1, L0_ffn_W2, L0_ffn_b2), axis=-1)
    x = _layernorm(x + _L1_attn_ref(x, L1_attn_w_qkv, L1_attn_b_qkv, L1_attn_w_out, L1_attn_b_out), axis=-1)
    x = _layernorm(x + _L1_xattn_ref(x, ctx_1024, mask_BxSxS2_ff0, L1_xattn_Wq, L1_xattn_bq, L1_xattn_Wk, L1_xattn_bk, L1_xattn_Wv, L1_xattn_bv, L1_xattn_Wo, L1_xattn_bo), axis=-1)
    x = _layernorm(x + _L1_ffn_ref(x, L1_ffn_clip_x, L1_ffn_clip_down, L1_ffn_w_gate, L1_ffn_w_up, L1_ffn_w_down), axis=-1)
    x = _layernorm(x + _L2_attn_ref(x, L2_attn_Wq, L2_attn_bq, L2_attn_Wk, L2_attn_bk, L2_attn_Wv, L2_attn_bv, L2_attn_Wo, L2_attn_bo), axis=-1)
    x = _layernorm(x + _L2_xattn_ref(x, ctx_1024, L2_xattn_Wq, L2_xattn_Wkv, L2_xattn_Wc), axis=-1)
    x = _layernorm(x + _L2_ffn_ref(x, L2_ffn_w_gate, L2_ffn_w_up, L2_ffn_w_down), axis=-1)
    x = _layernorm(x + _L3_attn_ref(x, L3_attn_Wq, L3_attn_Wk, L3_attn_Wv), axis=-1)
    x = _layernorm(x + _L3_xattn_ref(x, ctx_1024, L3_xattn_Wq_self, L3_xattn_bq_self, L3_xattn_Wq_cross, L3_xattn_bq_cross, L3_xattn_g1, L3_xattn_beta1, L3_xattn_g2, L3_xattn_beta2, L3_xattn_g3, L3_xattn_beta3, L3_xattn_w1, L3_xattn_b1, L3_xattn_w2, L3_xattn_b2), axis=-1)
    x = _layernorm(x + _L3_ffn_ref(x, L3_ffn_w_gate, L3_ffn_w1_e, L3_ffn_w3_e, L3_ffn_w2_e, L3_ffn_w1_s, L3_ffn_w3_s, L3_ffn_w2_s), axis=-1)
    return x

_drawn_inputs = setup_inputs


def setup_inputs(seed=0):
    import zlib

    import numpy as np

    out = dict(_drawn_inputs(seed))
    spreads = {'L0_ffn_bg': (0.0, 0.564),
     'L0_ffn_b1': (0.0, 0.8),
     'L0_ffn_b2': (0.0, 0.379),
     'L1_attn_b_qkv': (0.0, 0.1),
     'L1_attn_b_out': (0.0, 0.1),
     'L1_xattn_bq': (0.0, 0.347),
     'L1_xattn_bk': (0.0, 0.8),
     'L1_xattn_bv': (0.0, 0.1),
     'L1_xattn_bo': (0.0, 0.1),
     'L3_xattn_g1': (1.0, 0.2),
     'L3_xattn_beta1': (0.0, 0.1),
     'L3_xattn_g2': (1.0, 0.2),
     'L3_xattn_beta2': (0.0, 0.1),
     'L3_xattn_g3': (1.0, 0.2),
     'L3_xattn_beta3': (0.0, 0.1)}
    factors = {'L0_attn_Wq': 8.0,
     'L0_attn_Wk': 8.0,
     'L0_attn_Wv': 8.0,
     'L0_attn_Wbeta': 8.0,
     'L0_attn_Wtg': 8.0,
     'L0_attn_mode_logits': 8.0,
     'L0_attn_log_decay': 8.0,
     'L0_attn_omega_log_scale': 8.0,
     'L0_attn_Wg': 8.0,
     'L0_attn_Wo': 8.0,
     'L0_xattn_Wq': 2.995,
     'L0_xattn_bq': 8.0,
     'L0_xattn_Wk': 8.0,
     'L0_xattn_bk': 8.0,
     'L0_ffn_W1': 2.941,
     'L0_ffn_W2': 2.754,
     'L2_attn_bq': 8.0,
     'L2_attn_bk': 8.0,
     'L2_attn_bv': 4.812,
     'L3_xattn_bq_self': 5.974,
     'L3_xattn_bq_cross': 5.212,
     'L3_xattn_b1': 8.0,
     'L3_xattn_b2': 5.581,
     'L3_ffn_w_gate': 8.0,
     'L3_ffn_w1_e': 8.0,
     'L3_ffn_w3_e': 8.0,
     'L3_ffn_w2_e': 8.0,
     'L3_ffn_w1_s': 3.427,
     'L3_ffn_w3_s': 3.383,
     'L3_ffn_w2_s': 3.424}
    for name, (base, spread) in spreads.items():
        noise = np.random.default_rng([zlib.crc32(name.encode()), seed]).standard_normal(out[name].shape)
        drawn = base * np.exp(spread * noise) if base else spread * noise
        out[name] = jnp.asarray(drawn.astype(out[name].dtype))
    for name, factor in factors.items():
        out[name] = (out[name] * factor).astype(out[name].dtype)
    return out
```

```python
from contextlib import ExitStack

import numpy as np

import concourse.bass as bass
from concourse import mybir

F32 = mybir.dt.float32
BF16 = mybir.dt.bfloat16
U8 = mybir.dt.uint8
I32 = mybir.dt.int32
ALU = mybir.AluOpType
ACT = mybir.ActivationFunctionType
AX = mybir.AxisListType

P = 128
B = 16
D = 256
C = D // P
TILES = 4
TURNS = B // TILES
N = TILES * P
H = 16
DH = D // H
HH = H // C
LN_EPS = 1e-5
BANKS = 8


class Chain:

    def __init__(self, eng, sem, turn=0, per_turn=0):
        self.eng, self.sem, self.base, self.per_turn, self.n = eng, sem, turn * per_turn, per_turn, 0

    def __call__(self, ins):
        self.n += 1
        ins.then_inc(self.sem, 1)
        self.eng.wait_ge(self.sem, self.base + self.n)

    def end(self):
        assert self.n == self.per_turn, (self.n, self.per_turn)


class Semaphores:

    def __init__(self, nc, stage):
        self.nc, self.stage, self.all = nc, stage, []

    def __call__(self, name):
        self.all.append(self.nc.alloc_semaphore(f"{self.stage}_{name}"))
        return self.all[-1]

    def release(self):
        self.nc.clear_and_free_semaphores(self.all)
        self.nc.all_engine_barrier()


class Arena:

    def __init__(self, tensor, words):
        self.tensor, self.words, self.at = tensor, words, 0

    def reset(self):
        self.at = 0

    def __call__(self, *shape, dtype=F32, rows=P):
        size = 4 if dtype in (F32, I32) else 2 if dtype == BF16 else 1
        n = int(np.prod(shape))
        words = (n * size + 31) // 32 * 8
        ap = self.tensor[0:rows, self.at:self.at + n * size // 4]
        self.at += words
        assert self.at <= self.words, (self.at, self.words)
        if dtype != F32:
            ap = ap.bitcast(dtype)
        if len(shape) > 1:
            names = "abcd"[:len(shape)]
            ap = ap.rearrange("p (%s) -> p %s" % (" ".join(names), " ".join(names)),
                              **{k: v for k, v in zip(names[1:], shape[1:])})
        return ap


def bc(ap, axis, n):
    ap = ap.unsqueeze(axis)
    shape = list(ap.shape)
    shape[axis] = n
    return ap.to_broadcast(shape)


class Norm:

    def __init__(self, k, sem, src, dst, gain=None, shift=None, tiles=TILES):
        self.k, self.src, self.dst, self.gain, self.shift, self.tiles = k, src, dst, gain, shift, tiles
        self.r, self.stats = k.arena(tiles, D), k.arena(tiles, 6)
        self.mean_var, self.root, self.spare = k.arena(tiles, 2), k.arena(tiles), k.arena(1)
        self.added, self.measured, self.rooted = sem("residual_added"), sem("measured"), sem("rooted")

    def open(self, dve):
        dve.memset(self.spare, 0.0).then_inc(self.added, 1)

    def wait_added(self, eng, n):
        eng.wait_ge(self.added, n + 1)

    def add(self, dve, chain, g, u, y, factor=None):
        x = self.src[:, bass.ds(g * self.tiles + u, 1), :].rearrange("p a d -> p (a d)")
        if factor is None:
            dve.tensor_tensor(self.r[:, u, :], y, x, ALU.add).then_inc(self.added, 1)
        else:
            dve.scalar_tensor_tensor(out=self.r[:, u, :], in0=y, scalar=factor, in1=x, op0=ALU.mult, op1=ALU.add
                                     ).then_inc(self.added, 1)
        self.wait_added(dve, g * self.tiles + u + 1)
        chain(dve.bn_stats(self.stats[:, u, :], self.r[:, u, :]))

    def moments(self, dve, chain, g):
        dve.tensor_copy(self.spare[:, :], self.stats[:, self.tiles - 1, 0:1])
        for u in range(self.tiles):
            a = dve.bn_aggr(self.mean_var[:, u, :], self.stats[:, u, :])
        a.then_inc(self.measured, 1)

    def roots(self, pool, g):
        pool.wait_ge(self.measured, g + 1)
        pool.tensor_tensor(self.root[:, :], self.mean_var[:, :, 1], self.k.eps[:, 0:self.tiles], ALU.add).then_inc(self.rooted, 1)
        pool.wait_ge(self.rooted, 2 * g + 1)
        pool.tensor_tensor(self.root[:, :], self.root[:, :], self.k.minus_half[:, 0:self.tiles], ALU.pow
                           ).then_inc(self.rooted, 1)

    def apply(self, dve, chain, g):
        dve.wait_ge(self.rooted, 2 * g + 2)
        to = self.dst[:, bass.ds(g * self.tiles, self.tiles), :]
        for u in range(self.tiles):
            out = self.r[:, u, :] if self.gain is not None else to[:, u, :]
            chain(dve.tensor_scalar(out, self.r[:, u, :], self.mean_var[:, u, 0:1], self.root[:, u:u + 1],
                                    ALU.subtract, ALU.mult))
        if self.gain is not None:
            chain(dve.tensor_tensor(self.r[:, :, :], self.r[:, :, :], bc(self.gain, 1, self.tiles), ALU.mult))
            chain(dve.tensor_tensor(to, self.r[:, :, :], bc(self.shift, 1, self.tiles), ALU.add))

    def chained(self):
        return 2 * self.tiles + (2 if self.gain is not None else 0)


class Turned:

    def __init__(self, k, sem, src, bank, xT=None):
        self.k, self.src, self.bank = k, src, bank
        self.xs = k.arena(TILES, D)
        self.xT = k.arena(C, N) if xT is None else xT
        self.staged, self.turned, self.ready = sem("x_staged"), sem("x_turned"), sem("xT_ready")

    def stage(self, pool, g):
        pool.tensor_copy(self.xs[:, :, :], self.src[:, bass.ds(g * TILES, TILES), :]).then_inc(self.staged, 1)

    def stage_next(self, pool, g):
        pool.wait_ge(self.turned, (g + 1) * C)
        self.stage(pool, g + 1)

    def turn(self, pe, g):
        pe.wait_ge(self.staged, g + 1)
        for c in range(C):
            for u in range(TILES):
                mm = pe.transpose(self.k.psum[:, self.bank + c, u * P:(u + 1) * P],
                                  self.xs[:, u, c * P:(c + 1) * P], self.k.ident[:, :])
            mm.then_inc(self.turned, 1)

    def copy(self, act, g, to=None):
        to = self.xT if to is None else to
        for c in range(C):
            act.wait_ge(self.turned, g * C + c + 1)
            act.copy(to[:, c, :], self.k.psum[:, self.bank + c, :]).then_inc(self.ready, 1)


def attention_stage(k, stage, src, dst, rope=False, cross=False, mask=None, affine=False, out_proj=True,
                    recalled=False):
    nc, ps = k.nc, k.psum
    w = k.begin(stage)
    sem, A = Semaphores(nc, stage), k.arena
    x_staged, x_turned, xT_ready = sem("x_staged"), sem("x_turned"), sem("xT_ready")
    projected, qk_evacuated, v_ready = sem("projected"), sem("qk_evacuated"), sem("v_ready")
    rotated, keys_spread = sem("rotated"), sem("keys_spread")
    scores_ready, shifted, probs_ready = sem("scores_ready"), sem("shifted"), sem("probs_ready")
    probs_turned, probsT_ready, o_ready = sem("probs_turned"), sem("probsT_ready"), sem("o_ready")
    o_normalised, oT_turned, oT_ready = sem("o_normalised"), sem("oT_turned"), sem("oT_ready")
    y_ready = sem("y_ready")
    loaded, ones_set, dve_chain = sem("loaded"), sem("ones_set"), sem("dve_chain")

    xs = A(TILES, D)
    xT = A(C, N)
    kvT = A(C, N) if cross else xT
    qT, kT = A(C, N), A(C, N)
    half = [A(N) for _ in range(2)] if rope else None
    km = A(2, HH, P)
    va = A(TILES, H, DH + 1)
    pr = A(2, HH, P)
    pT = A(2, HH, P)
    mx, on, oT, ri = A(2, HH), A(D), A(C, P), A(H)
    norm = Norm(k, sem, src, dst, *((w.gain, w.shift) if affine else ()))
    mk = A(TILES, P) if mask == "batch" else None
    ones = A(P)

    qk = [(n, c) for n in (("q", "qs", "k", "ks") if rope else ("q", "k")) for c in range(C)]
    if rope:
        qk = [(n + s, c) for n in "qk" for c in range(C) for s in ("", "s")]
    if recalled:
        qk = [("q", c) for c in range(C)]
    NQK, NP = len(qk), len(qk) + (0 if recalled else 2)
    SPREADS = TILES if recalled else TILES * C
    UNITS = TILES * C
    STEPS = range(UNITS + 3)
    S_BANK, T_BANK, O_BANK, Y_BANK = 0, 4, 6, 7

    def s_psum(j):
        return ps[:, S_BANK + 2 * (j % 2):S_BANK + 2 * (j % 2) + 2, :].rearrange("p b (h t) -> p (b h) t", t=P)

    pt_psum = ps[:, T_BANK:T_BANK + 2, :].rearrange("p b (h t) -> p (b h) t", t=P)
    o_psum = ps[:, O_BANK, 0:H * (DH + 1)].rearrange("p (h e) -> p h e", e=DH + 1)
    oT_psum = ps[:, Y_BANK, 0:D].rearrange("p (c t) -> p c t", c=C)
    y_psum = ps[:, Y_BANK, D:2 * D]

    with nc.Block() as block:
        @block.sync
        def _(sp):
            def load(g):
                if cross:
                    sp.dma_start(kvT[:, :, :], k.ctxT[g]).then_inc(loaded, 16)
                if mask == "batch":
                    sp.dma_start(mk[:, :, :], k.maskb[g]).then_inc(loaded, 16)
            if cross or mask == "batch":
                load(0)
            k.prefetch(sp, stage)
            if cross or mask == "batch":
                with sp.Fori(1, TURNS) as g:
                    if mask == "batch":
                        sp.wait_ge(shifted, g * UNITS)
                    else:
                        sp.wait_ge(projected, g * NP)
                    load(g)

        LOADS = 16 * ((1 if cross else 0) + (1 if mask == "batch" else 0))

        @block.gpsimd
        def _(pool):
            k.wait_weights(pool, stage)
            pool.memset(va[:, :, :, DH:DH + 1], 1.0).then_inc(ones_set, 1)
            pool.memset(ones[:, :], 1.0).then_inc(ones_set, 1)

            def stage_x(g):
                pool.tensor_copy(xs[:, :, :], src[:, bass.ds(g * TILES, TILES), :]).then_inc(x_staged, 1)

            def spread(g):
                if rope:
                    for p in range(NQK // 2):
                        pool.wait_ge(qk_evacuated, g * NQK + 2 * p + 2)
                        to = (qT if p < C else kT)[:, p % C, :]
                        pool.tensor_tensor(to, to, half[p % 2], ALU.add).then_inc(rotated, 1)
                    pool.wait_ge(rotated, (g + 1) * (NQK // 2))
                else:
                    pool.wait_ge(qk_evacuated, (g + 1) * NQK)
                if recalled:
                    for u in range(TILES):
                        if u >= 2:
                            pool.wait_ge(scores_ready, g * UNITS + (u - 1) * C)
                        keys = k.Y[:, bass.ds(g * TILES + u, 1), 0:P].rearrange("p a t -> p (a t)")
                        pool.tensor_tensor(km[:, u % 2, :, :], bc(keys, 1, HH), bc(w.heads, 2, P),
                                           ALU.mult).then_inc(keys_spread, 1)
                    return
                for j in range(UNITS):
                    if j >= 2:
                        pool.wait_ge(scores_ready, g * UNITS + j - 1)
                    u, c = divmod(j, C)
                    keys = kT[:, c, u * P:(u + 1) * P]
                    pool.tensor_tensor(km[:, j % 2, :, :], bc(keys, 1, HH), bc(w.heads, 2, P),
                                       ALU.mult).then_inc(keys_spread, 1)

            stage_x(0)
            with pool.Fori(0, TURNS - 1) as g:
                spread(g)
                pool.wait_ge(x_turned, (g + 1) * C)
                stage_x(g + 1)
                norm.roots(pool, g)
            spread(TURNS - 1)
            norm.roots(pool, TURNS - 1)

        @block.tensor
        def _(pe):
            k.wait_weights(pe, stage)
            pe.wait_ge(ones_set, 2)

            with pe.Fori(0, TURNS) as g:
                pe.wait_ge(x_staged, g + 1)
                for c in range(C):
                    for u in range(TILES):
                        mm = nc.tensor.transpose(ps[:, T_BANK + c, u * P:(u + 1) * P],
                                                 xs[:, u, c * P:(c + 1) * P], k.ident[:, :])
                    mm.then_inc(x_turned, 1)
                pe.wait_ge(xT_ready, (g + 1) * C)
                if cross:
                    pe.wait_ge(loaded, (g + 1) * LOADS)
                for p in range(NP):
                    bank = ps[:, S_BANK + p % 4, :]
                    if p >= 4:
                        pe.wait_ge(qk_evacuated, g * NQK + p - 3)
                    if p < NQK:
                        name, co = qk[p]
                        frm = xT if name[0] == "q" else kvT
                        for ci in range(C):
                            mm = nc.tensor.matmul(bank, w["w" + name][:, ci, co * P:(co + 1) * P], frm[:, ci, :],
                                                  start=(ci == 0), stop=(ci == C - 1))
                    else:
                        for u in (0, 1):
                            t = 2 * (p - NQK) + u
                            for ci in range(C):
                                mm = nc.tensor.matmul(bank[:, u * D:(u + 1) * D], kvT[:, ci, t * P:(t + 1) * P],
                                                      w.wv[:, ci, :], start=(ci == 0), stop=(ci == C - 1))
                    mm.then_inc(projected, 1)

                def scores(j):
                    u, c = divmod(j, C)
                    at = u if recalled else j
                    pe.wait_ge(keys_spread, g * SPREADS + at + 1)
                    if j == 0:
                        pe.wait_ge(qk_evacuated, (g + 1) * NQK)
                        if rope:
                            pe.wait_ge(rotated, (g + 1) * (NQK // 2))
                        if not recalled:
                            pe.wait_ge(v_ready, (g + 1) * 2)
                    if j >= 2:
                        pe.wait_ge(shifted, g * UNITS + j - 1)
                    out = s_psum(j)
                    for b in range(2):
                        mm = nc.tensor.matmul(out[:, b * 4:b * 4 + 4, :], qT[:, c, u * P:(u + 1) * P],
                                              km[:, at % 2, b * 4:b * 4 + 4, :], start=True, stop=True)
                    mm.then_inc(scores_ready, 1)

                def values(j):
                    u, c = divmod(j, C)
                    pe.wait_ge(probsT_ready, g * UNITS + j + 1)
                    if c == 0 and u >= 1:
                        pe.wait_ge(o_normalised, g * TILES + u)
                    for h in range(HH):
                        v = (k.Y[:, bass.ds(g * TILES + u, 1), P:P + DH + 1].rearrange("p a e -> p (a e)") if recalled
                             else va[:, u, c * HH + h, :])
                        mm = nc.tensor.matmul(o_psum[:, c * HH + h, :], pT[:, j % 2, h, :], v,
                                              start=True, stop=True)
                    if c == C - 1:
                        mm.then_inc(o_ready, 1)

                def turn_probs(j):
                    pe.wait_ge(probs_ready, g * UNITS + j + 1)
                    for h in range(HH):
                        mm = nc.tensor.transpose(pt_psum[:, h, :], pr[:, j % 2, h, :], k.ident[:, :])
                    mm.then_inc(probs_turned, 1)

                def turn_o(u):
                    pe.wait_ge(o_normalised, g * TILES + u + 1)
                    if u >= 1:
                        norm.wait_added(pe, g * TILES + u)
                    for c in range(C):
                        mm = nc.tensor.transpose(oT_psum[:, c, :], on[:, c * P:(c + 1) * P], k.ident[:, :])
                    mm.then_inc(oT_turned, 1)

                def project_out(u):
                    pe.wait_ge(oT_ready, g * TILES + u + 1)
                    for c in range(C):
                        mm = nc.tensor.matmul(y_psum, oT[:, c, :], w.wo[:, c, :], start=(c == 0),
                                              stop=(recalled and c == C - 1))
                    if not recalled:
                        mm = nc.tensor.matmul(y_psum, ones[0:1, :], w.bo[0:1, :], start=False, stop=True)
                    mm.then_inc(y_ready, 1)

                scores(0)
                for j in STEPS:
                    if j + 1 < UNITS:
                        scores(j + 1)
                    if 1 <= j <= UNITS:
                        values(j - 1)
                    if j < UNITS:
                        turn_probs(j)
                    if out_proj and j >= 3 and j % 2 == 1 and (j - 3) // 2 < TILES:
                        turn_o((j - 3) // 2)
                    if out_proj and j >= 4 and j % 2 == 0:
                        project_out((j - 4) // 2)

        @block.scalar
        def _(act):
            k.wait_weights(act, stage)
            act.wait_ge(ones_set, 2)
            with act.Fori(0, TURNS) as g:
                for c in range(C):
                    act.wait_ge(x_turned, g * C + c + 1)
                    nc.scalar.copy(xT[:, c, :], ps[:, T_BANK + c, :]).then_inc(xT_ready, 1)
                if not rope:
                    for p, (name, c) in enumerate(qk):
                        act.wait_ge(projected, g * NP + p + 1)
                        bias = 0.0 if recalled else (w.bq if name == "q" else w.bk)[:, c:c + 1]
                        nc.scalar.activation((qT if name == "q" else kT)[:, c, :], ps[:, S_BANK + p % 4, :],
                                             ACT.Identity, bias=bias).then_inc(qk_evacuated, 1)
                for p in range(NQK, NP):
                    act.wait_ge(projected, g * NP + p + 1)
                    t = 2 * (p - NQK)
                    nc.scalar.copy(va[:, t:t + 2, :, 0:DH],
                                   ps[:, S_BANK + p % 4, :].rearrange("p (u h e) -> p u h e", u=2, e=DH)
                                   ).then_inc(v_ready, 1)
                for j in STEPS:
                    if j < UNITS:
                        act.wait_ge(shifted, g * UNITS + j + 1)
                        nc.scalar.activation(pr[:, j % 2, :, :], pr[:, j % 2, :, :], ACT.Exp,
                                             scale=1.0 if mask else DH ** -0.5).then_inc(probs_ready, 1)
                    if 1 <= j <= UNITS:
                        act.wait_ge(probs_turned, g * UNITS + j)
                        nc.scalar.copy(pT[:, (j - 1) % 2, :, :], pt_psum).then_inc(probsT_ready, 1)
                    if out_proj and j >= 3 and j % 2 == 1 and (j - 3) // 2 < TILES:
                        act.wait_ge(oT_turned, g * TILES + (j - 3) // 2 + 1)
                        for c in range(C):
                            a = nc.scalar.activation(oT[:, c, :], oT_psum[:, c, :], ACT.Identity,
                                                     bias=0.0 if recalled else w.bv[:, c:c + 1])
                        a.then_inc(oT_ready, 1)

        @block.vector
        def _(dve):
            k.wait_weights(dve, stage)

            def turn(g, chain):
                if rope:
                    for p, (name, c) in enumerate(qk):
                        dve.wait_ge(projected, g * NP + p + 1)
                        if p % 2 and p >= 5:
                            dve.wait_ge(rotated, g * (NQK // 2) + (p - 3) // 2)
                        to = half[(p // 2) % 2] if p % 2 else (qT if name[0] == "q" else kT)[:, c, :]
                        table = w["sin" if p % 2 else "cos"]
                        dve.scalar_tensor_tensor(out=to.rearrange("p (u t) -> p u t", t=P),
                                                 in0=ps[:, S_BANK + p % 4, :].rearrange("p (u t) -> p u t", t=P),
                                                 scalar=w["b" + name][:, c:c + 1], in1=bc(table, 1, TILES),
                                                 op0=ALU.add, op1=ALU.mult).then_inc(qk_evacuated, 1)
                for j in STEPS:
                    if j < UNITS:
                        n = g * UNITS + j
                        dve.wait_ge(scores_ready, n + 1)
                        if j >= 2:
                            dve.wait_ge(probs_turned, n - 1)
                        s = s_psum(j)
                        if mask:
                            if mask == "batch":
                                if j == 0:
                                    dve.wait_ge(loaded, (g + 1) * LOADS)
                                m = mk[:, j // C, :]
                            else:
                                m = w.causal
                            chain(dve.scalar_tensor_tensor(out=pr[:, j % 2, :, :], in0=s, scalar=DH ** -0.5,
                                                           in1=bc(m, 1, HH), op0=ALU.mult, op1=ALU.add))
                            s = pr[:, j % 2, :, :]
                        chain(dve.tensor_reduce(mx[:, j % 2, :], s, AX.X, ALU.max))
                        dve.tensor_tensor(pr[:, j % 2, :, :], s, bc(mx[:, j % 2, :], 2, P), ALU.subtract).then_inc(shifted, 1)
                    if j >= 2 and j % 2 == 0 and (j - 2) // 2 < TILES:
                        u = (j - 2) // 2
                        dve.wait_ge(o_ready, g * TILES + u + 1)
                        chain(dve.reciprocal(ri[:, :], o_psum[:, :, DH]))
                        if out_proj and u >= 1:
                            dve.wait_ge(oT_turned, g * TILES + u)
                        dve.tensor_tensor(on[:, :].rearrange("p (h e) -> p h e", e=DH), o_psum[:, :, 0:DH],
                                          bc(ri[:, :], 2, DH), ALU.mult).then_inc(o_normalised, 1)
                        if not out_proj:
                            dve.wait_ge(o_normalised, g * TILES + u + 1)
                            chain(dve.tensor_tensor(on[:, :], on[:, :], w.bv_row, ALU.add))
                            norm.add(dve, chain, g, u, on[:, :])
                    if out_proj and j >= 4 and j % 2 == 0:
                        u = (j - 4) // 2
                        dve.wait_ge(y_ready, g * TILES + u + 1)
                        norm.add(dve, chain, g, u, y_psum)
                norm.moments(dve, chain, g)
                norm.apply(dve, chain, g)
                chain.end()

            per = UNITS * (2 if mask else 1) + TILES * (1 if out_proj else 2) + norm.chained()
            norm.open(dve)
            with dve.Fori(0, TURNS) as g:
                turn(g, Chain(dve, dve_chain, g, per))
    sem.release()


def delta_stage(k):
    stage = "L0_attn"
    nc, ps, w, A = k.nc, k.psum, k.begin(stage), k.arena
    sem = Semaphores(nc, stage)
    M, DK, DHEADS = 8, 64, 8
    HALVES = 2
    HALF = DHEADS // HALVES
    CH = HALF * M
    PAIRS = DHEADS // 2
    Q = 32
    NQ = P // Q
    GROUPS, PACKS_ = CH // 4, CH // 8
    W = DHEADS * DK
    norm = Norm(k, sem, k.X, k.X, tiles=1)
    names = """x_staged x_turned xT_ready projected evacuated squared squares_summed roots_ready qk_normalised
    qk_turned qkT_ready swapped swapped_ready decays_clipped decays_ready consts_ready tables_ready
    angles_ready reduced halves_ready rotated keys_padded masked_decays exponents_ready decay_ready products_ready
    blocks_ready outputs_ready blocks_taken inverse_ready solved coupled solution_ready rest_ready weighted
    o_ready o_gated y_ready dve_chain pool_chain act_chain""".split()
    s = {n: sem(n) for n in names}

    def chains(i):
        at = (i // 4 * 2 + i % 2) * M + i // 2 % 2 * 4
        return slice(at, at + 4)

    def flat(ap):
        letters = "abcd"[:len(ap.shape) - 1]
        return ap.rearrange("p %s -> p (%s)" % (" ".join(letters), " ".join(letters)))

    xs, xT = A(D), A(C, P)
    v, gateT, bt = A(W), A(PAIRS, P), A(2 * DHEADS * M)
    qkT, qkS = A(2, PAIRS, P), A(2, PAIRS, P)
    kq = A(2, 4, 2, P)
    kz = A(2, 2, 4, P)
    t1, gm = A(2, 4, P), A(2, 4, P)
    qkn, squares = flat(t1), flat(gm)
    Ls, Bs = [A(CH, P) for _ in range(HALVES)], [A(CH, P) for _ in range(HALVES)]
    inv, prod = A(Q, Q), A(Q * Q // 4)
    ur = A(HALF, M, DK)
    ogT = gm[:, 0, :, :]
    ss, exponent, decay = A(2 * DHEADS), A(2 * DHEADS), A(DHEADS * M)
    rho, modes, mode_sum = A(DHEADS * M), A(DHEADS, M), A(DHEADS)
    wb, omega, tiny = A(DHEADS, M), A(PAIRS, M), A(2 * DHEADS)
    ident_h, later_h = A(P, dtype=BF16), A(4, P, dtype=BF16)
    sin = flat(k.Y).rearrange("p (c m t) -> p c m t", m=M, t=P)
    other = Arena(k.next_region(stage), REGION)
    cos, lanes, Ts = other(PAIRS, M, P), other(Q, Q), [other(CH, Q) for _ in range(HALVES)]

    TWO_PI = 2 * np.pi
    C1 = 6.28125
    C2 = float(np.float32(np.floor((TWO_PI - C1) * 2 ** 22) / 2 ** 22))
    C3 = float(np.float32(TWO_PI - C1 - C2))
    PI = float(np.float32(3.1415925))
    MAGIC = 1.5 * 2 ** 23

    with nc.Block() as block:
        @block.sync
        def _(sp):
            sp.wait_ge(s["y_ready"], B)
            k.prefetch(sp, stage)

        @block.gpsimd
        def _(pool):
            k.wait_weights(pool, stage)
            pool.memset(exponent, -0.5)
            pool.memset(tiny, 1e-6)
            pool.memset(flat(kz), 0.0).then_inc(s["consts_ready"], 1)
            pool.wait_ge(s["consts_ready"], 1)

            def stage_x(g):
                pool.tensor_copy(xs, k.X[:, bass.ds(g, 1), :].rearrange("p a d -> p (a d)")).then_inc(s["x_staged"], 1)

            def turn(g, more):
                pool.wait_ge(s["x_turned"], g + 1)
                if more:
                    stage_x(g + 1)
                ch = Chain(pool, s["pool_chain"], g, 1)
                pool.wait_ge(s["squares_summed"], g + 1)
                ch(pool.tensor_tensor(ss, ss, tiny, ALU.add))
                pool.tensor_tensor(ss, ss, exponent, ALU.pow).then_inc(s["roots_ready"], 1)
                pool.wait_ge(s["decays_ready"], g + 1)
                for hf in range(HALVES):
                    u = g * HALVES + hf
                    for p in range(PACKS_):
                        n = u * PACKS_ + p
                        for hh in range(2):
                            i = 2 * p + hh
                            if hf or i >= 2:
                                pool.wait_ge(s["exponents_ready"], u * GROUPS + i - 1)
                            at = (hf * HALF + p // 2 * 2 + hh) * M + p % 2 * 4
                            pool.tensor_tensor(gm[:, hh, :, :], bc(decay[:, at:at + 4], 2, P), bc(w.incl, 1, 4),
                                               ALU.mult).then_inc(s["masked_decays"], 1)
                        for j in range(2):
                            pool.wait_ge(s["halves_ready"], n * 2 + j + 1)
                            both = kq[:, p % 2, :, j, :]
                            pool.tensor_tensor(both, both, t1[:, j, :, :], ALU.add).then_inc(s["rotated"], 1)
                for hf in range(HALVES):
                    for h in range(HALF):
                        u = g * HALVES + hf
                        pool.wait_ge(s["solution_ready"], ((u * NQ) + NQ - 1) * HALF + h + 1)
                        pool.tensor_tensor(ur[:, h, :, :], ur[:, h, :, :], bc(wb[:, hf * HALF + h, :], 2, DK), ALU.mult
                                           ).then_inc(s["weighted"], 1)
                norm.roots(pool, g)

            stage_x(0)
            with pool.Fori(0, B - 1) as g:
                turn(g, True)
            turn(B - 1, False)

        @block.tensor
        def _(pe):
            k.wait_weights(pe, stage)
            pe.wait_ge(s["tables_ready"], 1)
            pe.wait_ge(s["consts_ready"], 1)

            def carrier():
                nc.tensor.matmul(ps[:, 0, 0:1], ident_h, ident_h[:, 0:1], start=True, stop=True)

            with pe.Fori(0, B) as g:
                pe.wait_ge(s["x_staged"], g + 1)
                for c in range(C):
                    mm = nc.tensor.transpose(ps[:, 0, c * P:(c + 1) * P], xs[:, c * P:(c + 1) * P], k.ident)
                mm.then_inc(s["x_turned"], 1)
                pe.wait_ge(s["xT_ready"], g + 1)
                for i, m in enumerate((w.wk, w.wq, w.wv, w.wbt)):
                    for c in range(C):
                        mm = nc.tensor.matmul(ps[:, 1 + i, 0:m.shape[2]], xT[:, c, :], m[:, c, :],
                                              start=(c == 0), stop=(c == C - 1))
                    mm.then_inc(s["projected"], 1)
                for co in range(PAIRS):
                    for c in range(C):
                        mm = nc.tensor.matmul(ps[:, 5, co * P:(co + 1) * P], w.wg[:, c, co * P:(co + 1) * P], xT[:, c, :],
                                              start=(c == 0), stop=(c == C - 1))
                mm.then_inc(s["projected"], 1)
                pe.wait_ge(s["qk_normalised"], g + 1)
                for j in range(2):
                    for c in range(PAIRS):
                        mm = nc.tensor.transpose(ps[:, 6 + j, c * P:(c + 1) * P],
                                                 qkn[:, j * W + c * P:j * W + (c + 1) * P], k.ident)
                    mm.then_inc(s["qk_turned"], 1)
                for j in range(2):
                    pe.wait_ge(s["qkT_ready"], g * 2 + j + 1)
                    nc.tensor.matmul(ps[:, 1 + j, :], w.swap, qkT[:, j, :, :], start=True, stop=True
                                     ).then_inc(s["swapped"], 1)
                pe.wait_ge(s["swapped_ready"], (g + 1) * 2)
                pe.wait_ge(s["evacuated"], (g + 1) * 3)

                for hf in range(HALVES):
                    u = g * HALVES + hf
                    for i in range(GROUPS):
                        n, p, hh = u * GROUPS + i, i // 2, i % 2
                        pe.wait_ge(s["masked_decays"], n + 1)
                        if hf or i >= 2:
                            pe.wait_ge(s["decay_ready"], n - 1)
                        bank = ps[:, hh, :]
                        nc.tensor.matmul(bank, w.after, gm[:, hh, :, :], start=True, stop=False)
                        nc.tensor.matmul(bank, ident_h, later_h[:, :, :], start=False, stop=True
                                         ).then_inc(s["exponents_ready"], 1)
                        if hh == 0:
                            pe.wait_ge(s["rotated"], (u * PACKS_ + p + 1) * 2)
                            pe.wait_ge(s["keys_padded"], u * PACKS_ + p + 1)
                        if hf or i >= 2:
                            pe.wait_ge(s["outputs_ready"], n - 1)
                        for m in range(4):
                            mm = nc.tensor.matmul(ps[:, 2 + 2 * hh + m // 2, (m % 2) * 2 * P:(m % 2 + 1) * 2 * P],
                                                  kz[:, p % 2, hh, m, :], kq[:, p % 2, m, :, :], start=True, stop=True)
                        mm.then_inc(s["products_ready"], 1)

                pe.wait_ge(s["outputs_ready"], (g + 1) * HALVES * GROUPS)
                for hf in range(HALVES):
                    u = g * HALVES + hf
                    Lt, Bt, Tt = Ls[hf], Bs[hf], Ts[hf]
                    pe.wait_ge(s["inverse_ready"], u + 1)
                    carrier()
                    for q in range(NQ):
                        rows = slice(q * Q, (q + 1) * Q)
                        if q:
                            for h in range(HALF):
                                pe.wait_ge(s["solution_ready"], (u * NQ + q - 1) * HALF + h + 1)
                                carrier()
                                for m in range(M):
                                    mm = nc.tensor.matmul(ps[rows, 4 + h, m * DK:(m + 1) * DK],
                                                          Lt[0:q * Q, h * M + m, rows], ur[0:q * Q, h, m, :],
                                                          start=True, stop=True)
                                mm.then_inc(s["coupled"], 1)
                        for h in range(HALF):
                            if q:
                                pe.wait_ge(s["rest_ready"], (u * (NQ - 1) + q - 1) * HALF + h + 1)
                                carrier()
                            for m in range(M):
                                rhs = ur[rows, h, m, :] if q else v[rows, (hf * HALF + h) * DK:(hf * HALF + h + 1) * DK]
                                mm = nc.tensor.matmul(ps[rows, 4 + h, m * DK:(m + 1) * DK], Tt[rows, h * M + m, :], rhs,
                                                      start=True, stop=True)
                            mm.then_inc(s["solved"], 1)
                    for h in range(HALF):
                        pe.wait_ge(s["weighted"], u * HALF + h + 1)
                        for m in range(M):
                            mm = nc.tensor.matmul(ps[h % 2 * DK:(h % 2 + 1) * DK, 2 + hf, h // 2 * P:(h // 2 + 1) * P],
                                                  ur[:, h, m, :], Bt[:, h * M + m, :], start=(m == 0), stop=(m == M - 1))
                    mm.then_inc(s["o_ready"], 1)
                pe.wait_ge(s["o_gated"], (g + 1) * HALVES)
                for c in range(PAIRS):
                    mm = nc.tensor.matmul(ps[:, 1, 0:D], ogT[:, c, :], w.wo[:, c, :], start=(c == 0), stop=(c == PAIRS - 1))
                mm.then_inc(s["y_ready"], 1)
                norm.wait_added(pe, g + 1)

        @block.scalar
        def _(act):
            k.wait_weights(act, stage)
            nc.scalar.activation(omega[:, :, :], w.omega, ACT.Exp).then_inc(s["angles_ready"], 1)
            nc.scalar.activation(rho, w.log_decay, ACT.Sigmoid, scale=-1.0).then_inc(s["angles_ready"], 1)
            act.wait_ge(s["reduced"], 1)
            act.wait_ge(s["consts_ready"], 1)
            nc.scalar.activation(modes[:, :, :], modes[:, :, :], ACT.Exp).then_inc(s["angles_ready"], 1)
            for c in range(PAIRS):
                act.wait_ge(s["reduced"], c + 2)
                for table in (sin, cos):
                    nc.scalar.activation(table[:, c, :, :], table[:, c, :, :], ACT.Sin).then_inc(s["act_chain"], 1)
            act.wait_ge(s["act_chain"], 2 * PAIRS)
            nc.scalar.copy(ident_h, k.ident).then_inc(s["tables_ready"], 1)

            with act.Fori(0, B) as g:
                act.wait_ge(s["x_turned"], g + 1)
                nc.scalar.copy(xT[:, :, :], ps[:, 0, 0:D].rearrange("p (c t) -> p c t", t=P)).then_inc(s["xT_ready"], 1)
                for j in range(2):
                    act.wait_ge(s["projected"], g * 5 + j + 1)
                    nc.scalar.activation(squares[:, j * W:(j + 1) * W], ps[:, 1 + j, :], ACT.Square
                                         ).then_inc(s["squared"], 1)
                act.wait_ge(s["projected"], g * 5 + 3)
                nc.scalar.copy(v, ps[:, 3, :]).then_inc(s["evacuated"], 1)
                act.wait_ge(s["projected"], g * 5 + 4)
                nc.scalar.activation(bt, ps[:, 4, 0:2 * DHEADS * M], ACT.Sigmoid).then_inc(s["evacuated"], 1)
                act.wait_ge(s["projected"], g * 5 + 5)
                nc.scalar.activation(gateT[:, :, :], ps[:, 5, :].rearrange("p (c t) -> p c t", t=P), ACT.Sigmoid
                                     ).then_inc(s["evacuated"], 1)
                act.wait_ge(s["decays_clipped"], g + 1)
                nc.scalar.activation(decay, decay, ACT.Ln).then_inc(s["decays_ready"], 1)
                for j in range(2):
                    act.wait_ge(s["qk_turned"], g * 2 + j + 1)
                    nc.scalar.copy(qkT[:, j, :, :], ps[:, 6 + j, :].rearrange("p (c t) -> p c t", t=P)
                                   ).then_inc(s["qkT_ready"], 1)
                for j in range(2):
                    act.wait_ge(s["swapped"], g * 2 + j + 1)
                    nc.scalar.copy(qkS[:, j, :, :], ps[:, 1 + j, :].rearrange("p (c t) -> p c t", t=P)
                                   ).then_inc(s["swapped_ready"], 1)
                for hf in range(HALVES):
                    u = g * HALVES + hf
                    for p in range(PACKS_):
                        n = u * PACKS_ + p
                        act.wait_ge(s["rotated"], n * 2 + 1)
                        for hh in range(2):
                            rows = slice(hh * DK, (hh + 1) * DK)
                            a = nc.scalar.copy(kz[rows, p % 2, hh, :, :], kq[rows, p % 2, :, 0, :])
                        a.then_inc(s["keys_padded"], 1)
                        for i in (2 * p, 2 * p + 1):
                            act.wait_ge(s["exponents_ready"], u * GROUPS + i + 1)
                            nc.scalar.activation(Bs[hf][:, chains(i), :],
                                                 ps[:, i % 2, :].rearrange("p (c t) -> p c t", t=P),
                                                 ACT.Exp).then_inc(s["decay_ready"], 1)
                for hf in range(HALVES):
                    u = g * HALVES + hf
                    for q in range(NQ):
                        rows = slice(q * Q, (q + 1) * Q)
                        for h in range(HALF):
                            act.wait_ge(s["solved"], (u * NQ + q) * HALF + h + 1)
                            nc.scalar.copy(ur[rows, h, :, :], ps[rows, 4 + h, :].rearrange("p (m e) -> p m e", e=DK)
                                           ).then_inc(s["solution_ready"], 1)

        @block.vector
        def _(dve):
            k.wait_weights(dve, stage)
            norm.open(dve)
            once = Chain(dve, s["dve_chain"])
            once(dve.tensor_reduce(mode_sum, w.modes, AX.X, ALU.max))
            dve.tensor_tensor(modes[:, :, :], w.modes, bc(mode_sum, 2, M), ALU.subtract).then_inc(s["reduced"], 1)
            once(dve.tensor_scalar(later_h[:, 0, :], w.incl, -1.0, 1e30, ALU.add, ALU.mult))
            once(dve.tensor_copy(later_h[:, 1:4, :], bc(later_h[:, 0, :], 1, 3)))
            dve.wait_ge(s["angles_ready"], 3)
            once(dve.tensor_reduce(mode_sum, modes[:, :, :], AX.X, ALU.add))
            once(dve.reciprocal(mode_sum, mode_sum))
            once(dve.tensor_tensor(modes[:, :, :], modes[:, :, :], bc(mode_sum, 2, M), ALU.mult))
            x, n = Ls[0][:, 0:M, :], Ls[0][:, M:2 * M, :]
            for c in range(PAIRS):
                once(dve.tensor_tensor(x, bc(w.position, 1, M), bc(omega[:, c, :], 2, P), ALU.mult))
                once(dve.tensor_scalar(x, x, w.inv_freq[:, 0:1], None, ALU.mult))
                for table, quarter in ((sin, 0.0), (cos, 0.25)):
                    r = table[:, c, :, :]
                    once(dve.tensor_scalar(n, x, 1 / TWO_PI, quarter, ALU.mult, ALU.add))
                    once(dve.tensor_scalar(n, n, MAGIC, MAGIC, ALU.add, ALU.subtract))
                    once(dve.scalar_tensor_tensor(out=r, in0=n, scalar=-C1, in1=x, op0=ALU.mult, op1=ALU.add))
                    once(dve.scalar_tensor_tensor(out=r, in0=n, scalar=-C2, in1=r, op0=ALU.mult, op1=ALU.add))
                    once(dve.scalar_tensor_tensor(out=r, in0=n, scalar=-C3, in1=r, op0=ALU.mult, op1=ALU.add))
                    once(dve.tensor_scalar(r, r, quarter * TWO_PI, PI, ALU.add, ALU.min))
                    a = dve.tensor_scalar(r, r, -PI, None, ALU.max)
                    if table is cos:
                        a.then_inc(s["reduced"], 1)
                    else:
                        once(a)
            dve.wait_ge(s["tables_ready"], 1)

            def rotate(g, hf, p):
                n = (g * HALVES + hf) * PACKS_ + p
                c, modes4 = hf * 2 + p // 2, slice(p % 2 * 4, p % 2 * 4 + 4)
                for j in range(2):
                    dve.tensor_tensor(kq[:, p % 2, :, j, :], bc(qkT[:, j, c, :], 1, 4), cos[:, c, modes4, :], ALU.mult)
                    if hf or p:
                        dve.wait_ge(s["rotated"], (n - 1) * 2 + j + 1)
                    dve.tensor_tensor(t1[:, j, :, :], bc(qkS[:, j, c, :], 1, 4), sin[:, c, modes4, :], ALU.mult
                                      ).then_inc(s["halves_ready"], 1)

            def evacuate(g, hf, p):
                for i in (2 * p, 2 * p + 1):
                    n = (g * HALVES + hf) * GROUPS + i
                    c0 = chains(i).start
                    Lt, Bt = Ls[hf], Bs[hf]
                    dve.wait_ge(s["products_ready"], n + 1)
                    dve.wait_ge(s["decay_ready"], n + 1)
                    kk = ps[:, 2 + 2 * (i % 2):4 + 2 * (i % 2), :].rearrange("p b (c k t) -> p (b c) k t", c=2, k=2)
                    for m in range(4):
                        at = hf * CH + c0 + m
                        a = dve.scalar_tensor_tensor(out=Lt[:, c0 + m, :], in0=kk[:, m, 0, :], scalar=bt[:, at:at + 1],
                                                     in1=Bt[:, c0 + m, :], op0=ALU.mult, op1=ALU.mult)
                    a.then_inc(s["blocks_ready"], 1)
                    dve.wait_ge(s["blocks_ready"], n + 1)
                    dve.tensor_tensor(Bt[:, chains(i), :], kk[:, :, 1, :], Bt[:, chains(i), :], ALU.mult
                                      ).then_inc(s["outputs_ready"], 1)

            def invert(g, hf, ch, between):
                u = g * HALVES + hf
                Lt, Tt = Ls[hf], Ts[hf]
                dve.wait_ge(s["outputs_ready"], (u + 1) * GROUPS)
                for q in range(NQ):
                    rows = slice(q * Q, (q + 1) * Q)
                    a = dve.transpose(lanes[rows, :, :], Lt[rows, :, rows].rearrange("p c t -> p t c"))
                a.then_inc(s["blocks_taken"], 1)
                dve.wait_ge(s["blocks_taken"], u + 1)
                ch(dve.tensor_scalar(inv[:, :, :], lanes[:, :, :], -1.0, None, ALU.mult))
                dve.memset(flat(inv)[:, 0:Q * Q:Q + 1], 1.0)
                for j in range(1, Q - 1):
                    below = Q - 1 - j
                    part = prod[:, 0:below * j].rearrange("p (a b) -> p a b", b=j)
                    ch(dve.tensor_tensor(part, bc(lanes[:, j + 1:, j], 2, j), bc(inv[:, j, 0:j], 1, below), ALU.mult))
                    ch(dve.tensor_tensor(inv[:, j + 1:, 0:j], inv[:, j + 1:, 0:j], part, ALU.subtract))
                    if j in between:
                        between[j]()
                dve.transpose(Tt[:, :, :].rearrange("p c t -> p t c"), inv[:, :, :]).then_inc(s["inverse_ready"], 1)

            def rest(g, hf, q, h):
                n = (g * HALVES + hf) * (NQ - 1) + q - 1
                rows = slice(q * Q, (q + 1) * Q)
                dve.wait_ge(s["coupled"], n * HALF + h + 1)
                at = (hf * HALF + h) * DK
                dve.tensor_tensor(ur[rows, h, :, :], bc(v[rows, at:at + DK], 1, M),
                                  ps[rows, 4 + h, :].rearrange("p (m e) -> p m e", e=DK), ALU.subtract
                                  ).then_inc(s["rest_ready"], 1)

            def gated(g, hf):
                dve.wait_ge(s["o_ready"], g * HALVES + hf + 1)
                dve.tensor_tensor(ogT[:, 2 * hf:2 * hf + 2, :], ps[:, 2 + hf, 0:2 * P].rearrange("p (c t) -> p c t", t=P),
                                  gateT[:, 2 * hf:2 * hf + 2, :], ALU.mult).then_inc(s["o_gated"], 1)

            with dve.Fori(0, B) as g:
                ch = Chain(dve, s["dve_chain"], g, 2 + HALVES * (2 * (Q - 2) + 1) + norm.chained())
                ch.base = once.n + g * ch.per_turn
                dve.wait_ge(s["squared"], (g + 1) * 2)
                dve.tensor_reduce(ss, squares.rearrange("p (h e) -> p h e", e=DK), AX.X, ALU.add
                                  ).then_inc(s["squares_summed"], 1)
                dve.wait_ge(s["evacuated"], g * 3 + 2)
                ch(dve.tensor_tensor(decay, bt[:, DHEADS * M:], rho, ALU.mult))
                dve.tensor_scalar(decay, decay, 1e-6, None, ALU.max).then_inc(s["decays_clipped"], 1)
                dve.tensor_tensor(wb[:, :, :], bt[:, 0:DHEADS * M].rearrange("p (h m) -> p h m", m=M), modes[:, :, :],
                                  ALU.mult)
                dve.wait_ge(s["roots_ready"], g + 1)
                for j in range(2):
                    out = qkn[:, j * W:(j + 1) * W].rearrange("p (h e) -> p h e", e=DK)
                    a = dve.scalar_tensor_tensor(out=out, in0=ps[:, 1 + j, :].rearrange("p (h e) -> p h e", e=DK),
                                                 scalar=DK ** -0.5 if j else 1.0,
                                                 in1=bc(ss[:, j * DHEADS:(j + 1) * DHEADS], 2, DK),
                                                 op0=ALU.mult, op1=ALU.mult)
                a.then_inc(s["qk_normalised"], 1)
                dve.wait_ge(s["swapped_ready"], (g + 1) * 2)
                ch(dve.tensor_copy(norm.spare, qkS[:, 1, 0, 0:1]))
                rotate(g, 0, 0)
                rotate(g, 0, 1)
                for p in range(PACKS_):
                    evacuate(g, 0, p)
                    rotate(g, (p + 2) // PACKS_, (p + 2) % PACKS_)

                def second(p):
                    evacuate(g, 1, p)
                    if p + 2 < PACKS_:
                        rotate(g, 1, p + 2)
                invert(g, 0, ch, {4 + 7 * p: (lambda p=p: second(p)) for p in range(PACKS_)})
                steps = [(q, h) for q in range(1, NQ) for h in range(HALF)]
                invert(g, 1, ch, {6 + 2 * i: (lambda q=q, h=h: rest(g, 0, q, h)) for i, (q, h) in enumerate(steps)})
                gated(g, 0)
                for q, h in steps:
                    rest(g, 1, q, h)
                gated(g, 1)
                dve.wait_ge(s["y_ready"], g + 1)
                norm.add(dve, ch, g, 0, ps[:, 1, 0:D])
                norm.moments(dve, ch, g)
                norm.apply(dve, ch, g)
                ch.end()
    sem.release()


def experts_stage(k, stage):
    nc, ps, w, A = k.nc, k.psum, k.begin(stage), k.arena
    gated = stage == "L3_ffn"
    routed = w.wg.shape[2]
    E = k.dram["experts_" + stage].shape[0]
    FC = 1 if gated else 1024 // P
    sem = Semaphores(nc, stage)
    turned = Turned(k, sem, k.X, 4)
    norm = Norm(k, sem, k.X, k.X)
    logits_ready, combine_ready = sem("logits_ready"), sem("combine_ready")
    shifted, scores_ready = sem("logits_shifted"), sem("scores_ready")
    combineT_turned, combineT_ready, start_ready = sem("combineT_turned"), sem("combineT_ready"), sem("start_ready")
    arrived = [sem(f"expert_arrived_{s}") for s in range(2)]
    up_ready, silu_ready, h_ready = sem("up_ready"), sem("silu_ready"), sem("h_ready")
    y_ready, accumulated, dve_chain = sem("y_ready"), sem("accumulated"), sem("dve_chain")
    ones_set = sem("ones_set")

    words = k.dram["experts_" + stage].shape[2]
    xT = A(TURNS, C, N)
    ew = A(2, words)
    h = A(2, FC, N)
    sg = A(2, N) if gated else None
    comb = A(B, E)
    comb_now = A(2, B)
    combT = None if gated else A(B * P, rows=P)
    router = Router(k, w, routed, comb)
    ones = A(P)
    acc = k.Y
    F = FC * P

    def weights(s):
        a, at = ew[:, s, :], 0
        out = {}
        for name, shape in ([("w1", (C, F)), ("w3", (C, F)), ("w2", (FC, D))] if gated else
                            [("w1", (C, F)), ("w2", (FC, D)), ("b1", (FC,))]):
            n = int(np.prod(shape))
            out[name] = a[:, at:at + n] if len(shape) == 1 else a[:, at:at + n].rearrange("p (a b) -> p a b", b=shape[1])
            at += n
        return out

    W = [weights(0), weights(1)]
    STEPS = 2 * TURNS
    lg = ps[:, 0, 0:B * routed].rearrange("p (b e) -> p b e", e=routed)

    with nc.Block() as block:
        @block.sync
        def _(sp):
            def load(e, s):
                one = k.dram["experts_" + stage][bass.ds(e, 1), :, :].rearrange("a p n -> p (a n)")
                sp.dma_start(ew[:, s, :], one).then_inc(arrived[s], 16)
            load(0, 0)
            load(1, 1)
            k.prefetch(sp, stage)
            with sp.Fori(1, E // 2) as i:
                for s in range(2):
                    sp.wait_ge(y_ready, STEPS * i - TURNS + TURNS * s)
                    load(2 * i + s, s)

        @block.gpsimd
        def _(pool):
            k.wait_weights(pool, stage)
            pool.memset(ones[:, :], 1.0).then_inc(ones_set, 1)
            turned.stage(pool, 0)
            for g in range(TURNS - 1):
                turned.stage_next(pool, g)
            for g in range(TURNS):
                norm.roots(pool, g)

        @block.tensor
        def _(pe):
            k.wait_weights(pe, stage)
            pe.wait_ge(ones_set, 1)
            for g in range(TURNS):
                if g:
                    pe.wait_ge(turned.ready, g * C)
                turned.turn(pe, g)
            pe.wait_ge(turned.ready, TURNS * C)
            for b in range(B):
                g, u = divmod(b, TILES)
                for c in range(C):
                    mm = nc.tensor.matmul(lg[:, b, :], xT[:, g, c, u * P:(u + 1) * P], w.wg[:, c, :],
                                          start=(c == 0), stop=(gated and c == C - 1))
                if not gated:
                    mm = nc.tensor.matmul(lg[:, b, :], ones[0:1, :], w.bg[0:1, :], start=False, stop=True)
            mm.then_inc(logits_ready, 1)
            if not gated:
                pe.wait_ge(combine_ready, 1)
                for b in range(B):
                    mm = nc.tensor.transpose(ps[0:E, 4 + b // TILES, (b % TILES) * P:(b % TILES + 1) * P],
                                             comb[:, b, :], k.ident[:, :])
                mm.then_inc(combineT_turned, 1)
                pe.wait_ge(combineT_ready, 1)
                for half in range(2):
                    if half:
                        pe.wait_ge(accumulated, 1)
                    for j in range(B // 2):
                        b = half * B // 2 + j
                        mm = nc.tensor.matmul(ps[:, j // 2, (j % 2) * D:(j % 2 + 1) * D], combT[0:E, b * P:(b + 1) * P],
                                              w.b2[0:E, :], start=True, stop=True)
                    mm.then_inc(start_ready, 1)

            with pe.Fori(0, E // 2) as i:
                def up(m):
                    n = i * STEPS + m
                    s, g = divmod(m, TURNS)
                    if g == 0:
                        pe.wait_ge(arrived[s], 16 * (i + 1))
                    if m == 0:
                        pe.wait_ge(accumulated, n + 2)
                    for f in range(FC):
                        for part, name in enumerate(("w1", "w3") if gated else ("w1",)):
                            if gated:
                                bank = 2 * (m % 2) + part
                                if part == 0 and m >= 2:
                                    pe.wait_ge(h_ready, n - 1)
                            else:
                                bank = f % 4
                                if m or f >= 4:
                                    pe.wait_ge(h_ready, n * FC + f - 3)
                            for c in range(C):
                                mm = nc.tensor.matmul(ps[:, bank, :], W[s][name][:, c, f * P:(f + 1) * P], xT[:, g, c, :],
                                                      start=(c == 0), stop=(c == C - 1))
                        mm.then_inc(up_ready, 1)

                def down(m):
                    n = i * STEPS + m
                    s = m // TURNS
                    pe.wait_ge(h_ready, (n + 1) * FC)
                    pe.wait_ge(accumulated, n + 1)
                    for u in range(TILES):
                        out = ps[:, 4 + 2 * (m % 2) + u // 2, (u % 2) * D:(u % 2 + 1) * D]
                        for f in range(FC):
                            mm = nc.tensor.matmul(out, h[:, m % 2, f, u * P:(u + 1) * P], W[s]["w2"][:, f, :],
                                                  start=(f == 0), stop=(f == FC - 1))
                    mm.then_inc(y_ready, 1)

                for m in range(STEPS):
                    up(m)
                    if m:
                        down(m - 1)
                down(STEPS - 1)

        @block.scalar
        def _(act):
            k.wait_weights(act, stage)
            for g in range(TURNS):
                turned.copy(act, g, xT[:, g, :, :])
            if gated:
                act.wait_ge(logits_ready, 1)
                nc.scalar.activation(router.scores, lg, ACT.Sigmoid).then_inc(scores_ready, 1)
            else:
                act.wait_ge(shifted, 1)
                nc.scalar.activation(router.scores, router.scores, ACT.Exp).then_inc(scores_ready, 1)
                act.wait_ge(combineT_turned, 1)
                nc.scalar.copy(combT[0:E, :], ps[0:E, 4:8, :].rearrange("p a b -> p (a b)")).then_inc(combineT_ready, 1)
            with act.Fori(0, E // 2) as i:
                for m in range(STEPS):
                    n = i * STEPS + m
                    s = m // TURNS
                    for f in range(FC):
                        act.wait_ge(up_ready, n * FC + f + 1)
                        if gated:
                            nc.scalar.activation(sg[:, m % 2, :], ps[:, 2 * (m % 2), :], ACT.Silu).then_inc(silu_ready, 1)
                        else:
                            if m >= 2 and f == 0:
                                act.wait_ge(y_ready, n - 1)
                            nc.scalar.activation(h[:, m % 2, f, :], ps[:, f % 4, :], ACT.Silu,
                                                 bias=W[s]["b1"][:, f:f + 1]).then_inc(h_ready, 1)

        @block.vector
        def _(dve):
            k.wait_weights(dve, stage)
            chain = Chain(dve, dve_chain)
            norm.open(dve)
            if gated:
                dve.wait_ge(scores_ready, 1)
                router.grouped(dve, chain).then_inc(combine_ready, 1)
            else:
                dve.wait_ge(logits_ready, 1)
                router.top1(dve, chain, lg).then_inc(shifted, 1)
                dve.wait_ge(scores_ready, 1)
                router.top1_weight(dve, chain).then_inc(combine_ready, 1)
            dve.wait_ge(combine_ready, 1)
            if gated:
                dve.memset(acc[:, :, :], 0.0).then_inc(accumulated, 2)
                dve.wait_ge(accumulated, 2)
            else:
                for half in range(2):
                    dve.wait_ge(start_ready, half + 1)
                    dve.tensor_copy(acc[:, half * B // 2:(half + 1) * B // 2, :],
                                    ps[:, 0:4, :].rearrange("p a (b d) -> p (a b) d", d=D)).then_inc(accumulated, 1)
                dve.wait_ge(accumulated, 2)
            with dve.Fori(0, E // 2) as i:
                def accumulate(m):
                    n = i * STEPS + m
                    s, g = divmod(m, TURNS)
                    dve.wait_ge(y_ready, n + 1)
                    dve.wait_ge(accumulated, n + 2)
                    for u in range(TILES):
                        b = g * TILES + u
                        a = dve.scalar_tensor_tensor(
                            out=acc[:, b, :], in0=ps[:, 4 + 2 * (m % 2) + u // 2, (u % 2) * D:(u % 2 + 1) * D],
                            scalar=comb_now[:, s, b:b + 1], in1=acc[:, b, :], op0=ALU.mult, op1=ALU.add)
                    a.then_inc(accumulated, 1)

                dve.wait_ge(accumulated, STEPS * i + 2)
                dve.tensor_copy(comb_now[:, :, :], comb[:, :, bass.ds(2 * i, 2)].rearrange("p b s -> p s b")
                                ).then_inc(combine_ready, 1)
                dve.wait_ge(combine_ready, i + 2)
                for m in range(STEPS):
                    n = i * STEPS + m
                    if gated:
                        dve.wait_ge(silu_ready, n + 1)
                        if m >= 2:
                            dve.wait_ge(y_ready, n - 1)
                        dve.tensor_tensor(h[:, m % 2, 0, :], sg[:, m % 2, :], ps[:, 2 * (m % 2) + 1, :], ALU.mult
                                          ).then_inc(h_ready, 1)
                    if m:
                        accumulate(m - 1)
                accumulate(STEPS - 1)
            for g in range(TURNS):
                for u in range(TILES):
                    if g == 0 and u == 0:
                        dve.wait_ge(accumulated, E * TURNS + 2)
                    norm.add(dve, chain, g, u, acc[:, g * TILES + u, :])
                norm.moments(dve, chain, g)
                norm.apply(dve, chain, g)
    sem.release()


def rank(dve, chain, out, s, n, before, tmp, tmp2):
    i_ = bc(s, 3, n)
    j_ = bc(s, 2, n)
    chain(dve.tensor_tensor(tmp, j_, i_, ALU.is_gt))
    chain(dve.tensor_tensor(tmp2, j_, i_, ALU.is_equal))
    chain(dve.tensor_tensor(tmp2, tmp2, bc(before, 1, B), ALU.mult))
    chain(dve.tensor_tensor(tmp, tmp, tmp2, ALU.add))
    chain(dve.tensor_reduce(out, tmp, AX.X, ALU.add))


class Router:

    def __init__(self, k, w, n, comb):
        self.w, self.n, self.comb, A = w, n, comb, k.arena
        self.scores, self.masked, self.place = A(B, n), A(B, n), A(B, n)
        self.t1, self.t2 = A(B, n, n), A(B, n, n)
        self.a, self.b, self.c = A(B * 4), A(B * 4), A(B * 4)

    def top1(self, dve, chain, logits):
        chain(dve.tensor_reduce(self.a[:, 0:B], logits, AX.X, ALU.max))
        chain(dve.tensor_tensor(self.scores, logits, bc(self.a[:, 0:B], 2, self.n), ALU.subtract))
        rank(dve, chain, self.place, self.scores, self.n, self.w.before, self.t1, self.t2)
        return dve.tensor_scalar(self.comb, self.place, 0.5, None, ALU.is_lt)

    def top1_weight(self, dve, chain):
        chain(dve.tensor_reduce(self.a[:, 0:B], self.scores, AX.X, ALU.add))
        chain(dve.reciprocal(self.b[:, 0:B], self.a[:, 0:B]))
        return dve.tensor_tensor(self.comb, self.comb, bc(self.b[:, 0:B], 2, self.n), ALU.mult)

    def grouped(self, dve, chain):
        G, J = 4, self.n // 4
        s = self.scores.rearrange("p b (g j) -> p (b g) j", j=J)
        q = [s[:, :, j] for j in range(J)]
        a, b, c = self.a, self.b, self.c
        t = self.t1.rearrange("p b i j -> p (b i j)")[:, 0:B * G]
        chain(dve.tensor_tensor(a, q[0], q[1], ALU.max))
        chain(dve.tensor_tensor(b, q[0], q[1], ALU.min))
        chain(dve.tensor_tensor(c, q[2], q[3], ALU.max))
        chain(dve.tensor_tensor(t, q[2], q[3], ALU.min))
        chain(dve.tensor_tensor(b, b, t, ALU.max))
        chain(dve.tensor_tensor(t, a, c, ALU.min))
        chain(dve.tensor_tensor(b, b, t, ALU.max))
        chain(dve.tensor_tensor(a, a, c, ALU.max))
        chain(dve.tensor_tensor(a, a, b, ALU.add))
        small = [x.rearrange("p b i j -> p (b i j)")[:, 0:B * G * G].rearrange("p (b i j) -> p b i j", i=G, j=G)
                 for x in (self.t1, self.t2)]
        rank(dve, chain, b.rearrange("p (b g) -> p b g", g=G), a.rearrange("p (b g) -> p b g", g=G), G,
             self.w.before[:, 0:G, 0:G], *small)
        chain(dve.tensor_scalar(a, b, 1.5, None, ALU.is_lt))
        chain(dve.tensor_scalar(b, a, 1.0, None, ALU.subtract))
        m = self.masked.rearrange("p b (g j) -> p (b g) j", j=J)
        chain(dve.tensor_tensor(m, s, bc(a, 2, J), ALU.mult))
        chain(dve.tensor_tensor(m, m, bc(b, 2, J), ALU.add))
        rank(dve, chain, self.place, self.masked, self.n, self.w.before, self.t1, self.t2)
        chain(dve.tensor_scalar(self.place, self.place, 3.5, None, ALU.is_lt))
        chain(dve.tensor_tensor(self.masked, self.scores, self.place, ALU.mult))
        chain(dve.tensor_reduce(a[:, 0:B], self.masked, AX.X, ALU.add))
        chain(dve.tensor_scalar(a[:, 0:B], a[:, 0:B], 1e-6, None, ALU.add))
        chain(dve.reciprocal(b[:, 0:B], a[:, 0:B]))
        chain(dve.tensor_tensor(self.comb[:, :, 0:self.n], self.masked, bc(b[:, 0:B], 2, self.n), ALU.mult))
        return dve.memset(self.comb[:, :, self.n:], 1.0)


def linear_attention_stage(k):
    stage = "L0_xattn"
    nc, ps, w, A = k.nc, k.psum, k.begin(stage), k.arena
    sem = Semaphores(nc, stage)
    turned, norm = Turned(k, sem, k.X, 4), Norm(k, sem, k.X, k.X)
    xT = turned.xT
    QS, KS = C * TILES, TILES * H
    ones_set, loaded, mask_loaded, keep_ready = sem("ones_set"), sem("loaded"), sem("mask_loaded"), sem("keep_ready")
    qk_projected, v_projected, v_ready = sem("qk_projected"), sem("v_projected"), sem("v_ready")
    clipped, exp_ready = sem("clipped"), sem("exp_ready")
    squares_ready, roots_ready, scaled = sem("squares_ready"), sem("roots_ready"), sem("scaled")
    kv_ready, kv_masked, oT_ready, oT_copied = sem("kv_ready"), sem("kv_masked"), sem("oT_ready"), sem("oT_copied")
    y_ready, dve_chain = sem("y_ready"), sem("dve_chain")
    ones, cT = A(P), A(C, N)
    low, high = A(4, N), A(4, N)
    v = A(TILES, D)
    squares, exponent = A(QS + KS), A(QS + KS)
    kv, oT = A(TILES * C, P), A(TILES * C, P)
    pad, keep = A(B, dtype=U8), A(B)
    kv_psum = ps[:, 4:6, :].rearrange("p a (b e) -> p (a b) e", e=P)
    oT_psum = ps[:, 0:2, :].rearrange("p a (b e) -> p (a b) e", e=P)

    with nc.Block() as block:
        @block.sync
        def _(sp):
            sp.dma_start(pad, k.dram["padding"]).then_inc(mask_loaded, 16)
            sp.dma_start(cT[:, :, :], k.ctxT[0]).then_inc(loaded, 16)
            k.prefetch(sp, stage)
            with sp.Fori(1, TURNS) as g:
                sp.wait_ge(v_projected, g * 2)
                sp.dma_start(cT[:, :, :], k.ctxT[bass.ds(g, 1)].rearrange("a p c n -> p (a c) n")).then_inc(loaded, 16)

        @block.gpsimd
        def _(pool):
            pool.memset(ones, 1.0).then_inc(ones_set, 1)
            pool.memset(exponent, -0.5).then_inc(ones_set, 1)
            pool.wait_ge(ones_set, 2)
            turned.stage(pool, 0)

            def roots(g):
                pool.wait_ge(squares_ready, g + 1)
                pool.tensor_tensor(squares, squares, exponent, ALU.pow).then_inc(roots_ready, 1)

            with pool.Fori(0, TURNS - 1) as g:
                turned.stage_next(pool, g)
                roots(g)
                norm.roots(pool, g)
            roots(TURNS - 1)
            norm.roots(pool, TURNS - 1)

        @block.tensor
        def _(pe):
            k.wait_weights(pe, stage)
            pe.wait_ge(ones_set, 1)
            with pe.Fori(0, TURNS) as g:
                turned.turn(pe, g)
                pe.wait_ge(turned.ready, (g + 1) * C)
                for co in range(C):
                    for ci in range(C):
                        mm = nc.tensor.matmul(ps[:, co, :], w.wq[:, ci, co * P:(co + 1) * P], xT[:, ci, :],
                                              start=(ci == 0), stop=(ci == C - 1))
                    mm.then_inc(qk_projected, 1)
                pe.wait_ge(loaded, 16 * (g + 1))
                norm.wait_added(pe, g * TILES)
                for m, b, bank, done in ((w.wk, w.bk, 2, qk_projected), (w.wv, w.bv, 6, v_projected)):
                    for u in range(TILES):
                        out = ps[:, bank + u // 2, (u % 2) * D:(u % 2 + 1) * D]
                        for ci in range(C):
                            nc.tensor.matmul(out, cT[:, ci, u * P:(u + 1) * P], m[:, ci, :], start=(ci == 0), stop=False)
                        mm = nc.tensor.matmul(out, ones[0:1, :], b[0:1, :], start=False, stop=True)
                        if u % 2:
                            mm.then_inc(done, 1)
                pe.wait_ge(scaled, (g + 1) * 2)
                pe.wait_ge(v_ready, (g + 1) * 2)
                for u in range(TILES):
                    for c in range(C):
                        mm = nc.tensor.matmul(kv_psum[:, u * C + c, :],
                                              low[:, 2 + u // 2, (u % 2) * D + c * P:(u % 2) * D + (c + 1) * P],
                                              v[:, u, c * P:(c + 1) * P], start=True, stop=True)
                mm.then_inc(kv_ready, 1)
                pe.wait_ge(kv_masked, g + 1)
                for u in range(TILES):
                    for c in range(C):
                        mm = nc.tensor.matmul(oT_psum[:, u * C + c, :], kv[:, u * C + c, :],
                                              low[:, c, u * P:(u + 1) * P], start=True, stop=True)
                mm.then_inc(oT_ready, 1)
                pe.wait_ge(oT_copied, g + 1)
                for u in range(TILES):
                    out = ps[:, 2 + u // 2, (u % 2) * D:(u % 2 + 1) * D]
                    for c in range(C):
                        nc.tensor.matmul(out, oT[:, u * C + c, :], w.wo[:, c, :], start=(c == 0), stop=False)
                    mm = nc.tensor.matmul(out, ones[0:1, :], w.bo[0:1, :], start=False, stop=True)
                mm.then_inc(y_ready, 1)

        @block.scalar
        def _(act):
            k.wait_weights(act, stage)
            with act.Fori(0, TURNS) as g:
                turned.copy(act, g)
                for i in range(4):
                    act.wait_ge(clipped, g * 4 + i + 1)
                    bias = w.bq[:, i:i + 1] if i < C else 0.0
                    nc.scalar.activation(high[:, i, :], ps[:, i, :], ACT.Relu, bias=bias)
                    nc.scalar.activation(low[:, i, :], low[:, i, :], ACT.Exp).then_inc(exp_ready, 1)
                for i in range(2):
                    act.wait_ge(v_projected, g * 2 + i + 1)
                    nc.scalar.copy(v[:, 2 * i:2 * i + 2, :], ps[:, 6 + i, :].rearrange("p (u d) -> p u d", d=D)
                                   ).then_inc(v_ready, 1)
                act.wait_ge(oT_ready, g + 1)
                nc.scalar.copy(oT[:, :, :], oT_psum).then_inc(oT_copied, 1)

        @block.vector
        def _(dve):
            k.wait_weights(dve, stage)
            norm.open(dve)
            dve.wait_ge(mask_loaded, 16)
            dve.tensor_scalar(keep, pad, -1.0, 1.0, ALU.mult, ALU.add).then_inc(keep_ready, 1)
            dve.wait_ge(keep_ready, 1)
            with dve.Fori(0, TURNS) as g:
                chain = Chain(dve, dve_chain, g, 3 * 4 + 1 + norm.chained())
                for i in range(4):
                    dve.wait_ge(qk_projected, g * 4 + i + 1)
                    bias = w.bq[:, i:i + 1] if i < C else 0.0
                    dve.tensor_scalar(low[:, i, :], ps[:, i, :], bias, 0.0, ALU.add, ALU.min).then_inc(clipped, 1)
                for i in range(4):
                    dve.wait_ge(exp_ready, g * 4 + i + 1)
                    chain(dve.tensor_tensor(low[:, i, :], low[:, i, :], high[:, i, :], ALU.add))
                    chain(dve.tensor_tensor(high[:, i, :], low[:, i, :], low[:, i, :], ALU.mult))
                    if i < C:
                        chain(dve.tensor_reduce(squares[:, i * TILES:(i + 1) * TILES],
                                                high[:, i, :].rearrange("p (u t) -> p u t", t=P), AX.X, ALU.add))
                    else:
                        at = QS + (i - C) * 2 * H
                        chain(dve.tensor_reduce(squares[:, at:at + 2 * H],
                                                high[:, i, :].rearrange("p (h e) -> p h e", e=DH), AX.X, ALU.add))
                dve.tensor_scalar(squares, squares, 1e-24, None, ALU.max).then_inc(squares_ready, 1)
                dve.wait_ge(roots_ready, g + 1)
                kq = squares[:, QS:].rearrange("p (u h) -> p u h", h=H)
                chain(dve.tensor_tensor(kq, kq, bc(keep[:, bass.ds(g * TILES, TILES)], 2, H), ALU.mult))
                q = low[:, 0:C, :].rearrange("p c (u t) -> p (c u) t", t=P)
                dve.tensor_tensor(q, q, bc(squares[:, 0:QS], 2, P), ALU.mult).then_inc(scaled, 1)
                kk = low[:, 2:4, :].rearrange("p a (h e) -> p (a h) e", e=DH)
                dve.tensor_tensor(kk, kk, bc(squares[:, QS:], 2, DH), ALU.mult).then_inc(scaled, 1)
                dve.wait_ge(kv_ready, g + 1)
                dve.tensor_tensor(kv[:, :, :], kv_psum, bc(w.blocks, 1, TILES * C), ALU.mult).then_inc(kv_masked, 1)
                dve.wait_ge(y_ready, g + 1)
                for u in range(TILES):
                    norm.add(dve, chain, g, u, ps[:, 2 + u // 2, (u % 2) * D:(u % 2 + 1) * D])
                norm.moments(dve, chain, g)
                norm.apply(dve, chain, g)
                chain.end()
    sem.release()


def recall_stage(k):
    stage = "L2_recall"
    nc, ps, w, A = k.nc, k.psum, k.begin(stage), k.arena
    sem = Semaphores(nc, stage)
    turned = Turned(k, sem, k.X, 4)
    xT = turned.xT
    loaded, q_projected, q_ready = sem("loaded"), sem("q_projected"), sem("q_ready")
    kv_projected, kv_ready, scores_ready, chosen = sem("kv_projected"), sem("kv_ready"), sem("scores_ready"), sem("chosen")
    chosen_turned, chosenT_ready, recalled, stored = sem("chosen_turned"), sem("chosenT_ready"), sem("recalled"), sem("stored")
    dve_chain = sem("dve_chain")
    R = P + DH
    cT, qT = A(C, N), A(C, N)
    kvp = A(TILES, R)
    best, one, oneT = A(TILES), A(TILES, P), A(TILES, P)
    s_psum = ps[:, 6, :].rearrange("p (u t) -> p u t", t=P)
    oneT_psum = ps[:, 7, :].rearrange("p (u t) -> p u t", t=P)

    with nc.Block() as block:
        @block.sync
        def _(sp):
            sp.dma_start(cT[:, :, :], k.ctxT[0]).then_inc(loaded, 16)
            k.prefetch(sp, stage)
            with sp.Fori(1, TURNS) as g:
                sp.wait_ge(scores_ready, g)
                sp.dma_start(cT[:, :, :], k.ctxT[bass.ds(g, 1)].rearrange("a p c n -> p (a c) n")).then_inc(loaded, 16)

        @block.gpsimd
        def _(pool):
            turned.stage(pool, 0)
            with pool.Fori(0, TURNS - 1) as g:
                turned.stage_next(pool, g)

        @block.tensor
        def _(pe):
            k.wait_weights(pe, stage)
            with pe.Fori(0, TURNS) as g:
                turned.turn(pe, g)
                pe.wait_ge(turned.ready, (g + 1) * C)
                for co in range(C):
                    for ci in range(C):
                        mm = nc.tensor.matmul(ps[:, co, :], w.wq[:, ci, co * P:(co + 1) * P], xT[:, ci, :],
                                              start=(ci == 0), stop=(ci == C - 1))
                    mm.then_inc(q_projected, 1)
                pe.wait_ge(loaded, 16 * (g + 1))
                for u in range(TILES):
                    for ci in range(C):
                        mm = nc.tensor.matmul(ps[:, 2 + u // 2, (u % 2) * D:(u % 2) * D + R],
                                              cT[:, ci, u * P:(u + 1) * P], w.wkv[:, ci, :],
                                              start=(ci == 0), stop=(ci == C - 1))
                    if u % 2:
                        mm.then_inc(kv_projected, 1)
                pe.wait_ge(q_ready, (g + 1) * C)
                for u in range(TILES):
                    for ci in range(C):
                        mm = nc.tensor.matmul(s_psum[:, u, :], qT[:, ci, u * P:(u + 1) * P], cT[:, ci, u * P:(u + 1) * P],
                                              start=(ci == 0), stop=(ci == C - 1))
                mm.then_inc(scores_ready, 1)
                pe.wait_ge(chosen, g + 1)
                for u in range(TILES):
                    mm = nc.tensor.transpose(oneT_psum[:, u, :], one[:, u, :], k.ident)
                mm.then_inc(chosen_turned, 1)
                pe.wait_ge(chosenT_ready, g + 1)
                pe.wait_ge(kv_ready, (g + 1) * 2)
                for u in range(TILES):
                    nc.tensor.matmul(ps[:, 0, u * P:(u + 1) * P], kvp[:, u, 0:P], oneT[:, u, :], start=True, stop=True)
                    mm = nc.tensor.matmul(ps[:, 1, u * DH:(u + 1) * DH], oneT[:, u, :], kvp[:, u, P:R], start=True, stop=True)
                mm.then_inc(recalled, 1)
                pe.wait_ge(stored, g + 1)

        @block.scalar
        def _(act):
            with act.Fori(0, TURNS) as g:
                turned.copy(act, g)
                for c in range(C):
                    act.wait_ge(q_projected, g * C + c + 1)
                    nc.scalar.copy(qT[:, c, :], ps[:, c, :]).then_inc(q_ready, 1)
                for i in range(2):
                    act.wait_ge(kv_projected, g * 2 + i + 1)
                    nc.scalar.copy(kvp[:, 2 * i:2 * i + 2, :], ps[:, 2 + i, :].rearrange("p (u d) -> p u d", d=D)[:, :, 0:R]
                                   ).then_inc(kv_ready, 1)
                act.wait_ge(chosen_turned, g + 1)
                nc.scalar.copy(oneT[:, :, :], oneT_psum).then_inc(chosenT_ready, 1)

        @block.vector
        def _(dve):
            k.wait_weights(dve, stage)
            chain = Chain(dve, dve_chain)
            chain(dve.memset(k.Y[:, :, P + DH:P + DH + 1], 1.0))
            with dve.Fori(0, TURNS) as g:
                ch = Chain(dve, dve_chain)
                ch.base = 1 + g * 5
                dve.wait_ge(scores_ready, g + 1)
                ch(dve.tensor_reduce(best, s_psum, AX.X, ALU.max))
                ch(dve.tensor_tensor(one[:, :, :], s_psum, bc(best, 2, P), ALU.is_equal))
                ch(dve.tensor_tensor(one[:, :, :], one[:, :, :], bc(w.countdown, 1, TILES), ALU.mult))
                ch(dve.tensor_reduce(best, one[:, :, :], AX.X, ALU.max))
                dve.tensor_tensor(one[:, :, :], one[:, :, :], bc(best, 2, P), ALU.is_equal).then_inc(chosen, 1)
                dve.wait_ge(recalled, g + 1)
                t = bass.ds(g * TILES, TILES)
                ch(dve.tensor_copy(k.Y[:, t, 0:P], ps[:, 0, :].rearrange("p (u t) -> p u t", t=P)))
                dve.tensor_copy(k.Y[:, t, P:P + DH], ps[:, 1, 0:TILES * DH].rearrange("p (u e) -> p u e", e=DH)
                                ).then_inc(stored, 1)
                assert ch.n == 5
    sem.release()


def correlation_stage(k):
    stage = "L2_attn"
    nc, ps, w, A = k.nc, k.psum, k.begin(stage), k.arena
    sem = Semaphores(nc, stage)
    PAIR = 2
    PAIRS = B // PAIR
    SL = PAIR * C
    FR = P // 2 + 1
    ROUNDS = P // 8
    norm = Norm(k, sem, k.X, k.X, tiles=PAIR)
    staged, x_turned, xT_ready, ones_set = sem("x_staged"), sem("x_turned"), sem("xT_ready"), sem("ones_set")
    qk_projected, qk_ready, v_projected, v_masked = sem("qk_projected"), sem("qk_ready"), sem("v_projected"), sem("v_masked")
    spectra_ready, k_copied, product_ready = sem("spectra_ready"), sem("k_copied"), sem("product_ready")
    corr_ready, corr_copied, shifted, exp_ready = sem("corr_ready"), sem("corr_copied"), sem("shifted"), sem("exp_ready")
    weights_ready, oT_ready, oT_copied, y_ready = sem("weights_ready"), sem("oT_ready"), sem("oT_copied"), sem("y_ready")
    dve_chain = sem("dve_chain")
    xs, xT = A(PAIR, D), A(C, PAIR * P)
    ones = A(P)
    q, kk = A(PAIR * D), A(PAIR * D)
    vb = A(PAIR, C, P)
    kspec = A(2, N)
    t1, t2, re, im = A(N), A(N), A(N), A(N)
    unsorted, ranked = A(SL, P), A(SL, P)
    total, oT, spare = A(SL), A(SL, P), A(2 * ROUNDS + 1)
    xfirst = A(C, PAIR, HH, DH)

    with nc.Block() as block:
        @block.sync
        def _(sp):
            k.prefetch(sp, stage)

        @block.gpsimd
        def _(pool):
            pool.memset(ones, 1.0).then_inc(ones_set, 1)

            def stage_x(g):
                pool.tensor_copy(xs[:, :, :], k.X[:, bass.ds(g * PAIR, PAIR), :]).then_inc(staged, 1)

            stage_x(0)
            with pool.Fori(0, PAIRS - 1) as g:
                pool.wait_ge(x_turned, g + 1)
                stage_x(g + 1)
                norm.roots(pool, g)
            norm.roots(pool, PAIRS - 1)

        @block.tensor
        def _(pe):
            k.wait_weights(pe, stage)
            pe.wait_ge(ones_set, 1)
            with pe.Fori(0, PAIRS) as g:
                pe.wait_ge(staged, g + 1)
                for c in range(C):
                    for u in range(PAIR):
                        mm = nc.tensor.transpose(ps[:, 0, c * PAIR * P + u * P:c * PAIR * P + (u + 1) * P],
                                                 xs[:, u, c * P:(c + 1) * P], k.ident)
                mm.then_inc(x_turned, 1)
                pe.wait_ge(xT_ready, (g + 1) * 2)
                for i, (m, b) in enumerate(((w.wq, w.bq), (w.wk, w.bk))):
                    for u in range(PAIR):
                        out = ps[:, 1 + i, u * D:(u + 1) * D]
                        for ci in range(C):
                            nc.tensor.matmul(out, xT[:, ci, u * P:(u + 1) * P], m[:, ci, :], start=(ci == 0), stop=False)
                        mm = nc.tensor.matmul(out, ones[0:1, :], b[0:1, :], start=False, stop=True)
                    mm.then_inc(qk_projected, 1)
                for u in range(PAIR):
                    out = ps[:, 3, u * D:(u + 1) * D]
                    for ci in range(C):
                        nc.tensor.matmul(out, xfirst[:, ci, u, :, :].rearrange("p h e -> p (h e)"), w.wv[:, ci, :],
                                         start=(ci == 0), stop=False)
                    mm = nc.tensor.matmul(out, ones[0:1, :], w.bv[0:1, :], start=False, stop=True)
                mm.then_inc(v_projected, 1)
                pe.wait_ge(qk_ready, (g + 1) * 2)
                for i, x in enumerate((q, kk)):
                    for j, table in enumerate((w.dcos, w.dsin)):
                        mm = nc.tensor.matmul(ps[0:FR, 4 + 2 * i + j, :], table, x, start=True, stop=True)
                    mm.then_inc(spectra_ready, 1)
                pe.wait_ge(product_ready, (g + 1) * 2)
                for u in range(PAIR):
                    for c in range(C):
                        at = u * D + c * P
                        out = ps[:, 0, (u * C + c) * P:(u * C + c + 1) * P]
                        nc.tensor.matmul(out, re[0:FR, at:at + P], w.icos[0:FR, :], start=True, stop=False)
                        mm = nc.tensor.matmul(out, im[0:FR, at:at + P], w.isin[0:FR, :], start=False, stop=True)
                mm.then_inc(corr_ready, 1)
                pe.wait_ge(weights_ready, g + 1)
                pe.wait_ge(v_masked, g + 1)
                for u in range(PAIR):
                    for c in range(C):
                        s = u * C + c
                        mm = nc.tensor.matmul(ps[:, 1, s * P:(s + 1) * P], vb[:, u, c, :], ranked[:, s, :],
                                              start=True, stop=True)
                mm.then_inc(oT_ready, 1)
                pe.wait_ge(oT_copied, g + 1)
                for u in range(PAIR):
                    out = ps[:, 2, u * D:(u + 1) * D]
                    for c in range(C):
                        nc.tensor.matmul(out, oT[:, u * C + c, :], w.wo[:, c, :], start=(c == 0), stop=False)
                    mm = nc.tensor.matmul(out, ones[0:1, :], w.bo[0:1, :], start=False, stop=True)
                mm.then_inc(y_ready, 1)
                norm.wait_added(pe, (g + 1) * PAIR)

        @block.scalar
        def _(act):
            with act.Fori(0, PAIRS) as g:
                act.wait_ge(x_turned, g + 1)
                turned = ps[:, 0, :].rearrange("p (c u t) -> p c u t", c=C, u=PAIR)
                nc.scalar.copy(xT[:, :, :], ps[:, 0, :].rearrange("p (c n) -> p c n", c=C)).then_inc(xT_ready, 1)
                for c in range(C):
                    a = nc.scalar.copy(xfirst[:, c, :, :, :], bc(turned[:, c, :, 0:DH], 2, HH))
                a.then_inc(xT_ready, 1)
                for i, to in enumerate((q, kk)):
                    act.wait_ge(qk_projected, g * 2 + i + 1)
                    nc.scalar.copy(to, ps[:, 1 + i, :]).then_inc(qk_ready, 1)
                act.wait_ge(spectra_ready, g * 2 + 2)
                nc.scalar.copy(kspec[0:FR, :, :], ps[0:FR, 6:8, :]).then_inc(k_copied, 1)
                act.wait_ge(corr_ready, g + 1)
                nc.scalar.copy(unsorted[:, :, :], ps[:, 0, :].rearrange("p (s t) -> p s t", t=P)).then_inc(corr_copied, 1)
                act.wait_ge(shifted, g + 1)
                nc.scalar.activation(ranked[:, :, :], ranked[:, :, :], ACT.Exp).then_inc(exp_ready, 1)
                act.wait_ge(oT_ready, g + 1)
                nc.scalar.copy(oT[:, :, :], ps[:, 1, :].rearrange("p (s t) -> p s t", t=P)).then_inc(oT_copied, 1)

        @block.vector
        def _(dve):
            k.wait_weights(dve, stage)
            norm.open(dve)
            with dve.Fori(0, PAIRS) as g:
                chain = Chain(dve, dve_chain, g, 4 + 2 * ROUNDS - 1 + 3 + norm.chained())
                dve.wait_ge(v_projected, g + 1)
                dve.tensor_tensor(vb[:, :, :, :], ps[:, 3, :].rearrange("p (u c e) -> p u c e", c=C, e=P),
                                  bc(bc(w.blocks, 1, C), 1, PAIR), ALU.mult).then_inc(v_masked, 1)
                dve.wait_ge(k_copied, g + 1)
                f = slice(0, FR)
                qc, qs, kc, ks = ps[f, 4, :], ps[f, 5, :], kspec[f, 0, :], kspec[f, 1, :]
                chain(dve.tensor_tensor(t1[f], qc, kc, ALU.mult))
                chain(dve.tensor_tensor(t2[f], qs, ks, ALU.mult))
                dve.tensor_tensor(re[f], t1[f], t2[f], ALU.add).then_inc(product_ready, 1)
                dve.wait_ge(product_ready, 2 * g + 1)
                chain(dve.tensor_tensor(t1[f], qc, ks, ALU.mult))
                chain(dve.tensor_tensor(t2[f], qs, kc, ALU.mult))
                dve.tensor_tensor(im[f], t1[f], t2[f], ALU.subtract).then_inc(product_ready, 1)
                dve.wait_ge(corr_copied, g + 1)
                dve.tensor_copy(spare[:, 2 * ROUNDS:2 * ROUNDS + 1], unsorted[:, 0, 0:1])
                for r in range(ROUNDS):
                    for s in range(SL):
                        top = dve.max(ranked[:, s, 8 * r:8 * r + 8], unsorted[:, s, :])
                    chain(top)
                    dve.tensor_copy(spare[:, 2 * r:2 * r + 1], ranked[:, SL - 1, 8 * r:8 * r + 1])
                    if r < ROUNDS - 1:
                        for s in range(SL):
                            left = dve.match_replace(unsorted[:, s, :], ranked[:, s, 8 * r:8 * r + 8],
                                                     unsorted[:, s, :], -3e38)
                        chain(left)
                        dve.tensor_copy(spare[:, 2 * r + 1:2 * r + 2], unsorted[:, SL - 1, 0:1])
                chain(dve.tensor_copy(total, ranked[:, :, 0]))
                dve.tensor_tensor(ranked[:, :, :], ranked[:, :, :], bc(total, 2, P), ALU.subtract).then_inc(shifted, 1)
                dve.wait_ge(exp_ready, g + 1)
                chain(dve.tensor_reduce(total, ranked[:, :, :], AX.X, ALU.add))
                chain(dve.reciprocal(total, total))
                dve.tensor_tensor(ranked[:, :, :], ranked[:, :, :], bc(total, 2, P), ALU.mult).then_inc(weights_ready, 1)
                dve.wait_ge(y_ready, g + 1)
                for u in range(PAIR):
                    norm.add(dve, chain, g, u, ps[:, 2, u * D:(u + 1) * D])
                norm.moments(dve, chain, g)
                norm.apply(dve, chain, g)
                chain.end()
    sem.release()

QMAX = 127.0
MAGIC = 1.5 * 2.0 ** 23
ABSMAX = bass.bass_isa.ReduceOp.absmax
SUM = bass.bass_isa.ReduceOp.add


def int8_ffn_stage(k):
    stage = "L1_ffn"
    nc, ps, w, A = k.nc, k.psum, k.begin(stage), k.arena
    sem = Semaphores(nc, stage)
    turned, norm = Turned(k, sem, k.X, 4), Norm(k, sem, k.X, k.X)
    IC = w.gate.shape[1]
    IP = w.down.shape[2] // IC
    ones_set, ident_ready = sem("ones_set"), sem("ident_ready")
    x_measured, x_max, clips = sem("x_measured"), sem("x_max"), sem("clips_ready")
    w_quantized, w_turned, wT_ready = sem("weights_quantized"), sem("weights_turned"), sem("weightsT_ready")
    scales_spread = sem("down_scales_spread")
    x_rounded, xq_ready = sem("x_rounded"), sem("xq_ready")
    up_ready, silu_ready, h_ready = sem("up_ready"), sem("silu_ready"), sem("h_ready")
    h_measured, h_max, h_rounded, hq_ready = sem("h_measured"), sem("h_max"), sem("h_rounded"), sem("hq_ready")
    y_ready, dve_chain, scale_ready = sem("y_ready"), sem("dve_chain"), sem("scale_ready")

    identb = A(P, dtype=BF16)
    ones = A(P)
    wmax, winv, wscale = A(3 * IC), A(3 * IC), A(3 * IC)
    wgT, wuT = A(C, IC * IP, dtype=BF16), A(C, IC * IP, dtype=BF16)
    wdT = A(IC, D, dtype=BF16)
    diag, down_scale = A(C, P), A(D)
    part, whole = A(4), A(4)
    sig, sx, sxi, sh, shi = A(2), A(1), A(1), A(1), A(1)
    sgate, sup = A(IC), A(IC)
    xr, xq = A(C, N), A(C, N, dtype=BF16)
    sg = A(2, N)
    h = A(IC, B * P)
    hw = h.rearrange("p a b -> p (a b)")
    wq = [hw[:, 0:IC * D // 2].bitcast(BF16).rearrange("p (a b) -> p a b", a=IC),
          hw[:, IC * D // 2:IC * D].bitcast(BF16).rearrange("p (a b) -> p a b", a=IC),
          hw[:, IC * D:IC * D + C * IC * IP // 2].bitcast(BF16).rearrange("p (a b) -> p a b", a=C)]
    hmax = A(TURNS)
    hq = A(IC, N, dtype=BF16)
    hr = k.Y.rearrange("p b d -> p (b d)").rearrange("p (a b) -> p a b", a=IC)
    wtmp = hr.rearrange("p a b -> p (a b)")[:, 0:IC * D].rearrange("p (a b) -> p a b", a=IC)

    def bank_bf16(b, n):
        return ps[:, b, :].bitcast(BF16)[:, 0:n]

    with nc.Block() as block:
        @block.sync
        def _(sp):
            k.prefetch(sp, stage)

        @block.gpsimd
        def _(pool):
            pool.memset(ones, 1.0).then_inc(ones_set, 1)
            pool.memset(part, 0.0).then_inc(ones_set, 1)
            turned.stage(pool, 0)
            pool.wait_ge(x_measured, 1)
            pool.partition_all_reduce(whole[:, 0:1], part[:, 0:1], P, ABSMAX).then_inc(x_max, 1)
            for g in range(TURNS - 1):
                turned.stage_next(pool, g)
            pool.wait_ge(h_measured, 1)
            pool.partition_all_reduce(whole[:, 1:2], part[:, 1:2], P, ABSMAX).then_inc(h_max, 1)
            with pool.Fori(0, TURNS) as g:
                norm.roots(pool, g)

        @block.tensor
        def _(pe):
            k.wait_weights(pe, stage)
            pe.wait_ge(ones_set, 2)
            pe.wait_ge(ident_ready, 1)
            for m in range(2):
                pe.wait_ge(w_quantized, m + 1)
                for c in range(C):
                    for i in range(IC):
                        mm = nc.tensor.transpose(bank_bf16(2 * m + c, IC * IP)[:, i * IP:(i + 1) * IP],
                                                 wq[m][0:IP, i, c * P:(c + 1) * P], identb[0:IP, 0:IP])
                mm.then_inc(w_turned, 1)
            pe.wait_ge(w_quantized, 3)
            for i in range(IC):
                for c in range(C):
                    mm = nc.tensor.transpose(bank_bf16(6 + i // 4, 4 * D)[0:IP, (i % 4) * D + c * P:(i % 4) * D + (c + 1) * P],
                                             wq[2][:, c, i * IP:(i + 1) * IP], identb[:, :])
            mm.then_inc(w_turned, 1)
            pe.wait_ge(wT_ready, 4)
            pe.wait_ge(scale_ready, 1)
            for c in range(C):
                mm = nc.tensor.matmul(ps[:, 6, c * P:(c + 1) * P], ones[:, :], diag[:, c, :], start=True, stop=True)
            mm.then_inc(scales_spread, 1)
            with pe.Fori(0, TURNS) as g:
                turned.turn(pe, g)
                pe.wait_ge(xq_ready, g + 1)
                for i in range(IC):
                    for part_, wT in enumerate((wgT, wuT)):
                        if i >= 2 and part_ == 0:
                            pe.wait_ge(h_ready, g * IC + i - 1)
                        for c in range(C):
                            mm = nc.tensor.matmul(ps[0:IP, 2 * (i % 2) + part_, :], wT[:, c, i * IP:(i + 1) * IP],
                                                  xq[:, c, :], start=(c == 0), stop=(c == C - 1))
                    mm.then_inc(up_ready, 1)
            pe.wait_ge(scale_ready, 2)
            with pe.Fori(0, TURNS) as g:
                pe.wait_ge(hq_ready, g + 1)
                for u in range(TILES):
                    norm.wait_added(pe, g * TILES + u - 1 if u >= 2 else g * TILES)
                    for i in range(IC):
                        mm = nc.tensor.matmul(ps[:, 4 + u % 2, 0:D], hq[0:IP, i, u * P:(u + 1) * P], wdT[0:IP, i, :],
                                              start=(i == 0), stop=(i == IC - 1))
                    mm.then_inc(y_ready, 1)

        @block.scalar
        def _(act):
            k.wait_weights(act, stage)
            nc.scalar.copy(identb[:, :], k.ident).then_inc(ident_ready, 1)
            nc.scalar.activation(sig, w.clip, ACT.Sigmoid).then_inc(clips, 1)
            for m, wT in enumerate((wgT, wuT)):
                act.wait_ge(w_turned, m + 1)
                for c in range(C):
                    a = nc.scalar.copy(wT[:, c, :], bank_bf16(2 * m + c, IC * IP))
                a.then_inc(wT_ready, 1)
            act.wait_ge(w_turned, 3)
            for b in range(2):
                nc.scalar.copy(wdT[0:IP, 4 * b:4 * b + 4, :], bank_bf16(6 + b, 4 * D)[0:IP, :].rearrange(
                    "p (i d) -> p i d", d=D)).then_inc(wT_ready, 1)
            act.wait_ge(scale_ready, 1)
            with act.Fori(0, TURNS) as g:
                act.wait_ge(x_rounded, g + 1)
                nc.scalar.activation(xq[:, :, :], xr[:, :, :], ACT.Copy, bias=-MAGIC).then_inc(xq_ready, 1)
                for i in range(IC):
                    act.wait_ge(up_ready, g * IC + i + 1)
                    nc.scalar.activation(sg[0:IP, i % 2, :], ps[0:IP, 2 * (i % 2), :], ACT.Silu,
                                         scale=sgate[0:IP, i:i + 1]).then_inc(silu_ready, 1)
            with act.Fori(0, TURNS) as g:
                act.wait_ge(h_rounded, g + 1)
                nc.scalar.activation(hq[0:IP, :, :], hr[0:IP, :, :], ACT.Copy, bias=-MAGIC).then_inc(hq_ready, 1)

        @block.vector
        def _(dve):
            k.wait_weights(dve, stage)
            chain = Chain(dve, dve_chain)
            norm.open(dve)
            dve.wait_ge(ones_set, 2)
            dve.tensor_reduce(part[:, 0:1], k.X.rearrange("p b d -> p (b d)"), AX.X, ALU.max, apply_absolute_value=True).then_inc(x_measured, 1)
            rows = [(0, IP, w.gate[0:IP]), (IC, IP, w.up[0:IP]), (2 * IC, P, w.down)]
            for m, (at, n, a) in enumerate(rows):
                cols = a.shape[1]
                chain(dve.tensor_reduce(wmax[0:n, at:at + cols], a, AX.X, ALU.max, apply_absolute_value=True))
                chain(dve.tensor_scalar(wscale[0:n, at:at + cols], wmax[0:n, at:at + cols], 1.0 / QMAX, None, ALU.mult))
                chain(dve.reciprocal(winv[0:n, at:at + cols], wscale[0:n, at:at + cols]))
                tmp = (wtmp if m < 2 else hr.rearrange("p a b -> p (a b)")[:, 0:C * IC * IP].rearrange(
                    "p (a b) -> p a b", a=C))[0:n]
                chain(dve.tensor_tensor(tmp, a, bc(winv[0:n, at:at + cols], 2, a.shape[2]), ALU.mult))
                dve.tensor_scalar(wq[m][0:n], tmp, MAGIC, MAGIC, ALU.add, ALU.subtract).then_inc(w_quantized, 1)
                dve.wait_ge(w_quantized, m + 1)
            for c in range(C):
                chain(dve.tensor_scalar(diag[:, c, :], k.ident, wscale[:, 2 * IC + c:2 * IC + c + 1], None, ALU.mult))

            def scale_of(out, inverse, clip, largest):
                chain(dve.tensor_tensor(out, clip, largest, ALU.mult))
                chain(dve.tensor_scalar(out, out, 1.0 / QMAX, None, ALU.mult))
                chain(dve.reciprocal(inverse, out))

            dve.wait_ge(x_max, 1)
            dve.wait_ge(clips, 1)
            scale_of(sx, sxi, sig[:, 0:1], whole[:, 0:1])
            chain(dve.tensor_scalar(sgate[0:IP], wscale[0:IP, 0:IC], sx[0:IP], None, ALU.mult))
            dve.tensor_scalar(sup[0:IP], wscale[0:IP, IC:2 * IC], sx[0:IP], None, ALU.mult).then_inc(scale_ready, 1)
            dve.wait_ge(scale_ready, 1)
            base = chain.n
            per = 2 + 1
            with dve.Fori(0, TURNS) as g:
                c1 = Chain(dve, dve_chain, 0, 0)
                c1.base = base + g * per
                for c in range(C):
                    dve.wait_ge(turned.turned, g * C + c + 1)
                    c1(dve.tensor_scalar(xr[:, c, :], ps[:, 4 + c, :], sxi, MAGIC, ALU.mult, ALU.add))
                dve.tensor_scalar(xr[:, :, :], xr[:, :, :], MAGIC + QMAX, MAGIC - QMAX - 1.0, ALU.min, ALU.max
                                  ).then_inc(x_rounded, 1)
                for i in range(IC):
                    dve.wait_ge(silu_ready, g * IC + i + 1)
                    dve.scalar_tensor_tensor(out=h[0:IP, i, bass.ds(g * N, N)], in0=ps[0:IP, 2 * (i % 2) + 1, :],
                                             scalar=sup[0:IP, i:i + 1], in1=sg[0:IP, i % 2, :],
                                             op0=ALU.mult, op1=ALU.mult).then_inc(h_ready, 1)
                dve.wait_ge(h_ready, (g + 1) * IC)
                c1(dve.tensor_reduce(hmax[0:IP, bass.ds(g, 1)], h[0:IP, :, bass.ds(g * N, N)], AX.XY, ALU.max, apply_absolute_value=True))
                assert c1.n == per
            chain.n += TURNS * per
            dve.tensor_reduce(part[0:IP, 1:2], hmax[0:IP], AX.X, ALU.max).then_inc(h_measured, 1)
            dve.wait_ge(h_max, 1)
            scale_of(sh, shi, sig[:, 1:2], whole[:, 1:2])
            dve.wait_ge(scales_spread, 1)
            dve.tensor_scalar(down_scale, ps[:, 6, 0:D], sh, None, ALU.mult).then_inc(scale_ready, 1)
            dve.wait_ge(scale_ready, 2)
            base2 = chain.n
            with dve.Fori(0, TURNS) as g:
                per2 = 1 + TILES + norm.chained()
                c2 = Chain(dve, dve_chain, 0, 0)
                c2.base = base2 + g * per2
                norm.wait_added(dve, g * TILES)
                c2(dve.tensor_scalar(hr[0:IP, :, :], h[0:IP, :, bass.ds(g * N, N)], shi[0:IP], MAGIC, ALU.mult, ALU.add))
                dve.tensor_scalar(hr[0:IP, :, :], hr[0:IP, :, :], MAGIC + QMAX, MAGIC - QMAX - 1.0, ALU.min, ALU.max
                                  ).then_inc(h_rounded, 1)
                for u in range(TILES):
                    dve.wait_ge(y_ready, g * TILES + u + 1)
                    y = norm.r[:, u, :]
                    c2(dve.tensor_tensor(y, ps[:, 4 + u % 2, 0:D], down_scale, ALU.mult))
                    norm.add(dve, c2, g, u, y)
                norm.moments(dve, c2, g)
                norm.apply(dve, c2, g)
                assert c2.n == per2
    sem.release()


def ternary_ffn_stage(k):
    stage = "L2_ffn"
    nc, ps, w, A = k.nc, k.psum, k.begin(stage), k.arena
    sem = Semaphores(nc, stage)
    norm = Norm(k, sem, k.X, k.X)
    F = w.gate.shape[2]
    FC = F // P
    ident_ready, w_summed, w_sums = sem("ident_ready"), sem("weights_summed"), sem("weight_sums_ready")
    w_rounded, w_ready = sem("weights_rounded"), sem("weights_ready")
    x_quantized, x_turned, xT_ready = sem("x_quantized"), sem("x_turned"), sem("xT_ready")
    up_ready, silu_ready, h_ready, h_rounded = sem("up_ready"), sem("silu_ready"), sem("h_ready"), sem("h_rounded")
    hq_ready, h_turned, hT_ready = sem("hq_ready"), sem("h_turned"), sem("hT_ready")
    y_ready, dve_chain = sem("y_ready"), sem("dve_chain")

    identb = A(P, dtype=BF16)
    sums, means, wmul = A(3), A(3), A(3)
    mags = A(C * F)
    wr = [A(C * F), A(C * F)]
    wt = [A(C, F, dtype=BF16), A(C, F, dtype=BF16), A(FC, D, dtype=BF16)]
    xm, xmul, xunit = A(TILES), A(TILES), A(TILES)
    gunit, uunit = A(TILES), A(TILES)
    xr, xq = A(TILES, D), A(TILES, D, dtype=BF16)
    xT = A(C, N, dtype=BF16)
    sg, hb = A(F), A(2, F)
    hm, hmul, hunit = A(2), A(2), A(2)
    hq, hT = A(2, F, dtype=BF16), A(2, FC, P, dtype=BF16)
    flat = [w.gate.rearrange("p c f -> p (c f)"), w.up.rearrange("p c f -> p (c f)"), w.down.rearrange("p c f -> p (c f)")]
    x_psum = ps[:, 4, :].bitcast(BF16).rearrange("p (c n) -> p c n", c=C)
    h_psum = ps[:, 5, :].bitcast(BF16).rearrange("p (f t) -> p f t", t=P)

    with nc.Block() as block:
        @block.sync
        def _(sp):
            k.prefetch(sp, stage)

        @block.gpsimd
        def _(pool):
            pool.wait_ge(w_summed, 3)
            pool.partition_all_reduce(means[:, :], sums[:, :], P, SUM).then_inc(w_sums, 1)
            with pool.Fori(0, TURNS) as g:
                norm.roots(pool, g)

        @block.tensor
        def _(pe):
            pe.wait_ge(ident_ready, 1)
            pe.wait_ge(w_ready, 3)
            with pe.Fori(0, TURNS) as g:
                pe.wait_ge(x_quantized, g + 1)
                for c in range(C):
                    for u in range(TILES):
                        mm = nc.tensor.transpose(x_psum[:, c, u * P:(u + 1) * P], xq[:, u, c * P:(c + 1) * P], identb)
                mm.then_inc(x_turned, 1)
                pe.wait_ge(xT_ready, g + 1)

                def down(u):
                    n = g * TILES + u
                    pe.wait_ge(hq_ready, n + 1)
                    for f in range(FC):
                        mm = nc.tensor.transpose(h_psum[:, f, :], hq[:, u % 2, f * P:(f + 1) * P], identb)
                    mm.then_inc(h_turned, 1)
                    pe.wait_ge(hT_ready, n + 1)
                    for f in range(FC):
                        mm = nc.tensor.matmul(ps[:, 6 + u % 2, 0:D], hT[:, u % 2, f, :], wt[2][:, f, :],
                                              start=(f == 0), stop=(f == FC - 1))
                    mm.then_inc(y_ready, 1)

                for u in range(TILES):
                    if u:
                        pe.wait_ge(h_ready, g * TILES + u)
                    for m in range(2):
                        for b in range(F // N):
                            for c in range(C):
                                mm = nc.tensor.matmul(ps[:, 2 * m + b, :], xT[:, c, u * P:(u + 1) * P],
                                                      wt[m][:, c, b * N:(b + 1) * N], start=(c == 0), stop=(c == C - 1))
                    mm.then_inc(up_ready, 1)
                    if u:
                        if u >= 3:
                            norm.wait_added(pe, g * TILES + u - 2)
                        down(u - 1)
                norm.wait_added(pe, g * TILES + TILES - 2)
                down(TILES - 1)

        @block.scalar
        def _(act):
            k.wait_weights(act, stage)
            nc.scalar.copy(identb[:, :], k.ident).then_inc(ident_ready, 1)
            for m in range(3):
                if m:
                    act.wait_ge(w_summed, m)
                nc.scalar.activation(mags, flat[m], ACT.Abs, accum_out=sums[:, m:m + 1]).then_inc(w_summed, 1)
            for m in range(3):
                act.wait_ge(w_rounded, m + 1)
                nc.scalar.activation(wt[m].rearrange("p c f -> p (c f)"), wr[m % 2], ACT.Copy, bias=-MAGIC
                                     ).then_inc(w_ready, 1)
            with act.Fori(0, TURNS) as g:
                act.wait_ge(x_turned, g + 1)
                nc.scalar.copy(xT[:, :, :], x_psum).then_inc(xT_ready, 1)

                def finish(u):
                    n = g * TILES + u
                    act.wait_ge(h_rounded, n + 1)
                    nc.scalar.activation(hq[:, u % 2, :], hb[:, u % 2, :], ACT.Copy, bias=-MAGIC).then_inc(hq_ready, 1)
                    act.wait_ge(h_turned, n + 1)
                    nc.scalar.copy(hT[:, u % 2, :, :], h_psum).then_inc(hT_ready, 1)

                for u in range(TILES):
                    act.wait_ge(up_ready, g * TILES + u + 1)
                    if u:
                        act.wait_ge(h_ready, g * TILES + u)
                    nc.scalar.activation(sg, ps[:, 0:2, :].rearrange("p a b -> p (a b)"), ACT.Silu,
                                         scale=gunit[:, u:u + 1]).then_inc(silu_ready, 1)
                    if u:
                        finish(u - 1)
                finish(TILES - 1)

        @block.vector
        def _(dve):
            k.wait_weights(dve, stage)
            norm.open(dve)
            chain = Chain(dve, dve_chain)
            dve.wait_ge(w_sums, 1)
            chain(dve.tensor_scalar(means, means, 1.0 / (C * P * F), 1e-5, ALU.mult, ALU.max))
            chain(dve.reciprocal(wmul, means))
            for m in range(3):
                if m == 2:
                    dve.wait_ge(w_ready, 1)
                chain(dve.tensor_scalar(wr[m % 2], flat[m], wmul[:, m:m + 1], MAGIC, ALU.mult, ALU.add))
                dve.tensor_scalar(wr[m % 2], wr[m % 2], MAGIC + 1.0, MAGIC - 1.0, ALU.min, ALU.max
                                  ).then_inc(w_rounded, 1)
            base = chain.n
            per = 6 + TILES * 4 + norm.chained()
            with dve.Fori(0, TURNS) as g:
                ch = Chain(dve, dve_chain)
                ch.base = base + g * per
                x = k.X[:, bass.ds(g * TILES, TILES), :]
                ch(dve.tensor_reduce(xm, x, AX.X, ALU.max, apply_absolute_value=True))
                ch(dve.tensor_scalar(xunit, xm, 1e-5, 1.0 / QMAX, ALU.max, ALU.mult))
                ch(dve.reciprocal(xmul, xunit))
                ch(dve.tensor_scalar(gunit, xunit, means[:, 0:1], None, ALU.mult))
                ch(dve.tensor_scalar(uunit, xunit, means[:, 1:2], None, ALU.mult))
                ch(dve.tensor_tensor(xr[:, :, :], x, bc(xmul, 2, D), ALU.mult))
                dve.tensor_scalar(xq[:, :, :], xr[:, :, :], MAGIC, MAGIC, ALU.add, ALU.subtract).then_inc(x_quantized, 1)

                def hidden(u):
                    n = g * TILES + u
                    b = hb[:, u % 2, :]
                    dve.wait_ge(silu_ready, n + 1)
                    dve.scalar_tensor_tensor(out=b, in0=ps[:, 2:4, :].rearrange("p a b -> p (a b)"),
                                             scalar=uunit[:, u:u + 1], in1=sg, op0=ALU.mult, op1=ALU.mult
                                             ).then_inc(h_ready, 1)
                    dve.wait_ge(h_ready, n + 1)
                    q = slice(u % 2, u % 2 + 1)
                    ch(dve.tensor_reduce(hm[:, q], b, AX.X, ALU.max, apply_absolute_value=True))
                    ch(dve.tensor_scalar(hunit[:, q], hm[:, q], 1e-5, 1.0 / QMAX, ALU.max, ALU.mult))
                    ch(dve.reciprocal(hmul[:, q], hunit[:, q]))
                    ch(dve.tensor_scalar(hunit[:, q], hunit[:, q], means[:, 2:3], None, ALU.mult))
                    dve.tensor_scalar(b, b, hmul[:, q], MAGIC, ALU.mult, ALU.add).then_inc(h_rounded, 1)
                    dve.wait_ge(h_rounded, n + 1)

                def finish(u):
                    dve.wait_ge(y_ready, g * TILES + u + 1)
                    norm.add(dve, ch, g, u, ps[:, 6 + u % 2, 0:D], hunit[:, u % 2:u % 2 + 1])

                for u in range(TILES):
                    hidden(u)
                    if u:
                        finish(u - 1)
                finish(TILES - 1)
                norm.moments(dve, ch, g)
                norm.apply(dve, ch, g)
                assert ch.n == per, (ch.n, per)
    sem.release()


def wide_attention_stage(k):
    stage = "L3_attn"
    nc, ps, w, A = k.nc, k.psum, k.begin(stage), k.arena
    sem = Semaphores(nc, stage)
    turned, norm = Turned(k, sem, k.X, 4), Norm(k, sem, k.X, k.X)
    xT = turned.xT
    ones_set, qk_projected, qk_ready = sem("ones_set"), sem("qk_projected"), sem("qk_ready")
    v_projected, v_ready, scores_ready, shifted = sem("v_projected"), sem("v_ready"), sem("scores_ready"), sem("shifted")
    probs_ready, probs_turned, probsT_ready = sem("probs_ready"), sem("probs_turned"), sem("probsT_ready")
    o_ready, dve_chain = sem("o_ready"), sem("dve_chain")
    qkT = A(2 * C, N)
    va = A(TILES, D + 1)
    pr, pT = A(TILES, P), A(TILES, P)
    mx, ri = A(TILES), A(TILES)
    s_psum = ps[:, 4, :].rearrange("p (u t) -> p u t", t=P)
    pT_psum = ps[:, 5, :].rearrange("p (u t) -> p u t", t=P)

    with nc.Block() as block:
        @block.sync
        def _(sp):
            k.prefetch(sp, stage)

        @block.gpsimd
        def _(pool):
            pool.memset(va[:, :, D:D + 1], 1.0).then_inc(ones_set, 1)
            turned.stage(pool, 0)
            with pool.Fori(0, TURNS - 1) as g:
                turned.stage_next(pool, g)
                norm.roots(pool, g)
            norm.roots(pool, TURNS - 1)

        @block.tensor
        def _(pe):
            k.wait_weights(pe, stage)
            pe.wait_ge(ones_set, 1)
            with pe.Fori(0, TURNS) as g:
                turned.turn(pe, g)
                pe.wait_ge(turned.ready, (g + 1) * C)
                norm.wait_added(pe, g * TILES)
                for p, (m, co) in enumerate([(w.wq, 0), (w.wq, 1), (w.wk, 0), (w.wk, 1)]):
                    for ci in range(C):
                        mm = nc.tensor.matmul(ps[:, p, :], m[:, ci, co * P:(co + 1) * P], xT[:, ci, :],
                                              start=(ci == 0), stop=(ci == C - 1))
                    mm.then_inc(qk_projected, 1)
                for u in range(TILES):
                    for ci in range(C):
                        mm = nc.tensor.matmul(ps[:, 6 + u // 2, (u % 2) * D:(u % 2 + 1) * D],
                                              xT[:, ci, u * P:(u + 1) * P], w.wv[:, ci, :],
                                              start=(ci == 0), stop=(ci == C - 1))
                    if u % 2:
                        mm.then_inc(v_projected, 1)
                pe.wait_ge(qk_ready, (g + 1) * 2 * C)
                for u in range(TILES):
                    for ci in range(C):
                        mm = nc.tensor.matmul(s_psum[:, u, :], qkT[:, ci, u * P:(u + 1) * P],
                                              qkT[:, C + ci, u * P:(u + 1) * P], start=(ci == 0), stop=(ci == C - 1))
                mm.then_inc(scores_ready, 1)
                pe.wait_ge(probs_ready, g + 1)
                for u in range(TILES):
                    mm = nc.tensor.transpose(pT_psum[:, u, :], pr[:, u, :], k.ident)
                mm.then_inc(probs_turned, 1)
                pe.wait_ge(probsT_ready, g + 1)
                pe.wait_ge(v_ready, (g + 1) * 2)
                for u in range(TILES):
                    nc.tensor.matmul(ps[:, u, 0:D + 1], pT[:, u, :], va[:, u, :], start=True, stop=True
                                     ).then_inc(o_ready, 1)

        @block.scalar
        def _(act):
            with act.Fori(0, TURNS) as g:
                turned.copy(act, g)
                for p in range(2 * C):
                    act.wait_ge(qk_projected, g * 2 * C + p + 1)
                    nc.scalar.copy(qkT[:, p, :], ps[:, p, :]).then_inc(qk_ready, 1)
                act.wait_ge(shifted, g + 1)
                nc.scalar.activation(pr[:, :, :], pr[:, :, :], ACT.Exp, scale=D ** -0.5).then_inc(probs_ready, 1)
                act.wait_ge(probs_turned, g + 1)
                nc.scalar.copy(pT[:, :, :], pT_psum).then_inc(probsT_ready, 1)

        @block.vector
        def _(dve):
            norm.open(dve)
            with dve.Fori(0, TURNS) as g:
                chain = Chain(dve, dve_chain, g, 1 + TILES + norm.chained())
                for i in range(2):
                    dve.wait_ge(v_projected, g * 2 + i + 1)
                    dve.tensor_copy(va[:, 2 * i:2 * i + 2, 0:D], ps[:, 6 + i, :].rearrange("p (u d) -> p u d", d=D)
                                    ).then_inc(v_ready, 1)
                dve.wait_ge(scores_ready, g + 1)
                chain(dve.tensor_reduce(mx, s_psum, AX.X, ALU.max))
                dve.tensor_tensor(pr[:, :, :], s_psum, bc(mx, 2, P), ALU.subtract).then_inc(shifted, 1)
                for u in range(TILES):
                    dve.wait_ge(o_ready, g * TILES + u + 1)
                    chain(dve.reciprocal(ri[:, u:u + 1], ps[:, u, D:D + 1]))
                    norm.add(dve, chain, g, u, ps[:, u, 0:D], ri[:, u:u + 1])
                norm.moments(dve, chain, g)
                norm.apply(dve, chain, g)
                chain.end()
    sem.release()


def relu_ffn_stage(k):
    stage = "L3_relu"
    nc, ps, w, A = k.nc, k.psum, k.begin(stage), k.arena
    sem = Semaphores(nc, stage)
    turned, norm = Turned(k, sem, k.Y, 4), Norm(k, sem, k.Y, k.Y, w.gain, w.shift)
    outer = Norm(k, lambda name: sem("outer_" + name), k.X, k.X)
    xT = turned.xT
    ones_set, up_ready, h_ready, y_ready = sem("ones_set"), sem("up_ready"), sem("h_ready"), sem("y_ready")
    dve_chain = sem("dve_chain")
    F = w.w1.shape[2]
    FC = F // P
    h, ones = A(FC, N), A(P)

    with nc.Block() as block:
        @block.sync
        def _(sp):
            k.prefetch(sp, stage)

        @block.gpsimd
        def _(pool):
            pool.memset(ones, 1.0).then_inc(ones_set, 1)
            turned.stage(pool, 0)
            for g in range(TURNS):
                if g + 1 < TURNS:
                    turned.stage_next(pool, g)
                norm.roots(pool, g)
                outer.roots(pool, g)

        @block.tensor
        def _(pe):
            k.wait_weights(pe, stage)
            pe.wait_ge(ones_set, 1)
            with pe.Fori(0, TURNS) as g:
                turned.turn(pe, g)
                pe.wait_ge(turned.ready, (g + 1) * C)
                for f in range(FC):
                    if f >= 4:
                        pe.wait_ge(h_ready, g * FC + f - 3)
                    for c in range(C):
                        mm = nc.tensor.matmul(ps[:, f % 4, :], w.w1[:, c, f * P:(f + 1) * P], xT[:, c, :],
                                              start=(c == 0), stop=(c == C - 1))
                    mm.then_inc(up_ready, 1)
                pe.wait_ge(h_ready, (g + 1) * FC)
                for u in range(TILES):
                    y = ps[:, 6 + u % 2, 0:D]
                    norm.wait_added(pe, g * TILES + u - 1 if u >= 2 else g * TILES)
                    for f in range(FC):
                        nc.tensor.matmul(y, h[:, f, u * P:(u + 1) * P], w.w2[:, f, :], start=(f == 0), stop=False)
                    nc.tensor.matmul(y, ones[0:1, :], w.b2[0:1, :], start=False, stop=True).then_inc(y_ready, 1)

        @block.scalar
        def _(act):
            k.wait_weights(act, stage)
            with act.Fori(0, TURNS) as g:
                turned.copy(act, g)
                for f in range(FC):
                    act.wait_ge(up_ready, g * FC + f + 1)
                    nc.scalar.activation(h[:, f, :], ps[:, f % 4, :], ACT.Relu, bias=w.b1[:, f:f + 1]
                                         ).then_inc(h_ready, 1)

        @block.vector
        def _(dve):
            k.wait_weights(dve, stage)
            norm.open(dve)
            outer.open(dve)
            with dve.Fori(0, TURNS) as g:
                chain = Chain(dve, dve_chain, g, norm.chained() + outer.chained())
                for u in range(TILES):
                    dve.wait_ge(y_ready, g * TILES + u + 1)
                    norm.add(dve, chain, g, u, ps[:, 6 + u % 2, 0:D])
                norm.moments(dve, chain, g)
                norm.apply(dve, chain, g)
                for u in range(TILES):
                    outer.add(dve, chain, g, u, k.Y[:, bass.ds(g * TILES + u, 1), :].rearrange("p a d -> p (a d)"))
                outer.moments(dve, chain, g)
                outer.apply(dve, chain, g)
                chain.end()
    sem.release()



def by_rows(a):
    a = np.asarray(a)
    return a.reshape(a.shape[0] // P, P, -1).transpose(1, 0, 2)


def col(b):
    return np.asarray(b).reshape(-1, P).T


def row(b):
    return np.broadcast_to(np.asarray(b).reshape(1, -1), (P, np.asarray(b).size))


def heads_mask():
    return (np.arange(P)[:, None] // DH == np.arange(HH)[None, :]).astype(np.float32)


def causal_mask(value):
    return np.where(np.tril(np.ones((P, P), bool)), 0.0, value).astype(np.float32)


def rope_tables():
    inv = (1.0 / 10000.0 ** (np.arange(0, DH, 2, dtype=np.float32) / DH)).astype(np.float32)
    f = np.arange(P, dtype=np.float32)[:, None] * inv[None, :]
    sin, cos = np.sin(f).T.astype(np.float32), np.cos(f).T.astype(np.float32)
    sin = np.stack([-sin, sin], 1).reshape(DH, P)
    return np.tile(np.repeat(cos, 2, 0), (HH, 1)), np.tile(sin, (HH, 1))


def swap_pairs(a):
    return np.asarray(a).reshape(-1, 2, *np.asarray(a).shape[1:])[:, ::-1].reshape(np.asarray(a).shape)


def pack_L1_attn(i):
    wq, wk, wv = np.split(np.asarray(i["L1_attn_w_qkv"]), 3, 0)
    bq, bk, bv = np.split(np.asarray(i["L1_attn_b_qkv"]), 3, 0)
    cos, sin = rope_tables()
    return dict(wq=by_rows(wq.T), wqs=by_rows(swap_pairs(wq).T), wk=by_rows(wk.T), wks=by_rows(swap_pairs(wk).T),
                wv=by_rows(wv.T), wo=by_rows(np.asarray(i["L1_attn_w_out"]).T), bq=col(bq), bqs=col(swap_pairs(bq)),
                bk=col(bk), bks=col(swap_pairs(bk)), bv=col(bv), bo=row(i["L1_attn_b_out"]), cos=cos, sin=sin,
                heads=heads_mask(), causal=causal_mask(-1e30))


def pack_L1_xattn(i):
    t = {n: by_rows(np.asarray(i["L1_xattn_W" + n]).T) for n in "qkvo"}
    return dict(wq=t["q"], wk=t["k"], wv=t["v"], wo=t["o"], bq=col(i["L1_xattn_bq"]), bk=col(i["L1_xattn_bk"]),
                bv=col(i["L1_xattn_bv"]), bo=row(i["L1_xattn_bo"]), heads=heads_mask())


def pack_L3(i, which):
    W = np.asarray(i[f"L3_xattn_Wq_{which}"]).transpose(1, 0, 2).reshape(D, D)
    b = np.asarray(i[f"L3_xattn_bq_{which}"]).reshape(-1)
    n = "1" if which == "self" else "2"
    out = dict(wq=by_rows(W), bq=col(b), bv_row=row(b), gain=row(i["L3_xattn_g" + n]),
               shift=row(i["L3_xattn_beta" + n]), heads=heads_mask())
    if which == "self":
        out["causal"] = causal_mask(-1e9)
    return out


PACKS = {
    "L1_attn": pack_L1_attn,
    "L1_xattn": pack_L1_xattn,
    "L3_self": lambda i: pack_L3(i, "self"),
    "L3_cross": lambda i: pack_L3(i, "cross"),
}
ALIASES = {"L3_self": dict(wk="wq", wv="wq", bk="bq"), "L3_cross": dict(wk="wq", wv="wq", bk="bq")}


def pack_L0_attn(i):
    a = {n: np.asarray(i["L0_attn_" + n]) for n in
         ("Wq", "Wk", "Wv", "Wg", "Wo", "Wbeta", "Wtg", "mode_logits", "log_decay", "omega_log_scale")}
    DK, M = 64, 8
    j, d = np.arange(P), np.arange(P)
    partner = np.where(d % DK < DK // 2, d + DK // 2, d - DK // 2)
    swap = np.zeros((P, P), np.float32)
    swap[partner, d] = np.where(d % DK < DK // 2, 1.0, -1.0)
    inv_freq = (1.0 / 10000.0 ** (np.arange(0, DK, 2, dtype=np.float32) / DK)).astype(np.float32)
    omega = a["omega_log_scale"].reshape(-1, 2, M)
    return dict(wq=by_rows(a["Wq"]), wk=by_rows(a["Wk"]), wv=by_rows(a["Wv"]), wg=by_rows(a["Wg"]), wo=by_rows(a["Wo"]),
                wbt=by_rows(np.concatenate([a["Wbeta"], a["Wtg"]], 1)), swap=swap,
                after=(j[:, None] > j[None, :]).astype(np.float32), incl=(j[:, None] <= j[None, :]).astype(np.float32),
                position=row(np.arange(P, dtype=np.float32)), inv_freq=inv_freq[d % (DK // 2)][:, None],
                omega=omega.transpose(1, 0, 2)[d // DK], log_decay=row(a["log_decay"].reshape(-1)),
                modes=np.broadcast_to(a["mode_logits"], (P, *a["mode_logits"].shape)))


PACKS["L0_attn"] = pack_L0_attn


def before_matrix(n):
    return np.broadcast_to(np.tril(np.ones((n, n), np.float32), -1), (P, n, n))


PACKS["L0_ffn"] = lambda i: dict(wg=by_rows(i["L0_ffn_Wg"]), bg=row(i["L0_ffn_bg"]), before=before_matrix(8),
                                 b2=np.concatenate([np.asarray(i["L0_ffn_b2"]), np.zeros((P - 8, D), np.float32)]))
PACKS["L3_ffn"] = lambda i: dict(wg=by_rows(np.asarray(i["L3_ffn_w_gate"]).T), before=before_matrix(16))


def flat_experts(*parts):
    return np.concatenate([np.asarray(p).reshape(*np.asarray(p).shape[:2], -1) for p in parts], 2)


def stream_L0(i):
    w1, w2 = np.asarray(i["L0_ffn_W1"]), np.asarray(i["L0_ffn_W2"])
    b1 = np.asarray(i["L0_ffn_b1"])
    E = w1.shape[0]
    return {"experts_L0_ffn": np.ascontiguousarray(flat_experts(
        w1.reshape(E, C, P, -1).transpose(0, 2, 1, 3), w2.reshape(E, -1, P, D).transpose(0, 2, 1, 3),
        b1.reshape(E, -1, P).transpose(0, 2, 1)))}


def stream_L3(i):
    up = [np.concatenate([np.asarray(i[f"L3_ffn_{n}_e"]), np.asarray(i[f"L3_ffn_{n}_s"]).reshape(-1, P, D)])
          for n in ("w1", "w3")]
    shared2 = np.asarray(i["L3_ffn_w2_s"]).reshape(D, -1, P).transpose(1, 0, 2)
    w2 = np.concatenate([np.asarray(i["L3_ffn_w2_e"]), shared2])
    E = w2.shape[0]
    return {"experts_L3_ffn": np.ascontiguousarray(flat_experts(
        *(a.transpose(0, 2, 1).reshape(E, C, P, P).transpose(0, 2, 1, 3) for a in up), w2.transpose(0, 2, 1)))}


STREAMS = {"L0_ffn": stream_L0, "L3_ffn": stream_L3}


def same_head():
    h = np.arange(P) // DH
    return (h[:, None] == h[None, :]).astype(np.float32)


def pack_L0_xattn(i):
    t = {n: by_rows(np.asarray(i["L0_xattn_W" + n]).T) for n in "qkvo"}
    return dict(wq=t["q"], wk=t["k"], wv=t["v"], wo=t["o"], bq=col(i["L0_xattn_bq"]), bk=row(i["L0_xattn_bk"]),
                bv=row(i["L0_xattn_bv"]), bo=row(i["L0_xattn_bo"]), blocks=same_head())


def pack_L2_recall(i):
    wkv = np.asarray(i["L2_xattn_Wkv"])
    return dict(wq=by_rows(np.asarray(i["L2_xattn_Wq"]).T),
                wkv=by_rows(np.concatenate([np.tile(wkv[:DH].T, (1, HH)), wkv[DH:].T], 1)),
                countdown=row(np.arange(P, 0, -1, dtype=np.float32)))


def pack_L2_xattn(i):
    return dict(wq=by_rows(np.asarray(i["L2_xattn_Wq"]).T), wo=by_rows(np.asarray(i["L2_xattn_Wc"]).T),
                heads=heads_mask())


def pack_L2_attn(i):
    f, t = np.arange(P)[:, None], np.arange(P)[None, :]
    angle = 2 * np.pi * ((f * t) % P) / P
    weight = np.where(f > P // 2, 0.0, np.where(f % (P // 2) == 0, 1.0, 2.0)) / P
    out = {"w" + n: by_rows(i["L2_attn_W" + n]) for n in "qkvo"}
    out.update({"b" + n: row(i["L2_attn_b" + n]) for n in "qkvo"})
    FR = P // 2 + 1
    return dict(out, dcos=np.cos(angle.T[:, :FR]).astype(np.float32), dsin=np.sin(angle.T[:, :FR]).astype(np.float32),
                icos=(weight * np.cos(angle)).astype(np.float32), isin=(-weight * np.sin(angle)).astype(np.float32),
                blocks=same_head())


PACKS.update(L0_xattn=pack_L0_xattn, L2_recall=pack_L2_recall, L2_xattn=pack_L2_xattn, L2_attn=pack_L2_attn)


def row_chunks(a, n):
    a = np.asarray(a).reshape(-1, n, a.shape[-1]).transpose(1, 0, 2)
    return np.concatenate([a, np.zeros((P - n, *a.shape[1:]), a.dtype)])


PACKS["L1_ffn"] = lambda i: dict(gate=row_chunks(i["L1_ffn_w_gate"], 88), up=row_chunks(i["L1_ffn_w_up"], 88),
                                 down=by_rows(i["L1_ffn_w_down"]),
                                 clip=np.concatenate([row(i["L1_ffn_clip_x"]), row(i["L1_ffn_clip_down"])], 1))
PACKS["L2_ffn"] = lambda i: dict(gate=by_rows(np.asarray(i["L2_ffn_w_gate"]).T), up=by_rows(np.asarray(i["L2_ffn_w_up"]).T),
                                 down=by_rows(np.asarray(i["L2_ffn_w_down"]).T))


PACKS["L3_attn"] = lambda i: {"w" + n: by_rows(np.asarray(i["L3_attn_W" + n]).T) for n in "qkv"}
PACKS["L3_relu"] = lambda i: dict(w1=by_rows(i["L3_xattn_w1"]), w2=by_rows(i["L3_xattn_w2"]), b1=col(i["L3_xattn_b1"]),
                                  b2=row(i["L3_xattn_b2"]), gain=row(i["L3_xattn_g3"]), shift=row(i["L3_xattn_beta3"]))


class Weights(dict):
    __getattr__ = dict.__getitem__


class Kernel:

    def __init__(self, nc, ctx, dram, shapes, stages):
        self.nc, self.dram, self.shapes, self.stages = nc, dram, shapes, stages

        def sb(name, words):
            return ctx.enter_context(nc.sbuf_tensor(name, [P, words], F32))

        self.X = sb("X", B * D)[:, :].rearrange("p (b d) -> p b d", d=D)
        self.Y = sb("Y", B * D)[:, :].rearrange("p (b d) -> p b d", d=D)
        self.ident = sb("ident", P)[:, :]
        self.eps = sb("eps", TILES)[:, :]
        self.minus_half = sb("minus_half", TILES)[:, :]
        self.regions = [sb(f"weights_{i}", REGION) for i in range(2)]
        self.arena = Arena(sb("arena", ARENA), ARENA)
        self.psum = ctx.enter_context(nc.psum_tensor("psum", [P, BANKS, N], F32))
        self.arrived = {s: nc.alloc_semaphore(f"{s}_weights_arrived") for s in stages}
        self.const_arrived = nc.alloc_semaphore("constants_arrived")
        if "ctxT" in dram:
            self.ctxT = dram["ctxT"]
        if "maskb" in dram:
            self.maskb = dram["maskb"]

    def words(self, stage):
        return sum(n for _, n, _ in self.shapes[stage])

    def load(self, sp, stage):
        n = self.words(stage)
        if n:
            to = self.regions[self.stages.index(stage) % 2]
            sp.dma_start(to[:, 0:n], self.dram["w_" + stage]).then_inc(self.arrived[stage], 16)

    def next_region(self, stage):
        return self.regions[(self.stages.index(stage) + 1) % 2]

    def prefetch(self, sp, stage):
        at = self.stages.index(stage) + 1
        if at < len(self.stages):
            self.load(sp, self.stages[at])

    def wait_weights(self, eng, stage):
        eng.wait_ge(self.const_arrived, 16)
        if self.words(stage):
            eng.wait_ge(self.arrived[stage], 16)

    def begin(self, stage):
        self.arena.reset()
        w, at = Weights(), 0
        region = self.regions[self.stages.index(stage) % 2]
        for name, n, dims in self.shapes[stage]:
            ap = region[:, at:at + n]
            if len(dims) > 1:
                letters = "abcd"[:len(dims)]
                ap = ap.rearrange("p (%s) -> p %s" % (" ".join(letters), " ".join(letters)),
                                  **dict(zip(letters[1:], dims[1:])))
            w[name] = ap
            at += n
        for new, old in ALIASES.get(stage, {}).items():
            w[new] = w[old]
        return w


RUN = {
    "L0_attn": lambda k: delta_stage(k),
    "L0_xattn": lambda k: linear_attention_stage(k),
    "L0_ffn": lambda k: experts_stage(k, "L0_ffn"),
    "L1_attn": lambda k: attention_stage(k, "L1_attn", k.X, k.X, rope=True, mask="causal"),
    "L1_xattn": lambda k: attention_stage(k, "L1_xattn", k.X, k.X, cross=True, mask="batch"),
    "L1_ffn": lambda k: int8_ffn_stage(k),
    "L2_attn": lambda k: correlation_stage(k),
    "L2_recall": lambda k: recall_stage(k),
    "L2_xattn": lambda k: attention_stage(k, "L2_xattn", k.X, k.X, recalled=True),
    "L2_ffn": lambda k: ternary_ffn_stage(k),
    "L3_attn": lambda k: wide_attention_stage(k),
    "L3_self": lambda k: attention_stage(k, "L3_self", k.X, k.Y, mask="causal", affine=True, out_proj=False),
    "L3_cross": lambda k: attention_stage(k, "L3_cross", k.Y, k.Y, cross=True, affine=True, out_proj=False),
    "L3_relu": lambda k: relu_ffn_stage(k),
    "L3_ffn": lambda k: experts_stage(k, "L3_ffn"),
}
STAGES = list(RUN)
REGION = 7168
ARENA = 30528


def program(nc, dram, out, shapes, stages=STAGES):
    with ExitStack() as ctx:
        k = Kernel(nc, ctx, dram, shapes, stages)
        x_in = dram["x"]
        with nc.Block() as block:
            @block.gpsimd
            def _(pool):
                pool.memset(k.minus_half, -0.5)
                pool.memset(k.eps, LN_EPS)

            @block.sync
            def _(sp):
                sp.dma_start(k.X[:, :, :], x_in.rearrange("b t d -> t b d")).then_inc(k.const_arrived, 16)
                sp.dma_start(k.ident[:, :], dram["ident"]).then_inc(k.const_arrived, 16)
                k.load(sp, stages[0])
                sp.wait_ge(k.const_arrived, 32)
        for s in stages:
            RUN[s](k)
        written = nc.alloc_semaphore("out_written")
        with nc.Block() as block:
            @block.sync
            def _(sp):
                sp.dma_start(out.rearrange("b t d -> t b d"), k.X[:, :, :]).then_inc(written, 16)
                sp.wait_ge(written, 16)


def lay_out(inputs, stages):
    arrays, shapes = {"x": np.ascontiguousarray(inputs["x"]), "ident": np.eye(P, dtype=np.float32)}, {}
    ctx = np.asarray(inputs["ctx_1024"])
    arrays["ctxT"] = np.ascontiguousarray(
        ctx.reshape(TURNS, TILES, P, C, P).transpose(0, 4, 3, 1, 2).reshape(TURNS, P, C, N))
    arrays["maskb"] = np.ascontiguousarray(
        np.asarray(inputs["mask_BxSxS2_ff0"]).reshape(TURNS, TILES, P, P).transpose(0, 2, 1, 3))
    arrays["padding"] = np.ascontiguousarray(np.asarray(inputs["mask_BxS2_bk1"]).T)
    for s in stages:
        packed = PACKS[s](inputs)
        shapes[s] = [(n, int(np.prod(a.shape[1:])), a.shape[1:]) for n, a in packed.items()]
        if packed:
            arrays["w_" + s] = np.ascontiguousarray(
                np.concatenate([np.asarray(a).reshape(P, -1) for a in packed.values()], 1))
    for s in stages:
        if s in STREAMS:
            arrays.update(STREAMS[s](inputs))
    return arrays, shapes


def kernel(**inputs):
    import numpy as _np
    import concourse.bacc as _bacc
    from concourse.bass_utils import run_bass_kernel_spmd as _run

    nc = _bacc.Bacc("TRN2", target_bir_lowering=False, num_devices=1)
    arrays, shapes = lay_out(inputs, STAGES)
    dram = {n: nc.dram_tensor(f"in_{n}", a.shape, mybir.dt.from_np(a.dtype), kind="ExternalInput").ap()
            for n, a in arrays.items()}
    out = nc.dram_tensor("out", (B, P, D), F32, kind="ExternalOutput").ap()
    program(nc, dram, out, shapes)
    r = _run(nc, [{f"in_{n}": a for n, a in arrays.items()}], core_ids=[0])
    return r.results[0]["out"]
```

```python
from contextlib import ExitStack

import numpy as np

import concourse.bass as bass
from concourse import mybir

F32 = mybir.dt.float32
BF16 = mybir.dt.bfloat16
U8 = mybir.dt.uint8
I32 = mybir.dt.int32
ALU = mybir.AluOpType
ACT = mybir.ActivationFunctionType
AX = mybir.AxisListType

P = 128
B = 16
D = 256
C = D // P
TILES = 4
TURNS = B // TILES
N = TILES * P
H = 16
DH = D // H
HH = H // C
LN_EPS = 1e-5
BANKS = 8


class Chain:

    def __init__(self, eng, sem, turn=0, per_turn=0):
        self.eng, self.sem, self.base, self.per_turn, self.n = eng, sem, turn * per_turn, per_turn, 0

    def __call__(self, ins):
        self.n += 1
        ins.then_inc(self.sem, 1)
        self.eng.wait_ge(self.sem, self.base + self.n)

    def end(self):
        assert self.n == self.per_turn, (self.n, self.per_turn)


class Semaphores:

    def __init__(self, nc, stage):
        self.nc, self.stage, self.all = nc, stage, []

    def __call__(self, name):
        self.all.append(self.nc.alloc_semaphore(f"{self.stage}_{name}"))
        return self.all[-1]

    def release(self):
        self.nc.clear_and_free_semaphores(self.all)
        self.nc.all_engine_barrier()


class Arena:

    def __init__(self, tensor, words):
        self.tensor, self.words, self.at = tensor, words, 0

    def reset(self):
        self.at = 0

    def __call__(self, *shape, dtype=F32, rows=P):
        size = 4 if dtype in (F32, I32) else 2 if dtype == BF16 else 1
        n = int(np.prod(shape))
        words = (n * size + 31) // 32 * 8
        ap = self.tensor[0:rows, self.at:self.at + n * size // 4]
        self.at += words
        assert self.at <= self.words, (self.at, self.words)
        if dtype != F32:
            ap = ap.bitcast(dtype)
        if len(shape) > 1:
            names = "abcd"[:len(shape)]
            ap = ap.rearrange("p (%s) -> p %s" % (" ".join(names), " ".join(names)),
                              **{k: v for k, v in zip(names[1:], shape[1:])})
        return ap


def bc(ap, axis, n):
    ap = ap.unsqueeze(axis)
    shape = list(ap.shape)
    shape[axis] = n
    return ap.to_broadcast(shape)


class Norm:

    def __init__(self, k, sem, src, dst, gain=None, shift=None, tiles=TILES):
        self.k, self.src, self.dst, self.gain, self.shift, self.tiles = k, src, dst, gain, shift, tiles
        self.r, self.stats = k.arena(tiles, D), k.arena(tiles, 6)
        self.mean_var, self.root, self.spare = k.arena(tiles, 2), k.arena(tiles), k.arena(1)
        self.added, self.measured, self.rooted = sem("residual_added"), sem("measured"), sem("rooted")

    def open(self, dve):
        dve.memset(self.spare, 0.0).then_inc(self.added, 1)

    def wait_added(self, eng, n):
        eng.wait_ge(self.added, n + 1)

    def add(self, dve, chain, g, u, y, factor=None, x=None):
        if x is None:
            x = self.src[:, bass.ds(g * self.tiles + u, 1), :].rearrange("p a d -> p (a d)")
        if factor is None:
            dve.tensor_tensor(self.r[:, u, :], y, x, ALU.add).then_inc(self.added, 1)
        else:
            dve.scalar_tensor_tensor(out=self.r[:, u, :], in0=y, scalar=factor, in1=x, op0=ALU.mult, op1=ALU.add
                                     ).then_inc(self.added, 1)
        self.wait_added(dve, g * self.tiles + u + 1)
        chain(dve.bn_stats(self.stats[:, u, :], self.r[:, u, :]))

    def moments(self, dve, chain, g):
        dve.tensor_copy(self.spare[:, :], self.stats[:, self.tiles - 1, 0:1])
        for u in range(self.tiles):
            a = dve.bn_aggr(self.mean_var[:, u, :], self.stats[:, u, :])
        a.then_inc(self.measured, 1)

    def roots(self, pool, g):
        pool.wait_ge(self.measured, g + 1)
        pool.tensor_tensor(self.root[:, :], self.mean_var[:, :, 1], self.k.eps[:, 0:self.tiles], ALU.add).then_inc(self.rooted, 1)
        pool.wait_ge(self.rooted, 2 * g + 1)
        pool.tensor_tensor(self.root[:, :], self.root[:, :], self.k.minus_half[:, 0:self.tiles], ALU.pow
                           ).then_inc(self.rooted, 1)

    def apply(self, dve, chain, g):
        dve.wait_ge(self.rooted, 2 * g + 2)
        to = self.dst[:, bass.ds(g * self.tiles, self.tiles), :]
        for u in range(self.tiles):
            out = self.r[:, u, :] if self.gain is not None else to[:, u, :]
            chain(dve.tensor_scalar(out, self.r[:, u, :], self.mean_var[:, u, 0:1], self.root[:, u:u + 1],
                                    ALU.subtract, ALU.mult))
        if self.gain is not None:
            chain(dve.tensor_tensor(self.r[:, :, :], self.r[:, :, :], bc(self.gain, 1, self.tiles), ALU.mult))
            chain(dve.tensor_tensor(to, self.r[:, :, :], bc(self.shift, 1, self.tiles), ALU.add))

    def chained(self):
        return 2 * self.tiles + (2 if self.gain is not None else 0)


class Biased:

    def __init__(self, k, sem, src, bias):
        self.src, self.bias, self.x, self.ready = src, bias, k.arena(TILES, D), sem("biased")

    def stage(self, pool, g):
        pool.tensor_tensor(self.x[:, :, :], self.src[:, bass.ds(g * TILES, TILES), :], bc(self.bias, 1, TILES),
                           ALU.add).then_inc(self.ready, 1)

    def tile(self, dve, g, u):
        dve.wait_ge(self.ready, g + 1)
        return self.x[:, u, :]


class Turned:

    def __init__(self, k, sem, src, bank, xT=None):
        self.k, self.src, self.bank = k, src, bank
        self.xs = k.arena(TILES, D)
        self.xT = k.arena(C, N) if xT is None else xT
        self.staged, self.turned, self.ready = sem("x_staged"), sem("x_turned"), sem("xT_ready")

    def stage(self, pool, g):
        pool.tensor_copy(self.xs[:, :, :], self.src[:, bass.ds(g * TILES, TILES), :]).then_inc(self.staged, 1)

    def stage_next(self, pool, g):
        pool.wait_ge(self.turned, (g + 1) * C)
        self.stage(pool, g + 1)

    def turn(self, pe, g):
        pe.wait_ge(self.staged, g + 1)
        for c in range(C):
            for u in range(TILES):
                mm = pe.transpose(self.k.psum[:, self.bank + c, u * P:(u + 1) * P],
                                  self.xs[:, u, c * P:(c + 1) * P], self.k.ident[:, :])
            mm.then_inc(self.turned, 1)

    def copy(self, act, g, to=None):
        to = self.xT if to is None else to
        for c in range(C):
            act.wait_ge(self.turned, g * C + c + 1)
            act.copy(to[:, c, :], self.k.psum[:, self.bank + c, :]).then_inc(self.ready, 1)


def attention_stage(k, stage, src, dst, rope=False, cross=False, mask=None, affine=False, out_proj=True,
                    recalled=False):
    nc, ps = k.nc, k.psum
    w = k.begin(stage)
    sem, A = Semaphores(nc, stage), k.arena
    x_staged, x_turned, xT_ready = sem("x_staged"), sem("x_turned"), sem("xT_ready")
    projected, qk_evacuated, v_ready = sem("projected"), sem("qk_evacuated"), sem("v_ready")
    rotated, keys_spread = sem("rotated"), sem("keys_spread")
    scores_ready, shifted, probs_ready = sem("scores_ready"), sem("shifted"), sem("probs_ready")
    probs_turned, probsT_ready, o_ready = sem("probs_turned"), sem("probsT_ready"), sem("o_ready")
    o_normalised, oT_turned, oT_ready = sem("o_normalised"), sem("oT_turned"), sem("oT_ready")
    y_ready = sem("y_ready")
    loaded, mask_loaded, ones_set, dve_chain = sem("loaded"), sem("mask_loaded"), sem("ones_set"), sem("dve_chain")

    xs = A(TILES, D)
    xT = A(C, N)
    kvT = A(C, N) if cross else xT
    qT, kT = A(C, N), A(C, N)
    half = [A(N) for _ in range(2)] if rope else None
    km = A(2, HH, P)
    va = A(TILES, H, DH + 1)
    pr = A(2, HH, P)
    pT = A(2, HH, P)
    mx, on, oT, ri = A(2, HH), A(D), A(C, P), A(H)
    norm = Norm(k, sem, src, dst, *((w.gain, w.shift) if affine else ()))
    biased = Biased(k, sem, src, w.bo) if out_proj and not recalled else None
    mk = A(TILES, P) if mask == "batch" else None

    qk = [(n + s, c) for n in ("q" if recalled else "kq") for c in range(C) for s in (("", "s") if rope else ("",))]
    NQK, NP = len(qk), len(qk) + (0 if recalled else 2)
    SPREADS = TILES if recalled else TILES * C
    UNITS = TILES * C
    STEPS = range(UNITS + 3)
    S_BANK, T_BANK, O_BANK, Y_BANK = 0, 4, 6, 7

    def s_psum(j):
        return ps[:, S_BANK + 2 * (j % 2):S_BANK + 2 * (j % 2) + 2, :].rearrange("p b (h t) -> p (b h) t", t=P)

    pt_psum = ps[:, T_BANK:T_BANK + 2, :].rearrange("p b (h t) -> p (b h) t", t=P)
    o_psum = ps[:, O_BANK, 0:H * (DH + 1)].rearrange("p (h e) -> p h e", e=DH + 1)
    oT_psum = ps[:, Y_BANK, 0:D].rearrange("p (c t) -> p c t", c=C)
    y_psum = ps[:, Y_BANK, D:2 * D]

    with nc.Block() as block:
        @block.sync
        def _(sp):
            if cross:
                sp.dma_start(kvT[:, :, :], k.ctxT[0]).then_inc(loaded, 16)
            if mask == "batch":
                sp.dma_start(mk[:, :, :], k.maskb[0]).then_inc(mask_loaded, 16)
            k.prefetch(sp, stage)
            if cross or mask == "batch":
                with sp.Fori(1, TURNS) as g:
                    if cross:
                        sp.wait_ge(projected, g * NP)
                        sp.dma_start(kvT[:, :, :], k.ctxT[g]).then_inc(loaded, 16)
                    if mask == "batch":
                        sp.wait_ge(shifted, g * UNITS)
                        sp.dma_start(mk[:, :, :], k.maskb[g]).then_inc(mask_loaded, 16)

        @block.gpsimd
        def _(pool):
            k.wait_weights(pool, stage)
            pool.memset(va[:, :, :, DH:DH + 1], 1.0).then_inc(ones_set, 1)

            def stage_x(g):
                pool.tensor_copy(xs[:, :, :], src[:, bass.ds(g * TILES, TILES), :]).then_inc(x_staged, 1)

            def rotate(g, pairs):
                for p in pairs:
                    pool.wait_ge(qk_evacuated, g * NQK + 2 * p + 2)
                    to = (kT if p < C else qT)[:, p % C, :]
                    pool.tensor_tensor(to, to, half[p % 2], ALU.add).then_inc(rotated, 1)

            def spread_unit(g, j):
                u, c = divmod(j, C)
                if j >= 2:
                    pool.wait_ge(scores_ready, g * UNITS + j - 1)
                keys = kT[:, c, u * P:(u + 1) * P]
                pool.tensor_tensor(km[:, j % 2, :, :], bc(keys, 1, HH), bc(w.heads, 2, P), ALU.mult
                                   ).then_inc(keys_spread, 1)

            def recalled_keys(g, u):
                keys = k.Y[:, bass.ds(g * TILES + u, 1), 0:P].rearrange("p a t -> p (a t)")
                pool.tensor_tensor(km[:, u % 2, :, :], bc(keys, 1, HH), bc(w.heads, 2, P), ALU.mult
                                   ).then_inc(keys_spread, 1)

            def first(g, before):
                if recalled:
                    if before is not None:
                        pool.wait_ge(scores_ready, before * UNITS + 3 * C)
                    recalled_keys(g, 0)
                    return
                if rope:
                    rotate(g, range(C))
                    pool.wait_ge(rotated, g * (NQK // 2) + C)
                else:
                    pool.wait_ge(qk_evacuated, g * NQK + C)
                if before is not None:
                    pool.wait_ge(scores_ready, before * UNITS + UNITS - 1)
                spread_unit(g, 0)
                if rope:
                    rotate(g, range(C, 2 * C))

            def spread(g):
                if recalled:
                    for u in range(1, TILES):
                        if u >= 2:
                            pool.wait_ge(scores_ready, g * UNITS + (u - 1) * C)
                        recalled_keys(g, u)
                    return
                for j in range(1, UNITS):
                    spread_unit(g, j)

            stage_x(0)
            if biased:
                biased.stage(pool, 0)
            first(0, None)
            with pool.Fori(0, TURNS - 1) as g:
                spread(g)
                pool.wait_ge(x_turned, (g + 1) * C)
                stage_x(g + 1)
                norm.roots(pool, g)
                first(g + 1, g)
                if biased:
                    biased.stage(pool, g + 1)
            spread(TURNS - 1)
            norm.roots(pool, TURNS - 1)

        @block.tensor
        def _(pe):
            k.wait_weights(pe, stage)
            pe.wait_ge(ones_set, 1)

            def turn_x(g):
                pe.wait_ge(x_staged, g + 1)
                for c in range(C):
                    for u in range(TILES):
                        mm = nc.tensor.transpose(ps[:, T_BANK + c, u * P:(u + 1) * P],
                                                 xs[:, u, c * P:(c + 1) * P], k.ident[:, :])
                    mm.then_inc(x_turned, 1)

            def project(g):
                pe.wait_ge(xT_ready, (g + 1) * C)
                if cross:
                    pe.wait_ge(loaded, (g + 1) * 16)
                for p in range(NP):
                    bank = ps[:, S_BANK + p % 4, :]
                    if p >= 4:
                        pe.wait_ge(qk_evacuated, g * NQK + p - 3)
                    if p < NQK:
                        name, co = qk[p]
                        frm = xT if name[0] == "q" else kvT
                        for ci in range(C):
                            mm = nc.tensor.matmul(bank, w["w" + name][:, ci, co * P:(co + 1) * P], frm[:, ci, :],
                                                  start=(ci == 0), stop=(ci == C - 1))
                    else:
                        for u in (0, 1):
                            t = 2 * (p - NQK) + u
                            for ci in range(C):
                                mm = nc.tensor.matmul(bank[:, u * D:(u + 1) * D], kvT[:, ci, t * P:(t + 1) * P],
                                                      w.wv[:, ci, :], start=(ci == 0), stop=(ci == C - 1))
                    mm.then_inc(projected, 1)

            def units(g, more):
                def scores(j):
                    u, c = divmod(j, C)
                    at = u if recalled else j
                    pe.wait_ge(keys_spread, g * SPREADS + at + 1)
                    if j == 0:
                        pe.wait_ge(qk_evacuated, (g + 1) * NQK)
                        if rope:
                            pe.wait_ge(rotated, (g + 1) * (NQK // 2))
                        if not recalled:
                            pe.wait_ge(v_ready, (g + 1) * 2)
                    if j >= 2:
                        pe.wait_ge(shifted, g * UNITS + j - 1)
                    out = s_psum(j)
                    for b in range(2):
                        mm = nc.tensor.matmul(out[:, b * 4:b * 4 + 4, :], qT[:, c, u * P:(u + 1) * P],
                                              km[:, at % 2, b * 4:b * 4 + 4, :], start=True, stop=True)
                    mm.then_inc(scores_ready, 1)

                def values(j):
                    u, c = divmod(j, C)
                    pe.wait_ge(probsT_ready, g * UNITS + j + 1)
                    if c == 0 and u >= 1:
                        pe.wait_ge(o_normalised, g * TILES + u)
                    for h in range(HH):
                        v = (k.Y[:, bass.ds(g * TILES + u, 1), P:P + DH + 1].rearrange("p a e -> p (a e)") if recalled
                             else va[:, u, c * HH + h, :])
                        mm = nc.tensor.matmul(o_psum[:, c * HH + h, :], pT[:, j % 2, h, :], v,
                                              start=True, stop=True)
                    if c == C - 1:
                        mm.then_inc(o_ready, 1)

                def turn_probs(j):
                    pe.wait_ge(probs_ready, g * UNITS + j + 1)
                    for h in range(HH):
                        mm = nc.tensor.transpose(pt_psum[:, h, :], pr[:, j % 2, h, :], k.ident[:, :])
                    mm.then_inc(probs_turned, 1)

                def turn_o(u):
                    pe.wait_ge(o_normalised, g * TILES + u + 1)
                    if u >= 1:
                        norm.wait_added(pe, g * TILES + u)
                    for c in range(C):
                        mm = nc.tensor.transpose(oT_psum[:, c, :], on[:, c * P:(c + 1) * P], k.ident[:, :])
                    mm.then_inc(oT_turned, 1)

                def project_out(u):
                    pe.wait_ge(oT_ready, g * TILES + u + 1)
                    for c in range(C):
                        mm = nc.tensor.matmul(y_psum, oT[:, c, :], w.wo[:, c, :], start=(c == 0),
                                              stop=(c == C - 1))
                    mm.then_inc(y_ready, 1)

                scores(0)
                for j in STEPS:
                    if j + 1 < UNITS:
                        scores(j + 1)
                    if 1 <= j <= UNITS:
                        values(j - 1)
                    if j < UNITS:
                        turn_probs(j)
                    if more and j == UNITS + 1:
                        turn_x(g + 1)
                    if out_proj and j >= 3 and j % 2 == 1 and (j - 3) // 2 < TILES:
                        turn_o((j - 3) // 2)
                    if out_proj and j >= 4 and j % 2 == 0:
                        project_out((j - 4) // 2)
                if more:
                    project(g + 1)

            turn_x(0)
            project(0)
            with pe.Fori(0, TURNS - 1) as g:
                units(g, True)
            units(TURNS - 1, False)

        @block.scalar
        def _(act):
            k.wait_weights(act, stage)
            act.wait_ge(ones_set, 1)
            def copy_x(g):
                for c in range(C):
                    act.wait_ge(x_turned, g * C + c + 1)
                    nc.scalar.copy(xT[:, c, :], ps[:, T_BANK + c, :]).then_inc(xT_ready, 1)

            def evacuate(g):
                if not rope:
                    for p, (name, c) in enumerate(qk):
                        act.wait_ge(projected, g * NP + p + 1)
                        bias = 0.0 if recalled else (w.bq if name == "q" else w.bk)[:, c:c + 1]
                        nc.scalar.activation((qT if name == "q" else kT)[:, c, :], ps[:, S_BANK + p % 4, :],
                                             ACT.Identity, bias=bias).then_inc(qk_evacuated, 1)
                for p in range(NQK, NP):
                    act.wait_ge(projected, g * NP + p + 1)
                    t = 2 * (p - NQK)
                    nc.scalar.copy(va[:, t:t + 2, :, 0:DH],
                                   ps[:, S_BANK + p % 4, :].rearrange("p (u h e) -> p u h e", u=2, e=DH)
                                   ).then_inc(v_ready, 1)

            def units(g, more):
                for j in STEPS:
                    if 1 <= j <= UNITS:
                        act.wait_ge(probs_turned, g * UNITS + j)
                        nc.scalar.copy(pT[:, (j - 1) % 2, :, :], pt_psum).then_inc(probsT_ready, 1)
                    if j < UNITS:
                        act.wait_ge(shifted, g * UNITS + j + 1)
                        nc.scalar.activation(pr[:, j % 2, :, :], pr[:, j % 2, :, :], ACT.Exp,
                                             scale=1.0 if mask else DH ** -0.5).then_inc(probs_ready, 1)
                    if more and j == UNITS + 1:
                        copy_x(g + 1)
                    if out_proj and j >= 3 and j % 2 == 1 and (j - 3) // 2 < TILES:
                        act.wait_ge(oT_turned, g * TILES + (j - 3) // 2 + 1)
                        for c in range(C):
                            a = nc.scalar.activation(oT[:, c, :], oT_psum[:, c, :], ACT.Identity,
                                                     bias=0.0 if recalled else w.bv[:, c:c + 1])
                        a.then_inc(oT_ready, 1)
                    if more and j == UNITS + 1:
                        evacuate(g + 1)

            copy_x(0)
            evacuate(0)
            with act.Fori(0, TURNS - 1) as g:
                units(g, True)
            units(TURNS - 1, False)

        @block.vector
        def _(dve):
            k.wait_weights(dve, stage)

            def evacuate(g):
                if rope:
                    for p, (name, c) in enumerate(qk):
                        dve.wait_ge(projected, g * NP + p + 1)
                        if p % 2 and p >= 5:
                            dve.wait_ge(rotated, g * (NQK // 2) + (p - 3) // 2)
                        to = half[(p // 2) % 2] if p % 2 else (qT if name[0] == "q" else kT)[:, c, :]
                        table = w["sin" if p % 2 else "cos"]
                        dve.scalar_tensor_tensor(out=to.rearrange("p (u t) -> p u t", t=P),
                                                 in0=ps[:, S_BANK + p % 4, :].rearrange("p (u t) -> p u t", t=P),
                                                 scalar=w["b" + name][:, c:c + 1], in1=bc(table, 1, TILES),
                                                 op0=ALU.add, op1=ALU.mult).then_inc(qk_evacuated, 1)

            def turn(g, chain, more):
                for j in STEPS:
                    if j < UNITS:
                        n = g * UNITS + j
                        dve.wait_ge(scores_ready, n + 1)
                        if j >= 2:
                            dve.wait_ge(probs_turned, n - 1)
                        s = s_psum(j)
                        if mask:
                            if mask == "batch":
                                if j == 0:
                                    dve.wait_ge(mask_loaded, (g + 1) * 16)
                                m = mk[:, j // C, :]
                            else:
                                m = w.causal
                            chain(dve.scalar_tensor_tensor(out=pr[:, j % 2, :, :], in0=s, scalar=DH ** -0.5,
                                                           in1=bc(m, 1, HH), op0=ALU.mult, op1=ALU.add))
                            s = pr[:, j % 2, :, :]
                        chain(dve.tensor_reduce(mx[:, j % 2, :], s, AX.X, ALU.max))
                        dve.tensor_tensor(pr[:, j % 2, :, :], s, bc(mx[:, j % 2, :], 2, P), ALU.subtract).then_inc(shifted, 1)
                    if j >= 2 and j % 2 == 0 and (j - 2) // 2 < TILES:
                        u = (j - 2) // 2
                        dve.wait_ge(o_ready, g * TILES + u + 1)
                        chain(dve.reciprocal(ri[:, :], o_psum[:, :, DH]))
                        if out_proj and u >= 1:
                            dve.wait_ge(oT_turned, g * TILES + u)
                        dve.tensor_tensor(on[:, :].rearrange("p (h e) -> p h e", e=DH), o_psum[:, :, 0:DH],
                                          bc(ri[:, :], 2, DH), ALU.mult).then_inc(o_normalised, 1)
                        if not out_proj:
                            dve.wait_ge(o_normalised, g * TILES + u + 1)
                            chain(dve.tensor_tensor(on[:, :], on[:, :], w.bv_row, ALU.add))
                            norm.add(dve, chain, g, u, on[:, :])
                    if out_proj and j >= 4 and j % 2 == 0:
                        u = (j - 4) // 2
                        dve.wait_ge(y_ready, g * TILES + u + 1)
                        norm.add(dve, chain, g, u, y_psum, x=biased.tile(dve, g, u) if biased else None)
                norm.moments(dve, chain, g)
                if more:
                    evacuate(g + 1)
                norm.apply(dve, chain, g)
                chain.end()

            per = UNITS * (2 if mask else 1) + TILES * (1 if out_proj else 2) + norm.chained()
            norm.open(dve)
            evacuate(0)
            with dve.Fori(0, TURNS - 1) as g:
                turn(g, Chain(dve, dve_chain, g, per), True)
            turn(TURNS - 1, Chain(dve, dve_chain, TURNS - 1, per), False)
    sem.release()


def delta_stage(k):
    stage = "L0_attn"
    nc, ps, w, A = k.nc, k.psum, k.begin(stage), k.arena
    sem = Semaphores(nc, stage)
    M, DK, DHEADS = 8, 64, 8
    HALVES = 2
    HALF = DHEADS // HALVES
    CH = HALF * M
    PAIRS = DHEADS // 2
    Q = 32
    NQ = P // Q
    GROUPS, NPACKS = CH // 4, CH // 8
    W = DHEADS * DK
    norm = Norm(k, sem, k.X, k.X, tiles=1)
    names = """x_staged x_turned xT_ready qk_projected projected evacuated squared squares_summed roots_ready qk_normalised
    qk_turned qkT_ready swapped swapped_ready decays_clipped decays_ready consts_ready tables_ready
    angles_ready reduced halves_ready rotated keys_padded masked_decays exponents_ready decay_ready products_ready
    blocks_ready outputs_ready blocks_taken inverse_ready solved coupled solution_ready rest_ready weighted
    o_ready o_gated y_ready dve_chain pool_chain act_chain""".split()
    s = {n: sem(n) for n in names}

    def chains(i):
        at = (i // 4 * 2 + i % 2) * M + i // 2 % 2 * 4
        return slice(at, at + 4)

    def flat(ap):
        letters = "abcd"[:len(ap.shape) - 1]
        return ap.rearrange("p %s -> p (%s)" % (" ".join(letters), " ".join(letters)))

    xs, xT = A(D), A(C, P)
    v, gateT, bt = A(W), A(PAIRS, P), A(2 * DHEADS * M)
    qkT, qkS = A(2, PAIRS, P), A(2, PAIRS, P)
    kq = A(2, 4, 2, P)
    kz = A(2, 2, 4, P)
    t1, gm = A(2, 4, P), A(2, 4, P)
    qkn, squares = flat(t1), flat(gm)
    Ls, Bs = [A(CH, P) for _ in range(HALVES)], [A(CH, P) for _ in range(HALVES)]
    inv, prod = A(Q, Q), A(Q * Q // 4)
    ur = A(HALF, M, DK)
    ogT = flat(kq)[:, 0:W].rearrange("p (c t) -> p c t", t=P)
    ss, exponent, decay = A(2 * DHEADS), A(2 * DHEADS), A(DHEADS * M)
    rho, modes, mode_sum = A(DHEADS * M), A(DHEADS, M), A(DHEADS)
    wb, omega, tiny = A(DHEADS, M), A(PAIRS, M), A(2 * DHEADS)
    minus_beta = bt[:, DHEADS * M:]
    ident_h, later_h = A(P, dtype=BF16), A(4, P, dtype=BF16)
    sin = flat(k.Y).rearrange("p (c m t) -> p c m t", m=M, t=P)
    other = Arena(k.next_region(stage), REGION)
    cos, lanes, Ts = other(PAIRS, M, P), other(Q, Q), [other(CH, Q) for _ in range(HALVES)]

    TWO_PI = 2 * np.pi
    C1 = 6.28125
    C2 = float(np.float32(np.floor((TWO_PI - C1) * 2 ** 22) / 2 ** 22))
    C3 = float(np.float32(TWO_PI - C1 - C2))
    PI = float(np.float32(3.1415925))
    MAGIC = 1.5 * 2 ** 23

    with nc.Block() as block:
        @block.sync
        def _(sp):
            sp.wait_ge(s["y_ready"], B)
            k.prefetch(sp, stage)

        @block.gpsimd
        def _(pool):
            k.wait_weights(pool, stage)
            pool.memset(exponent, -0.5)
            pool.memset(tiny, 1e-6)
            pool.memset(flat(kz), 0.0).then_inc(s["consts_ready"], 1)
            pool.wait_ge(s["consts_ready"], 1)

            def stage_x(g):
                pool.tensor_copy(xs, k.X[:, bass.ds(g, 1), :].rearrange("p a d -> p (a d)")).then_inc(s["x_staged"], 1)

            def roots(g):
                pool.wait_ge(s["squares_summed"], g + 1)
                pool.tensor_tensor(ss, ss, tiny, ALU.add).then_inc(s["pool_chain"], 1)
                pool.wait_ge(s["pool_chain"], g + 1)
                pool.tensor_tensor(ss, ss, exponent, ALU.pow).then_inc(s["roots_ready"], 1)

            def turn(g, more):
                pool.wait_ge(s["x_turned"], g + 1)
                if more:
                    stage_x(g + 1)
                pool.wait_ge(s["decays_ready"], g + 1)
                for hf in range(HALVES):
                    u = g * HALVES + hf
                    for p in range(NPACKS):
                        n = u * NPACKS + p
                        for hh in range(2):
                            i = 2 * p + hh
                            if hf or i >= 2:
                                pool.wait_ge(s["exponents_ready"], u * GROUPS + i - 1)
                            at = (hf * HALF + p // 2 * 2 + hh) * M + p % 2 * 4
                            pool.tensor_tensor(gm[:, hh, :, :], bc(decay[:, at:at + 4], 2, P), bc(w.incl, 1, 4),
                                               ALU.mult).then_inc(s["masked_decays"], 1)
                            for j in range(2 if hh == 0 else 0):
                                pool.wait_ge(s["halves_ready"], n * 2 + j + 1)
                                both = kq[:, p % 2, :, j, :]
                                pool.tensor_tensor(both, both, t1[:, j, :, :], ALU.add).then_inc(s["rotated"], 1)
                if more:
                    roots(g + 1)
                for hf in range(HALVES):
                    for h in range(HALF):
                        u = g * HALVES + hf
                        pool.wait_ge(s["solution_ready"], ((u * NQ) + NQ - 1) * HALF + h + 1)
                        pool.tensor_tensor(ur[:, h, :, :], ur[:, h, :, :], bc(wb[:, hf * HALF + h, :], 2, DK), ALU.mult
                                           ).then_inc(s["weighted"], 1)
                norm.roots(pool, g)

            stage_x(0)
            roots(0)
            with pool.Fori(0, B - 1) as g:
                turn(g, True)
            turn(B - 1, False)

        @block.tensor
        def _(pe):
            k.wait_weights(pe, stage)
            pe.wait_ge(s["tables_ready"], 1)
            pe.wait_ge(s["consts_ready"], 1)

            def carrier():
                nc.tensor.matmul(ps[:, 3, 0:1], ident_h, ident_h[:, 0:1], start=True, stop=True)

            def project(g):
                pe.wait_ge(s["x_staged"], g + 1)
                for c in range(C):
                    mm = nc.tensor.transpose(ps[:, 3, c * P:(c + 1) * P], xs[:, c * P:(c + 1) * P], k.ident)
                mm.then_inc(s["x_turned"], 1)
                pe.wait_ge(s["xT_ready"], g + 1)
                for i, m in enumerate((w.wk, w.wq)):
                    for c in range(C):
                        mm = nc.tensor.matmul(ps[:, i, :], xT[:, c, :], m[:, c, :], start=(c == 0), stop=(c == C - 1))
                    mm.then_inc(s["qk_projected"], 1)

            def turn_qk(g):
                pe.wait_ge(s["qk_normalised"], g + 1)
                for j in range(2):
                    for c in range(PAIRS):
                        mm = nc.tensor.transpose(ps[:, j, c * P:(c + 1) * P],
                                                 qkn[:, j * W + c * P:j * W + (c + 1) * P], k.ident)
                    mm.then_inc(s["qk_turned"], 1)

            def swap(g):
                for j in range(2):
                    pe.wait_ge(s["qkT_ready"], g * 2 + j + 1)
                    nc.tensor.matmul(ps[:, j, :], w.swap, qkT[:, j, :, :], start=True, stop=True
                                     ).then_inc(s["swapped"], 1)

            def turn(g, more):
                for bank, m in ((6, w.wbt), (7, w.wv)):
                    for c in range(C):
                        mm = nc.tensor.matmul(ps[:, bank, 0:m.shape[2]], xT[:, c, :], m[:, c, :],
                                              start=(c == 0), stop=(c == C - 1))
                    mm.then_inc(s["projected"], 1)
                for co in range(PAIRS):
                    for c in range(C):
                        mm = nc.tensor.matmul(ps[:, 5, co * P:(co + 1) * P], w.wg[:, c, co * P:(co + 1) * P], xT[:, c, :],
                                              start=(c == 0), stop=(c == C - 1))
                mm.then_inc(s["projected"], 1)
                pe.wait_ge(s["swapped_ready"], (g + 1) * 2)
                pe.wait_ge(s["evacuated"], (g + 1) * 3)

                for hf in range(HALVES):
                    u = g * HALVES + hf
                    for i in range(GROUPS):
                        n, p, hh = u * GROUPS + i, i // 2, i % 2
                        pe.wait_ge(s["masked_decays"], n + 1)
                        if hf or i >= 2:
                            pe.wait_ge(s["decay_ready"], n - 1)
                        bank = ps[:, hh, :]
                        nc.tensor.matmul(bank, w.after, gm[:, hh, :, :], start=True, stop=False)
                        nc.tensor.matmul(bank, ident_h, later_h[:, :, :], start=False, stop=True
                                         ).then_inc(s["exponents_ready"], 1)
                        if hh == 0:
                            pe.wait_ge(s["rotated"], (u * NPACKS + p + 1) * 2)
                            pe.wait_ge(s["keys_padded"], u * NPACKS + p + 1)
                        if hf or i >= 2:
                            pe.wait_ge(s["outputs_ready"], n - 1)
                        for m in range(4):
                            mm = nc.tensor.matmul(ps[:, 2 + 2 * hh + m // 2, (m % 2) * 2 * P:(m % 2 + 1) * 2 * P],
                                                  kz[:, p % 2, hh, m, :], kq[:, p % 2, m, :, :], start=True, stop=True)
                        mm.then_inc(s["products_ready"], 1)

                pe.wait_ge(s["outputs_ready"], (g + 1) * HALVES * GROUPS)
                if more:
                    project(g + 1)
                for hf in range(HALVES):
                    u = g * HALVES + hf
                    Lt, Bt, Tt = Ls[hf], Bs[hf], Ts[hf]
                    pe.wait_ge(s["inverse_ready"], u + 1)
                    carrier()
                    for q in range(NQ):
                        rows = slice(q * Q, (q + 1) * Q)
                        if q:
                            for h in range(HALF):
                                pe.wait_ge(s["solution_ready"], (u * NQ + q - 1) * HALF + h + 1)
                                carrier()
                                if hf == 0:
                                    nc.tensor.matmul(ps[rows, 4 + h, :], k.ident[:, rows],
                                                     bc(v[:, h * DK:(h + 1) * DK], 1, M), start=True, stop=False)
                                for m in range(M):
                                    mm = nc.tensor.matmul(ps[rows, 4 + h, m * DK:(m + 1) * DK],
                                                          Lt[0:q * Q, h * M + m, rows], ur[0:q * Q, h, m, :],
                                                          start=(hf == 1), stop=(hf == 1 or m == M - 1))
                                mm.then_inc(s["coupled"], 1)
                        for h in range(HALF):
                            if q:
                                pe.wait_ge(s["rest_ready"], (u * (NQ - 1) + q - 1) * HALF + h + 1)
                                carrier()
                            for m in range(M):
                                rhs = ur[rows, h, m, :] if q else v[rows, (hf * HALF + h) * DK:(hf * HALF + h + 1) * DK]
                                mm = nc.tensor.matmul(ps[rows, 4 + h, m * DK:(m + 1) * DK], Tt[rows, h * M + m, :], rhs,
                                                      start=True, stop=True)
                            mm.then_inc(s["solved"], 1)
                        if more and hf == 0 and q == 1:
                            turn_qk(g + 1)
                        if more and hf == 0 and q == 2:
                            swap(g + 1)
                    if hf:
                        pe.wait_ge(s["o_gated"], g * HALVES + 1)
                    for h in range(HALF):
                        pe.wait_ge(s["weighted"], u * HALF + h + 1)
                        for m in range(M):
                            mm = nc.tensor.matmul(ps[h % 2 * DK:(h % 2 + 1) * DK, 2, (hf * 2 + h // 2) * P:(hf * 2 + h // 2 + 1) * P],
                                                  ur[:, h, m, :], Bt[:, h * M + m, :], start=(m == 0), stop=(m == M - 1))
                    mm.then_inc(s["o_ready"], 1)
                pe.wait_ge(s["o_gated"], (g + 1) * HALVES)
                for c in range(PAIRS):
                    mm = nc.tensor.matmul(ps[:, 3, 0:D], ogT[:, c, :], w.wo[:, c, :], start=(c == 0), stop=(c == PAIRS - 1))
                mm.then_inc(s["y_ready"], 1)
                norm.wait_added(pe, g + 1)

            project(0)
            turn_qk(0)
            swap(0)
            with pe.Fori(0, B - 1) as g:
                turn(g, True)
            turn(B - 1, False)

        @block.scalar
        def _(act):
            k.wait_weights(act, stage)
            nc.scalar.activation(omega[:, :, :], w.omega, ACT.Exp).then_inc(s["angles_ready"], 1)
            nc.scalar.activation(rho, w.log_decay, ACT.Sigmoid, scale=-1.0).then_inc(s["angles_ready"], 1)
            act.wait_ge(s["reduced"], 1)
            act.wait_ge(s["consts_ready"], 1)
            nc.scalar.activation(modes[:, :, :], modes[:, :, :], ACT.Exp).then_inc(s["angles_ready"], 1)
            for c in range(PAIRS):
                act.wait_ge(s["reduced"], c + 2)
                for table in (sin, cos):
                    nc.scalar.activation(table[:, c, :, :], table[:, c, :, :], ACT.Sin).then_inc(s["act_chain"], 1)
            act.wait_ge(s["act_chain"], 2 * PAIRS)
            nc.scalar.copy(ident_h, k.ident).then_inc(s["tables_ready"], 1)

            def squared(g):
                act.wait_ge(s["x_turned"], g + 1)
                nc.scalar.copy(xT[:, :, :], ps[:, 3, 0:D].rearrange("p (c t) -> p c t", t=P)).then_inc(s["xT_ready"], 1)
                for j in range(2):
                    act.wait_ge(s["qk_projected"], g * 2 + j + 1)
                    nc.scalar.activation(squares[:, j * W:(j + 1) * W], ps[:, j, :], ACT.Square
                                         ).then_inc(s["squared"], 1)

            def take(g, to, turned, ready):
                for j in range(2):
                    act.wait_ge(s[turned], g * 2 + j + 1)
                    nc.scalar.copy(to[:, j, :, :], ps[:, j, :].rearrange("p (c t) -> p c t", t=P)
                                   ).then_inc(s[ready], 1)

            def turn(g, more):
                act.wait_ge(s["projected"], g * 3 + 1)
                nc.scalar.activation(bt, ps[:, 6, 0:2 * DHEADS * M], ACT.Sigmoid).then_inc(s["evacuated"], 1)
                act.wait_ge(s["projected"], g * 3 + 2)
                nc.scalar.copy(v, ps[:, 7, :]).then_inc(s["evacuated"], 1)
                act.wait_ge(s["projected"], g * 3 + 3)
                nc.scalar.activation(gateT[:, :, :], ps[:, 5, :].rearrange("p (c t) -> p c t", t=P), ACT.Sigmoid
                                     ).then_inc(s["evacuated"], 1)
                act.wait_ge(s["decays_clipped"], g + 1)
                nc.scalar.activation(decay, decay, ACT.Ln).then_inc(s["decays_ready"], 1)
                for hf in range(HALVES):
                    u = g * HALVES + hf
                    for p in range(NPACKS):
                        n = u * NPACKS + p
                        act.wait_ge(s["rotated"], n * 2 + 1)
                        for hh in range(2):
                            rows = slice(hh * DK, (hh + 1) * DK)
                            a = nc.scalar.copy(kz[rows, p % 2, hh, :, :], kq[rows, p % 2, :, 0, :])
                        a.then_inc(s["keys_padded"], 1)
                        for i in (2 * p, 2 * p + 1):
                            act.wait_ge(s["exponents_ready"], u * GROUPS + i + 1)
                            nc.scalar.activation(Bs[hf][:, chains(i), :],
                                                 ps[:, i % 2, :].rearrange("p (c t) -> p c t", t=P),
                                                 ACT.Exp).then_inc(s["decay_ready"], 1)
                if more:
                    squared(g + 1)
                for hf in range(HALVES):
                    u = g * HALVES + hf
                    for q in range(NQ):
                        rows = slice(q * Q, (q + 1) * Q)
                        for h in range(HALF if hf == 0 and q else 0):
                            act.wait_ge(s["coupled"], (u * (NQ - 1) + q - 1) * HALF + h + 1)
                            nc.scalar.copy(ur[rows, h, :, :], ps[rows, 4 + h, :].rearrange("p (m e) -> p m e", e=DK)
                                           ).then_inc(s["rest_ready"], 1)
                        for h in range(HALF):
                            act.wait_ge(s["solved"], (u * NQ + q) * HALF + h + 1)
                            nc.scalar.copy(ur[rows, h, :, :], ps[rows, 4 + h, :].rearrange("p (m e) -> p m e", e=DK)
                                           ).then_inc(s["solution_ready"], 1)
                        if more and hf == 0 and q == 1:
                            take(g + 1, qkT, "qk_turned", "qkT_ready")
                        if more and hf == 0 and q == 2:
                            take(g + 1, qkS, "swapped", "swapped_ready")

            squared(0)
            take(0, qkT, "qk_turned", "qkT_ready")
            take(0, qkS, "swapped", "swapped_ready")
            with act.Fori(0, B - 1) as g:
                turn(g, True)
            turn(B - 1, False)

        @block.vector
        def _(dve):
            k.wait_weights(dve, stage)
            norm.open(dve)
            once = Chain(dve, s["dve_chain"])
            once(dve.tensor_reduce(mode_sum, w.modes, AX.X, ALU.max))
            dve.tensor_tensor(modes[:, :, :], w.modes, bc(mode_sum, 2, M), ALU.subtract).then_inc(s["reduced"], 1)
            once(dve.tensor_scalar(later_h[:, 0, :], w.incl, -1.0, 1e30, ALU.add, ALU.mult))
            once(dve.tensor_copy(later_h[:, 1:4, :], bc(later_h[:, 0, :], 1, 3)))
            dve.wait_ge(s["angles_ready"], 3)
            once(dve.tensor_reduce(mode_sum, modes[:, :, :], AX.X, ALU.add))
            once(dve.reciprocal(mode_sum, mode_sum))
            once(dve.tensor_tensor(modes[:, :, :], modes[:, :, :], bc(mode_sum, 2, M), ALU.mult))
            x, n = Ls[0][:, 0:M, :], Ls[0][:, M:2 * M, :]
            for c in range(PAIRS):
                once(dve.tensor_tensor(x, bc(w.position, 1, M), bc(omega[:, c, :], 2, P), ALU.mult))
                once(dve.tensor_scalar(x, x, w.inv_freq[:, 0:1], None, ALU.mult))
                once(dve.tensor_scalar(n, x, 1 / TWO_PI, MAGIC, ALU.mult, ALU.add))
                once(dve.tensor_scalar(n, n, MAGIC, None, ALU.subtract))
                r, quarter = sin[:, c, :, :], cos[:, c, :, :]
                once(dve.scalar_tensor_tensor(out=r, in0=n, scalar=-C1, in1=x, op0=ALU.mult, op1=ALU.add))
                once(dve.scalar_tensor_tensor(out=r, in0=n, scalar=-C2, in1=r, op0=ALU.mult, op1=ALU.add))
                once(dve.scalar_tensor_tensor(out=r, in0=n, scalar=-C3, in1=r, op0=ALU.mult, op1=ALU.add))
                once(dve.tensor_scalar(n, r, TWO_PI / 4, -TWO_PI, ALU.is_gt, ALU.mult))
                once(dve.scalar_tensor_tensor(out=quarter, in0=r, scalar=TWO_PI / 4, in1=n, op0=ALU.add, op1=ALU.add))
                once(dve.tensor_scalar(r, r, PI, -PI, ALU.min, ALU.max))
                dve.tensor_scalar(quarter, quarter, PI, -PI, ALU.min, ALU.max).then_inc(s["reduced"], 1)
            dve.wait_ge(s["tables_ready"], 1)

            def rotate(g, hf, p):
                n = (g * HALVES + hf) * NPACKS + p
                c, modes4 = hf * 2 + p // 2, slice(p % 2 * 4, p % 2 * 4 + 4)
                for j in range(2):
                    dve.tensor_tensor(kq[:, p % 2, :, j, :], bc(qkT[:, j, c, :], 1, 4), cos[:, c, modes4, :], ALU.mult)
                    if hf or p:
                        dve.wait_ge(s["rotated"], (n - 1) * 2 + j + 1)
                    dve.tensor_tensor(t1[:, j, :, :], bc(qkS[:, j, c, :], 1, 4), sin[:, c, modes4, :], ALU.mult
                                      ).then_inc(s["halves_ready"], 1)

            def evacuate(g, hf, p):
                steps = []
                for i in (2 * p, 2 * p + 1):
                    n = (g * HALVES + hf) * GROUPS + i
                    c0 = chains(i).start
                    Lt, Bt = Ls[hf], Bs[hf]
                    kk = ps[:, 2 + 2 * (i % 2):4 + 2 * (i % 2), :].rearrange("p b (c k t) -> p (b c) k t", c=2, k=2)

                    def coupling(m, n=n, c0=c0, kk=kk):
                        if m == 0:
                            dve.wait_ge(s["products_ready"], n + 1)
                            dve.wait_ge(s["decay_ready"], n + 1)
                        at = hf * CH + c0 + m
                        a = dve.scalar_tensor_tensor(out=Lt[:, c0 + m, :], in0=kk[:, m, 0, :],
                                                     scalar=minus_beta[:, at:at + 1], in1=Bt[:, c0 + m, :],
                                                     op0=ALU.mult, op1=ALU.mult)
                        if m == 3:
                            a.then_inc(s["blocks_ready"], 1)

                    def outputs(n=n, i=i, kk=kk):
                        dve.wait_ge(s["blocks_ready"], n + 1)
                        dve.tensor_tensor(Bt[:, chains(i), :], kk[:, :, 1, :], Bt[:, chains(i), :], ALU.mult
                                          ).then_inc(s["outputs_ready"], 1)
                    steps += [lambda m=m, f=coupling: f(m) for m in range(4)] + [outputs]
                return steps

            def invert(g, hf, ch, between):
                u = g * HALVES + hf
                Lt, Tt = Ls[hf], Ts[hf]
                between = list(between)

                def linked(ins):
                    ins.then_inc(ch.sem, 1)
                    ch.n += 1
                    due = ch.base + ch.n
                    step = between.pop(0) if between else None
                    if step:
                        step()
                    dve.wait_ge(ch.sem, due)

                dve.wait_ge(s["outputs_ready"], (u + 1) * GROUPS)
                for q in range(NQ):
                    rows = slice(q * Q, (q + 1) * Q)
                    a = dve.transpose(lanes[rows, :, :], Lt[rows, :, rows].rearrange("p c t -> p t c"))
                a.then_inc(s["blocks_taken"], 1)
                dve.wait_ge(s["blocks_taken"], u + 1)
                linked(dve.tensor_copy(inv[:, :, :], lanes[:, :, :]))
                dve.memset(flat(inv)[:, 0:Q * Q:Q + 1], 1.0)
                for j in range(1, Q - 1):
                    below = Q - 1 - j
                    part = prod[:, 0:below * j].rearrange("p (a b) -> p a b", b=j)
                    linked(dve.tensor_tensor(part, bc(lanes[:, j + 1:, j], 2, j), bc(inv[:, j, 0:j], 1, below), ALU.mult))
                    linked(dve.tensor_tensor(inv[:, j + 1:, 0:j], inv[:, j + 1:, 0:j], part, ALU.add))
                assert not between
                dve.transpose(Tt[:, :, :].rearrange("p c t -> p t c"), inv[:, :, :]).then_inc(s["inverse_ready"], 1)

            def rest(g, q, h):
                n = (g * HALVES + 1) * (NQ - 1) + q - 1
                rows = slice(q * Q, (q + 1) * Q)
                dve.wait_ge(s["coupled"], n * HALF + h + 1)
                at = (HALF + h) * DK
                dve.tensor_tensor(ur[rows, h, :, :], bc(v[rows, at:at + DK], 1, M),
                                  ps[rows, 4 + h, :].rearrange("p (m e) -> p m e", e=DK), ALU.add
                                  ).then_inc(s["rest_ready"], 1)

            def gated(g, hf):
                dve.wait_ge(s["o_ready"], g * HALVES + hf + 1)
                dve.tensor_tensor(ogT[:, 2 * hf:2 * hf + 2, :], ps[:, 2, hf * 2 * P:(hf + 1) * 2 * P].rearrange("p (c t) -> p c t", t=P),
                                  gateT[:, 2 * hf:2 * hf + 2, :], ALU.mult).then_inc(s["o_gated"], 1)

            def sum_squares(g):
                dve.wait_ge(s["squared"], (g + 1) * 2)
                dve.tensor_reduce(ss, squares.rearrange("p (h e) -> p h e", e=DK), AX.X, ALU.add
                                  ).then_inc(s["squares_summed"], 1)

            def normalise(g):
                dve.wait_ge(s["roots_ready"], g + 1)
                for j in range(2):
                    out = qkn[:, j * W:(j + 1) * W].rearrange("p (h e) -> p h e", e=DK)
                    a = dve.scalar_tensor_tensor(out=out, in0=ps[:, j, :].rearrange("p (h e) -> p h e", e=DK),
                                                 scalar=DK ** -0.5 if j else 1.0,
                                                 in1=bc(ss[:, j * DHEADS:(j + 1) * DHEADS], 2, DK),
                                                 op0=ALU.mult, op1=ALU.mult)
                a.then_inc(s["qk_normalised"], 1)

            def turn(g, more):
                ch = Chain(dve, s["dve_chain"], g, 1 + HALVES * (2 * (Q - 2) + 1) + norm.chained())
                ch.base = once.n + g * ch.per_turn
                dve.wait_ge(s["evacuated"], g * 3 + 1)
                ch(dve.tensor_tensor(decay, bt[:, DHEADS * M:], rho, ALU.mult))
                dve.tensor_scalar(decay, decay, 1e-6, None, ALU.max).then_inc(s["decays_clipped"], 1)
                dve.tensor_scalar(minus_beta, bt[:, 0:DHEADS * M], -1.0, None, ALU.mult)
                dve.tensor_tensor(wb[:, :, :], bt[:, 0:DHEADS * M].rearrange("p (h m) -> p h m", m=M), modes[:, :, :],
                                  ALU.mult)
                dve.wait_ge(s["swapped_ready"], (g + 1) * 2)
                rotate(g, 0, 0)
                rotate(g, 0, 1)
                for p in range(NPACKS):
                    for step in evacuate(g, 0, p):
                        step()
                    rotate(g, (p + 2) // NPACKS, (p + 2) % NPACKS)
                second = []
                for p in range(NPACKS):
                    second += evacuate(g, 1, p)
                    if p + 2 < NPACKS:
                        second.append(lambda p=p: rotate(g, 1, p + 2))
                invert(g, 0, ch, second)
                invert(g, 1, ch, [None] * 3 + [lambda: sum_squares(g + 1)] + [None] * 25 + [lambda: normalise(g + 1)]
                       if more else [])
                gated(g, 0)
                for q in range(1, NQ):
                    for h in range(HALF):
                        rest(g, q, h)
                gated(g, 1)
                dve.wait_ge(s["y_ready"], g + 1)
                norm.add(dve, ch, g, 0, ps[:, 3, 0:D])
                norm.moments(dve, ch, g)
                norm.apply(dve, ch, g)
                ch.end()

            sum_squares(0)
            normalise(0)
            with dve.Fori(0, B - 1) as g:
                turn(g, True)
            turn(B - 1, False)
    sem.release()


def experts_stage(k, stage):
    nc, ps, w, A = k.nc, k.psum, k.begin(stage), k.arena
    gated = stage == "L3_ffn"
    routed = w.wg.shape[2]
    E = k.dram["experts_" + stage].shape[0]
    FC = 1 if gated else 1024 // P
    sem = Semaphores(nc, stage)
    turned = Turned(k, sem, k.X, 4)
    norm = Norm(k, sem, k.X, k.X)
    logits_ready, combine_ready = sem("logits_ready"), sem("combine_ready")
    shifted, scores_ready = sem("logits_shifted"), sem("scores_ready")
    combineT_turned, combineT_ready, start_ready = sem("combineT_turned"), sem("combineT_ready"), sem("start_ready")
    arrived = [sem(f"expert_arrived_{s}") for s in range(2)]
    up_ready, silu_ready, h_ready = sem("up_ready"), sem("silu_ready"), sem("h_ready")
    y_ready, accumulated, dve_chain = sem("y_ready"), sem("accumulated"), sem("dve_chain")
    ones_set = sem("ones_set")

    words = k.dram["experts_" + stage].shape[2]
    xT = A(TURNS, C, N)
    ew = A(2, words)
    h = A(2, FC, N)
    sg = A(2, N) if gated else None
    comb = A(B, E)
    comb_now = A(2, B)
    combT = None if gated else A(B * P, rows=P)
    router = Router(k, w, routed, comb)
    ones = A(P)
    acc = k.Y
    F = FC * P

    def weights(s):
        a, at = ew[:, s, :], 0
        out = {}
        for name, shape in ([("w1", (C, F)), ("w3", (C, F)), ("w2", (FC, D))] if gated else
                            [("w1", (C, F)), ("w2", (FC, D)), ("b1", (FC,))]):
            n = int(np.prod(shape))
            out[name] = a[:, at:at + n] if len(shape) == 1 else a[:, at:at + n].rearrange("p (a b) -> p a b", b=shape[1])
            at += n
        return out

    W = [weights(0), weights(1)]
    STEPS = 2 * TURNS
    lg = ps[:, 0, 0:B * routed].rearrange("p (b e) -> p b e", e=routed)

    with nc.Block() as block:
        @block.sync
        def _(sp):
            def load(e, s):
                one = k.dram["experts_" + stage][bass.ds(e, 1), :, :].rearrange("a p n -> p (a n)")
                sp.dma_start(ew[:, s, :], one).then_inc(arrived[s], 16)
            load(0, 0)
            load(1, 1)
            k.prefetch(sp, stage)
            with sp.Fori(1, E // 2) as i:
                for s in range(2):
                    sp.wait_ge(y_ready, STEPS * i - TURNS + TURNS * s)
                    load(2 * i + s, s)

        @block.gpsimd
        def _(pool):
            k.wait_weights(pool, stage)
            pool.memset(ones[:, :], 1.0).then_inc(ones_set, 1)
            turned.stage(pool, 0)
            for g in range(TURNS - 1):
                turned.stage_next(pool, g)
            for g in range(TURNS):
                norm.roots(pool, g)

        @block.tensor
        def _(pe):
            k.wait_weights(pe, stage)
            pe.wait_ge(ones_set, 1)
            for g in range(TURNS):
                if g:
                    pe.wait_ge(turned.ready, g * C)
                turned.turn(pe, g)
            pe.wait_ge(turned.ready, TURNS * C)
            for b in range(B):
                g, u = divmod(b, TILES)
                for c in range(C):
                    mm = nc.tensor.matmul(lg[:, b, :], xT[:, g, c, u * P:(u + 1) * P], w.wg[:, c, :],
                                          start=(c == 0), stop=(gated and c == C - 1))
                if not gated:
                    mm = nc.tensor.matmul(lg[:, b, :], ones[0:1, :], w.bg[0:1, :], start=False, stop=True)
            mm.then_inc(logits_ready, 1)
            if not gated:
                pe.wait_ge(combine_ready, 1)
                for b in range(B):
                    mm = nc.tensor.transpose(ps[0:E, 4 + b // TILES, (b % TILES) * P:(b % TILES + 1) * P],
                                             comb[:, b, :], k.ident[:, :])
                mm.then_inc(combineT_turned, 1)
                pe.wait_ge(combineT_ready, 1)
                for half in range(2):
                    if half:
                        pe.wait_ge(accumulated, 1)
                    for j in range(B // 2):
                        b = half * B // 2 + j
                        mm = nc.tensor.matmul(ps[:, j // 2, (j % 2) * D:(j % 2 + 1) * D], combT[0:E, b * P:(b + 1) * P],
                                              w.b2[0:E, :], start=True, stop=True)
                    mm.then_inc(start_ready, 1)

            with pe.Fori(0, E // 2) as i:
                def up(m):
                    n = i * STEPS + m
                    s, g = divmod(m, TURNS)
                    if g == 0:
                        pe.wait_ge(arrived[s], 16 * (i + 1))
                    if m == 0:
                        pe.wait_ge(accumulated, n + 2)
                    for f in range(FC):
                        for part, name in enumerate(("w1", "w3") if gated else ("w1",)):
                            if gated:
                                bank = 2 * (m % 2) + part
                                if part == 0 and m >= 2:
                                    pe.wait_ge(h_ready, n - 1)
                            else:
                                bank = f % 4
                                if m or f >= 4:
                                    pe.wait_ge(h_ready, n * FC + f - 3)
                            for c in range(C):
                                mm = nc.tensor.matmul(ps[:, bank, :], W[s][name][:, c, f * P:(f + 1) * P], xT[:, g, c, :],
                                                      start=(c == 0), stop=(c == C - 1))
                        mm.then_inc(up_ready, 1)

                def down(m):
                    n = i * STEPS + m
                    s = m // TURNS
                    pe.wait_ge(h_ready, (n + 1) * FC)
                    pe.wait_ge(accumulated, n + 1)
                    for u in range(TILES):
                        out = ps[:, 4 + 2 * (m % 2) + u // 2, (u % 2) * D:(u % 2 + 1) * D]
                        for f in range(FC):
                            mm = nc.tensor.matmul(out, h[:, m % 2, f, u * P:(u + 1) * P], W[s]["w2"][:, f, :],
                                                  start=(f == 0), stop=(f == FC - 1))
                    mm.then_inc(y_ready, 1)

                for m in range(STEPS):
                    up(m)
                    if m:
                        down(m - 1)
                down(STEPS - 1)

        @block.scalar
        def _(act):
            k.wait_weights(act, stage)
            for g in range(TURNS):
                turned.copy(act, g, xT[:, g, :, :])
            if gated:
                act.wait_ge(logits_ready, 1)
                nc.scalar.activation(router.scores, lg, ACT.Sigmoid).then_inc(scores_ready, 1)
            else:
                act.wait_ge(shifted, 1)
                nc.scalar.activation(router.scores, router.scores, ACT.Exp).then_inc(scores_ready, 1)
                act.wait_ge(combineT_turned, 1)
                nc.scalar.copy(combT[0:E, :], ps[0:E, 4:8, :].rearrange("p a b -> p (a b)")).then_inc(combineT_ready, 1)
            with act.Fori(0, E // 2) as i:
                for m in range(STEPS):
                    n = i * STEPS + m
                    s = m // TURNS
                    for f in range(FC):
                        act.wait_ge(up_ready, n * FC + f + 1)
                        if gated:
                            nc.scalar.activation(sg[:, m % 2, :], ps[:, 2 * (m % 2), :], ACT.Silu).then_inc(silu_ready, 1)
                        else:
                            if m >= 2 and f == 0:
                                act.wait_ge(y_ready, n - 1)
                            nc.scalar.activation(h[:, m % 2, f, :], ps[:, f % 4, :], ACT.Silu,
                                                 bias=W[s]["b1"][:, f:f + 1]).then_inc(h_ready, 1)

        @block.vector
        def _(dve):
            k.wait_weights(dve, stage)
            chain = Chain(dve, dve_chain)
            norm.open(dve)
            if gated:
                dve.wait_ge(scores_ready, 1)
                router.grouped(dve, chain).then_inc(combine_ready, 1)
            else:
                dve.wait_ge(logits_ready, 1)
                router.top1(dve, chain, lg).then_inc(shifted, 1)
                dve.wait_ge(scores_ready, 1)
                router.top1_weight(dve, chain).then_inc(combine_ready, 1)
            dve.wait_ge(combine_ready, 1)
            if gated:
                dve.memset(acc[:, :, :], 0.0).then_inc(accumulated, 2)
                dve.wait_ge(accumulated, 2)
            else:
                for half in range(2):
                    dve.wait_ge(start_ready, half + 1)
                    dve.tensor_copy(acc[:, half * B // 2:(half + 1) * B // 2, :],
                                    ps[:, 0:4, :].rearrange("p a (b d) -> p (a b) d", d=D)).then_inc(accumulated, 1)
                dve.wait_ge(accumulated, 2)

            def experts(i, last=False):
                def accumulate(m):
                    n = i * STEPS + m
                    s, g = divmod(m, TURNS)
                    dve.wait_ge(y_ready, n + 1)
                    dve.wait_ge(accumulated, n + 2)
                    for u in range(TILES):
                        b = g * TILES + u
                        a = dve.scalar_tensor_tensor(
                            out=acc[:, b, :], in0=ps[:, 4 + 2 * (m % 2) + u // 2, (u % 2) * D:(u % 2 + 1) * D],
                            scalar=comb_now[:, s, b:b + 1], in1=acc[:, b, :], op0=ALU.mult, op1=ALU.add)
                    a.then_inc(accumulated, 1)
                    if last and s:
                        if g:
                            norm.apply(dve, chain, g - 1)
                        dve.wait_ge(accumulated, n + 3)
                        for u in range(TILES):
                            norm.add(dve, chain, g, u, acc[:, g * TILES + u, :])
                        norm.moments(dve, chain, g)

                dve.wait_ge(accumulated, STEPS * i + 2)
                dve.tensor_copy(comb_now[:, :, :], comb[:, :, bass.ds(2 * i, 2)].rearrange("p b s -> p s b")
                                ).then_inc(combine_ready, 1)
                dve.wait_ge(combine_ready, i + 2)
                for m in range(STEPS):
                    n = i * STEPS + m
                    if gated:
                        dve.wait_ge(silu_ready, n + 1)
                        if m >= 2:
                            dve.wait_ge(y_ready, n - 1)
                        dve.tensor_tensor(h[:, m % 2, 0, :], sg[:, m % 2, :], ps[:, 2 * (m % 2) + 1, :], ALU.mult
                                          ).then_inc(h_ready, 1)
                    if m:
                        accumulate(m - 1)
                accumulate(STEPS - 1)

            with dve.Fori(0, E // 2 - 1) as i:
                experts(i)
            experts(E // 2 - 1, last=True)
            norm.apply(dve, chain, TURNS - 1)
    sem.release()


def rank(dve, chain, out, s, n, before, tmp, tmp2):
    i_ = bc(s, 3, n)
    j_ = bc(s, 2, n)
    chain(dve.tensor_tensor(tmp, j_, i_, ALU.is_gt))
    chain(dve.tensor_tensor(tmp2, j_, i_, ALU.is_equal))
    chain(dve.tensor_tensor(tmp2, tmp2, bc(before, 1, B), ALU.mult))
    chain(dve.tensor_tensor(tmp, tmp, tmp2, ALU.add))
    chain(dve.tensor_reduce(out, tmp, AX.X, ALU.add))


class Router:

    def __init__(self, k, w, n, comb):
        self.w, self.n, self.comb, A = w, n, comb, k.arena
        self.scores, self.masked, self.place = A(B, n), A(B, n), A(B, n)
        self.t1, self.t2 = A(B, n, n), A(B, n, n)
        self.a, self.b, self.c = A(B * 4), A(B * 4), A(B * 4)

    def top1(self, dve, chain, logits):
        chain(dve.tensor_reduce(self.a[:, 0:B], logits, AX.X, ALU.max))
        chain(dve.tensor_tensor(self.scores, logits, bc(self.a[:, 0:B], 2, self.n), ALU.subtract))
        rank(dve, chain, self.place, self.scores, self.n, self.w.before, self.t1, self.t2)
        return dve.tensor_scalar(self.comb, self.place, 0.5, None, ALU.is_lt)

    def top1_weight(self, dve, chain):
        chain(dve.tensor_reduce(self.a[:, 0:B], self.scores, AX.X, ALU.add))
        chain(dve.reciprocal(self.b[:, 0:B], self.a[:, 0:B]))
        return dve.tensor_tensor(self.comb, self.comb, bc(self.b[:, 0:B], 2, self.n), ALU.mult)

    def grouped(self, dve, chain):
        G, J = 4, self.n // 4
        s = self.scores.rearrange("p b (g j) -> p (b g) j", j=J)
        q = [s[:, :, j] for j in range(J)]
        a, b, c = self.a, self.b, self.c
        t = self.t1.rearrange("p b i j -> p (b i j)")[:, 0:B * G]
        chain(dve.tensor_tensor(a, q[0], q[1], ALU.max))
        chain(dve.tensor_tensor(b, q[0], q[1], ALU.min))
        chain(dve.tensor_tensor(c, q[2], q[3], ALU.max))
        chain(dve.tensor_tensor(t, q[2], q[3], ALU.min))
        chain(dve.tensor_tensor(b, b, t, ALU.max))
        chain(dve.tensor_tensor(t, a, c, ALU.min))
        chain(dve.tensor_tensor(b, b, t, ALU.max))
        chain(dve.tensor_tensor(a, a, c, ALU.max))
        chain(dve.tensor_tensor(a, a, b, ALU.add))
        small = [x.rearrange("p b i j -> p (b i j)")[:, 0:B * G * G].rearrange("p (b i j) -> p b i j", i=G, j=G)
                 for x in (self.t1, self.t2)]
        rank(dve, chain, b.rearrange("p (b g) -> p b g", g=G), a.rearrange("p (b g) -> p b g", g=G), G,
             self.w.before[:, 0:G, 0:G], *small)
        chain(dve.tensor_scalar(a, b, 1.5, None, ALU.is_lt))
        chain(dve.tensor_scalar(b, a, 1.0, None, ALU.subtract))
        m = self.masked.rearrange("p b (g j) -> p (b g) j", j=J)
        chain(dve.tensor_tensor(m, s, bc(a, 2, J), ALU.mult))
        chain(dve.tensor_tensor(m, m, bc(b, 2, J), ALU.add))
        rank(dve, chain, self.place, self.masked, self.n, self.w.before, self.t1, self.t2)
        chain(dve.tensor_scalar(self.place, self.place, 3.5, None, ALU.is_lt))
        chain(dve.tensor_tensor(self.masked, self.scores, self.place, ALU.mult))
        chain(dve.tensor_reduce(a[:, 0:B], self.masked, AX.X, ALU.add))
        chain(dve.tensor_scalar(a[:, 0:B], a[:, 0:B], 1e-6, None, ALU.add))
        chain(dve.reciprocal(b[:, 0:B], a[:, 0:B]))
        chain(dve.tensor_tensor(self.comb[:, :, 0:self.n], self.masked, bc(b[:, 0:B], 2, self.n), ALU.mult))
        return dve.memset(self.comb[:, :, self.n:], 1.0)


def linear_attention_stage(k):
    stage = "L0_xattn"
    nc, ps, w, A = k.nc, k.psum, k.begin(stage), k.arena
    sem = Semaphores(nc, stage)
    turned, norm, biased = Turned(k, sem, k.X, 4), Norm(k, sem, k.X, k.X), Biased(k, sem, k.X, w.bo)
    xT = turned.xT
    QS, KS = C * TILES, TILES * H
    ones_set, loaded, mask_loaded, keep_ready = sem("ones_set"), sem("loaded"), sem("mask_loaded"), sem("keep_ready")
    qk_projected, v_projected, v_ready = sem("qk_projected"), sem("v_projected"), sem("v_ready")
    clipped, exp_ready = sem("clipped"), sem("exp_ready")
    squares_ready, roots_ready, scaled = sem("squares_ready"), sem("roots_ready"), sem("scaled")
    kv_ready, kv_masked, oT_ready, oT_copied = sem("kv_ready"), sem("kv_masked"), sem("oT_ready"), sem("oT_copied")
    y_ready, dve_chain = sem("y_ready"), sem("dve_chain")
    ones, cT = A(P), A(C, N)
    low, high = A(4, N), A(4, N)
    v = A(TILES, D)
    squares, exponent = A(QS + KS), A(QS + KS)
    kv, oT = A(TILES * C, P), A(TILES * C, P)
    pad, keep = A(B, dtype=U8), A(B)
    kv_psum = ps[:, 4:6, :].rearrange("p a (b e) -> p (a b) e", e=P)
    oT_psum = kv_psum

    with nc.Block() as block:
        @block.sync
        def _(sp):
            sp.dma_start(pad, k.dram["padding"]).then_inc(mask_loaded, 16)
            sp.dma_start(cT[:, :, :], k.ctxT[0]).then_inc(loaded, 16)
            k.prefetch(sp, stage)
            with sp.Fori(1, TURNS) as g:
                sp.wait_ge(v_projected, g * 2)
                sp.dma_start(cT[:, :, :], k.ctxT[bass.ds(g, 1)].rearrange("a p c n -> p (a c) n")).then_inc(loaded, 16)

        @block.gpsimd
        def _(pool):
            pool.memset(ones, 1.0).then_inc(ones_set, 1)
            pool.memset(exponent, -0.5).then_inc(ones_set, 1)
            pool.wait_ge(ones_set, 2)
            k.wait_weights(pool, stage)
            turned.stage(pool, 0)
            biased.stage(pool, 0)

            def roots(g):
                pool.wait_ge(squares_ready, g + 1)
                pool.tensor_tensor(squares, squares, exponent, ALU.pow).then_inc(roots_ready, 1)

            with pool.Fori(0, TURNS - 1) as g:
                turned.stage_next(pool, g)
                roots(g)
                norm.roots(pool, g)
                biased.stage(pool, g + 1)
            roots(TURNS - 1)
            norm.roots(pool, TURNS - 1)

        @block.tensor
        def _(pe):
            k.wait_weights(pe, stage)
            pe.wait_ge(ones_set, 1)

            def project(g):
                turned.turn(pe, g)
                pe.wait_ge(turned.ready, (g + 1) * C)
                for co in range(C):
                    for ci in range(C):
                        mm = nc.tensor.matmul(ps[:, co, :], w.wq[:, ci, co * P:(co + 1) * P], xT[:, ci, :],
                                              start=(ci == 0), stop=(ci == C - 1))
                    mm.then_inc(qk_projected, 1)
                pe.wait_ge(loaded, 16 * (g + 1))
                for m, b, bank, done in ((w.wk, w.bk, 2, qk_projected), (w.wv, w.bv, 6, v_projected)):
                    for u in range(TILES):
                        out = ps[:, bank + u // 2, (u % 2) * D:(u % 2 + 1) * D]
                        for ci in range(C):
                            nc.tensor.matmul(out, cT[:, ci, u * P:(u + 1) * P], m[:, ci, :], start=(ci == 0), stop=False)
                        mm = nc.tensor.matmul(out, ones[0:1, :], b[0:1, :], start=False, stop=True)
                        if u % 2:
                            mm.then_inc(done, 1)

            def attend(g, more):
                if more:
                    pe.wait_ge(exp_ready, (g + 1) * 4)
                    pe.wait_ge(v_ready, (g + 1) * 2)
                    norm.wait_added(pe, g * TILES)
                    project(g + 1)
                pe.wait_ge(scaled, (g + 1) * 2)
                pe.wait_ge(v_ready, (g + 1) * 2)
                for u in range(TILES):
                    for c in range(C):
                        mm = nc.tensor.matmul(kv_psum[:, u * C + c, :],
                                              low[:, 2 + u // 2, (u % 2) * D + c * P:(u % 2) * D + (c + 1) * P],
                                              v[:, u, c * P:(c + 1) * P], start=True, stop=True)
                mm.then_inc(kv_ready, 1)
                pe.wait_ge(kv_masked, g + 1)
                for u in range(TILES):
                    for c in range(C):
                        mm = nc.tensor.matmul(oT_psum[:, u * C + c, :], kv[:, u * C + c, :],
                                              low[:, c, u * P:(u + 1) * P], start=True, stop=True)
                mm.then_inc(oT_ready, 1)
                pe.wait_ge(oT_copied, g + 1)
                for u in range(TILES):
                    out = ps[:, 4 + u // 2, (u % 2) * D:(u % 2 + 1) * D]
                    for c in range(C):
                        mm = nc.tensor.matmul(out, oT[:, u * C + c, :], w.wo[:, c, :], start=(c == 0), stop=(c == C - 1))
                mm.then_inc(y_ready, 1)

            project(0)
            with pe.Fori(0, TURNS - 1) as g:
                attend(g, True)
            attend(TURNS - 1, False)

        @block.scalar
        def _(act):
            k.wait_weights(act, stage)

            def turn(g, more):
                for i in range(4):
                    act.wait_ge(clipped, g * 4 + i + 1)
                    bias = w.bq[:, i:i + 1] if i < C else 0.0
                    nc.scalar.activation(high[:, i, :], ps[:, i, :], ACT.Relu, bias=bias)
                    nc.scalar.activation(low[:, i, :], low[:, i, :], ACT.Exp).then_inc(exp_ready, 1)
                for i in range(2):
                    act.wait_ge(v_projected, g * 2 + i + 1)
                    nc.scalar.copy(v[:, 2 * i:2 * i + 2, :], ps[:, 6 + i, :].rearrange("p (u d) -> p u d", d=D)
                                   ).then_inc(v_ready, 1)
                if more:
                    turned.copy(act, g + 1)
                act.wait_ge(oT_ready, g + 1)
                nc.scalar.copy(oT[:, :, :], oT_psum).then_inc(oT_copied, 1)

            turned.copy(act, 0)
            with act.Fori(0, TURNS - 1) as g:
                turn(g, True)
            turn(TURNS - 1, False)

        @block.vector
        def _(dve):
            k.wait_weights(dve, stage)
            norm.open(dve)
            dve.wait_ge(mask_loaded, 16)
            dve.tensor_scalar(keep, pad, -1.0, 1.0, ALU.mult, ALU.add).then_inc(keep_ready, 1)
            dve.wait_ge(keep_ready, 1)
            with dve.Fori(0, TURNS) as g:
                chain = Chain(dve, dve_chain, g, 3 * 4 + 1 + norm.chained())
                for i in range(4):
                    dve.wait_ge(qk_projected, g * 4 + i + 1)
                    bias = w.bq[:, i:i + 1] if i < C else 0.0
                    dve.tensor_scalar(low[:, i, :], ps[:, i, :], bias, 0.0, ALU.add, ALU.min).then_inc(clipped, 1)
                for i in range(4):
                    dve.wait_ge(exp_ready, g * 4 + i + 1)
                    chain(dve.tensor_tensor(low[:, i, :], low[:, i, :], high[:, i, :], ALU.add))
                    chain(dve.tensor_tensor(high[:, i, :], low[:, i, :], low[:, i, :], ALU.mult))
                    if i < C:
                        chain(dve.tensor_reduce(squares[:, i * TILES:(i + 1) * TILES],
                                                high[:, i, :].rearrange("p (u t) -> p u t", t=P), AX.X, ALU.add))
                    else:
                        at = QS + (i - C) * 2 * H
                        chain(dve.tensor_reduce(squares[:, at:at + 2 * H],
                                                high[:, i, :].rearrange("p (h e) -> p h e", e=DH), AX.X, ALU.add))
                dve.tensor_scalar(squares, squares, 1e-24, None, ALU.max).then_inc(squares_ready, 1)
                dve.wait_ge(roots_ready, g + 1)
                kq = squares[:, QS:].rearrange("p (u h) -> p u h", h=H)
                chain(dve.tensor_tensor(kq, kq, bc(keep[:, bass.ds(g * TILES, TILES)], 2, H), ALU.mult))
                q = low[:, 0:C, :].rearrange("p c (u t) -> p (c u) t", t=P)
                dve.tensor_tensor(q, q, bc(squares[:, 0:QS], 2, P), ALU.mult).then_inc(scaled, 1)
                kk = low[:, 2:4, :].rearrange("p a (h e) -> p (a h) e", e=DH)
                dve.tensor_tensor(kk, kk, bc(squares[:, QS:], 2, DH), ALU.mult).then_inc(scaled, 1)
                dve.wait_ge(kv_ready, g + 1)
                dve.tensor_tensor(kv[:, :, :], kv_psum, bc(w.blocks, 1, TILES * C), ALU.mult).then_inc(kv_masked, 1)
                dve.wait_ge(y_ready, g + 1)
                for u in range(TILES):
                    norm.add(dve, chain, g, u, ps[:, 4 + u // 2, (u % 2) * D:(u % 2 + 1) * D], x=biased.tile(dve, g, u))
                norm.moments(dve, chain, g)
                norm.apply(dve, chain, g)
                chain.end()
    sem.release()


def recall_stage(k):
    stage = "L2_recall"
    nc, ps, w, A = k.nc, k.psum, k.begin(stage), k.arena
    sem = Semaphores(nc, stage)
    turned = Turned(k, sem, k.X, 4)
    xT = turned.xT
    loaded, q_projected, q_ready = sem("loaded"), sem("q_projected"), sem("q_ready")
    kv_projected, kv_ready, scores_ready, chosen = sem("kv_projected"), sem("kv_ready"), sem("scores_ready"), sem("chosen")
    chosen_turned, chosenT_ready, recalled, stored = sem("chosen_turned"), sem("chosenT_ready"), sem("recalled"), sem("stored")
    dve_chain = sem("dve_chain")
    R = P + DH
    cT, qT = A(C, N), A(C, N)
    kvp = A(TILES, R)
    best, one, oneT = A(TILES), A(TILES, P), A(TILES, P)
    s_psum = ps[:, 6, :].rearrange("p (u t) -> p u t", t=P)
    oneT_psum = ps[:, 7, :].rearrange("p (u t) -> p u t", t=P)

    with nc.Block() as block:
        @block.sync
        def _(sp):
            sp.dma_start(cT[:, :, :], k.ctxT[0]).then_inc(loaded, 16)
            k.prefetch(sp, stage)
            with sp.Fori(1, TURNS) as g:
                sp.wait_ge(scores_ready, g)
                sp.dma_start(cT[:, :, :], k.ctxT[bass.ds(g, 1)].rearrange("a p c n -> p (a c) n")).then_inc(loaded, 16)

        @block.gpsimd
        def _(pool):
            turned.stage(pool, 0)
            with pool.Fori(0, TURNS - 1) as g:
                turned.stage_next(pool, g)

        @block.tensor
        def _(pe):
            k.wait_weights(pe, stage)
            with pe.Fori(0, TURNS) as g:
                turned.turn(pe, g)
                pe.wait_ge(turned.ready, (g + 1) * C)
                for co in range(C):
                    for ci in range(C):
                        mm = nc.tensor.matmul(ps[:, co, :], w.wq[:, ci, co * P:(co + 1) * P], xT[:, ci, :],
                                              start=(ci == 0), stop=(ci == C - 1))
                    mm.then_inc(q_projected, 1)
                pe.wait_ge(loaded, 16 * (g + 1))
                for u in range(TILES):
                    for ci in range(C):
                        mm = nc.tensor.matmul(ps[:, 2 + u // 2, (u % 2) * D:(u % 2) * D + R],
                                              cT[:, ci, u * P:(u + 1) * P], w.wkv[:, ci, :],
                                              start=(ci == 0), stop=(ci == C - 1))
                    if u % 2:
                        mm.then_inc(kv_projected, 1)
                pe.wait_ge(q_ready, (g + 1) * C)
                for u in range(TILES):
                    for ci in range(C):
                        mm = nc.tensor.matmul(s_psum[:, u, :], qT[:, ci, u * P:(u + 1) * P], cT[:, ci, u * P:(u + 1) * P],
                                              start=(ci == 0), stop=(ci == C - 1))
                mm.then_inc(scores_ready, 1)
                pe.wait_ge(chosen, g + 1)
                for u in range(TILES):
                    mm = nc.tensor.transpose(oneT_psum[:, u, :], one[:, u, :], k.ident)
                mm.then_inc(chosen_turned, 1)
                pe.wait_ge(chosenT_ready, g + 1)
                pe.wait_ge(kv_ready, (g + 1) * 2)
                for u in range(TILES):
                    nc.tensor.matmul(ps[:, 0, u * P:(u + 1) * P], kvp[:, u, 0:P], oneT[:, u, :], start=True, stop=True)
                    mm = nc.tensor.matmul(ps[:, 1, u * DH:(u + 1) * DH], oneT[:, u, :], kvp[:, u, P:R], start=True, stop=True)
                mm.then_inc(recalled, 1)
                pe.wait_ge(stored, g + 1)

        @block.scalar
        def _(act):
            with act.Fori(0, TURNS) as g:
                turned.copy(act, g)
                for c in range(C):
                    act.wait_ge(q_projected, g * C + c + 1)
                    nc.scalar.copy(qT[:, c, :], ps[:, c, :]).then_inc(q_ready, 1)
                for i in range(2):
                    act.wait_ge(kv_projected, g * 2 + i + 1)
                    nc.scalar.copy(kvp[:, 2 * i:2 * i + 2, :], ps[:, 2 + i, :].rearrange("p (u d) -> p u d", d=D)[:, :, 0:R]
                                   ).then_inc(kv_ready, 1)
                act.wait_ge(chosen_turned, g + 1)
                nc.scalar.copy(oneT[:, :, :], oneT_psum).then_inc(chosenT_ready, 1)

        @block.vector
        def _(dve):
            k.wait_weights(dve, stage)
            chain = Chain(dve, dve_chain)
            chain(dve.memset(k.Y[:, :, P + DH:P + DH + 1], 1.0))
            with dve.Fori(0, TURNS) as g:
                ch = Chain(dve, dve_chain)
                ch.base = 1 + g * 5
                dve.wait_ge(scores_ready, g + 1)
                ch(dve.tensor_reduce(best, s_psum, AX.X, ALU.max))
                ch(dve.tensor_tensor(one[:, :, :], s_psum, bc(best, 2, P), ALU.is_equal))
                ch(dve.tensor_tensor(one[:, :, :], one[:, :, :], bc(w.countdown, 1, TILES), ALU.mult))
                ch(dve.tensor_reduce(best, one[:, :, :], AX.X, ALU.max))
                dve.tensor_tensor(one[:, :, :], one[:, :, :], bc(best, 2, P), ALU.is_equal).then_inc(chosen, 1)
                dve.wait_ge(recalled, g + 1)
                t = bass.ds(g * TILES, TILES)
                ch(dve.tensor_copy(k.Y[:, t, 0:P], ps[:, 0, :].rearrange("p (u t) -> p u t", t=P)))
                dve.tensor_copy(k.Y[:, t, P:P + DH], ps[:, 1, 0:TILES * DH].rearrange("p (u e) -> p u e", e=DH)
                                ).then_inc(stored, 1)
                assert ch.n == 5
    sem.release()


def correlation_stage(k):
    stage = "L2_attn"
    nc, ps, w, A = k.nc, k.psum, k.begin(stage), k.arena
    sem = Semaphores(nc, stage)
    PAIR = 2
    PAIRS = B // PAIR
    SL = PAIR * C
    FR = P // 2 + 1
    ROUNDS = P // 8
    norm = Norm(k, sem, k.X, k.X, tiles=PAIR)
    staged, x_turned, xT_ready, ones_set = sem("x_staged"), sem("x_turned"), sem("xT_ready"), sem("ones_set")
    qk_projected, qk_ready, v_projected, v_masked = sem("qk_projected"), sem("qk_ready"), sem("v_projected"), sem("v_masked")
    spectra_ready, k_copied, product_ready = sem("spectra_ready"), sem("k_copied"), sem("product_ready")
    corr_ready, corr_copied, shifted, exp_ready = sem("corr_ready"), sem("corr_copied"), sem("shifted"), sem("exp_ready")
    weights_ready, oT_ready, oT_copied, y_ready = sem("weights_ready"), sem("oT_ready"), sem("oT_copied"), sem("y_ready")
    dve_chain, product_chain, norm_chain = sem("dve_chain"), sem("product_chain"), sem("norm_chain")
    xs, xT = A(PAIR, D), A(C, PAIR * P)
    ones = A(P)
    q, kk = A(PAIR * D), A(PAIR * D)
    vb = A(PAIR, C, P)
    kspec = A(2, N)
    t1, t2, re, im = A(N), A(N), A(N), A(N)
    unsorted, ranked = A(SL, P), A(SL, P)
    total, oT, spare = A(SL), A(SL, P), A(2 * ROUNDS + 5)
    xfirst = A(C, PAIR, HH, DH)

    with nc.Block() as block:
        @block.sync
        def _(sp):
            k.prefetch(sp, stage)

        @block.gpsimd
        def _(pool):
            pool.memset(ones, 1.0).then_inc(ones_set, 1)

            def stage_x(g):
                pool.tensor_copy(xs[:, :, :], k.X[:, bass.ds(g * PAIR, PAIR), :]).then_inc(staged, 1)

            stage_x(0)
            with pool.Fori(0, PAIRS - 1) as g:
                pool.wait_ge(x_turned, g + 1)
                stage_x(g + 1)
                norm.roots(pool, g)
            norm.roots(pool, PAIRS - 1)

        @block.tensor
        def _(pe):
            k.wait_weights(pe, stage)
            pe.wait_ge(ones_set, 1)

            def spectra(g, drained=None):
                pe.wait_ge(staged, g + 1)
                if not (isinstance(g, int) and g == 0):
                    pe.wait_ge(corr_copied, g)
                for c in range(C):
                    for u in range(PAIR):
                        mm = nc.tensor.transpose(ps[:, 0, c * PAIR * P + u * P:c * PAIR * P + (u + 1) * P],
                                                 xs[:, u, c * P:(c + 1) * P], k.ident)
                mm.then_inc(x_turned, 1)
                pe.wait_ge(xT_ready, (g + 1) * 2)
                for i, (m, b) in enumerate(((w.wq, w.bq), (w.wk, w.bk))):
                    if i and drained is not None:
                        norm.wait_added(pe, drained)
                    for u in range(PAIR):
                        out = ps[:, 1 + i, u * D:(u + 1) * D]
                        for ci in range(C):
                            nc.tensor.matmul(out, xT[:, ci, u * P:(u + 1) * P], m[:, ci, :], start=(ci == 0), stop=False)
                        mm = nc.tensor.matmul(out, ones[0:1, :], b[0:1, :], start=False, stop=True)
                    mm.then_inc(qk_projected, 1)
                if not (isinstance(g, int) and g == 0):
                    pe.wait_ge(v_masked, g)
                for u in range(PAIR):
                    out = ps[:, 3, u * D:(u + 1) * D]
                    for ci in range(C):
                        nc.tensor.matmul(out, xfirst[:, ci, u, :, :].rearrange("p h e -> p (h e)"), w.wv[:, ci, :],
                                         start=(ci == 0), stop=False)
                    mm = nc.tensor.matmul(out, ones[0:1, :], w.bv[0:1, :], start=False, stop=True)
                mm.then_inc(v_projected, 1)
                pe.wait_ge(qk_ready, (g + 1) * 2)
                for i, x in enumerate((q, kk)):
                    for j, table in enumerate((w.dcos, w.dsin)):
                        mm = nc.tensor.matmul(ps[0:FR, 4 + 2 * i + j, :], table, x, start=True, stop=True)
                    mm.then_inc(spectra_ready, 1)

            def correlation(g):
                pe.wait_ge(product_ready, (g + 1) * 2)
                for u in range(PAIR):
                    for c in range(C):
                        at = u * D + c * P
                        out = ps[:, 0, (u * C + c) * P:(u * C + c + 1) * P]
                        nc.tensor.matmul(out, re[0:FR, at:at + P], w.icos[0:FR, :], start=True, stop=False)
                        mm = nc.tensor.matmul(out, im[0:FR, at:at + P], w.isin[0:FR, :], start=False, stop=True)
                mm.then_inc(corr_ready, 1)

            def output(g):
                pe.wait_ge(weights_ready, g + 1)
                pe.wait_ge(v_masked, g + 1)
                for u in range(PAIR):
                    for c in range(C):
                        s = u * C + c
                        mm = nc.tensor.matmul(ps[:, 1, s * P:(s + 1) * P], vb[:, u, c, :], ranked[:, s, :],
                                              start=True, stop=True)
                mm.then_inc(oT_ready, 1)
                pe.wait_ge(oT_copied, g + 1)
                for u in range(PAIR):
                    out = ps[:, 2, u * D:(u + 1) * D]
                    for c in range(C):
                        nc.tensor.matmul(out, oT[:, u * C + c, :], w.wo[:, c, :], start=(c == 0), stop=False)
                    mm = nc.tensor.matmul(out, ones[0:1, :], w.bo[0:1, :], start=False, stop=True)
                mm.then_inc(y_ready, 1)

            spectra(0)
            correlation(0)
            spectra(1)
            correlation(1)
            output(0)
            with pe.Fori(1, PAIRS - 1) as g:
                spectra(g + 1, g * PAIR)
                correlation(g + 1)
                output(g)
            norm.wait_added(pe, (PAIRS - 1) * PAIR)
            output(PAIRS - 1)

        @block.scalar
        def _(act):
            def spectra(g):
                act.wait_ge(x_turned, g + 1)
                turned = ps[:, 0, :].rearrange("p (c u t) -> p c u t", c=C, u=PAIR)
                nc.scalar.copy(xT[:, :, :], ps[:, 0, :].rearrange("p (c n) -> p c n", c=C)).then_inc(xT_ready, 1)
                for c in range(C):
                    a = nc.scalar.copy(xfirst[:, c, :, :, :], bc(turned[:, c, :, 0:DH], 2, HH))
                a.then_inc(xT_ready, 1)
                for i, to in enumerate((q, kk)):
                    act.wait_ge(qk_projected, g * 2 + i + 1)
                    nc.scalar.copy(to, ps[:, 1 + i, :]).then_inc(qk_ready, 1)
                act.wait_ge(spectra_ready, g * 2 + 2)
                nc.scalar.copy(kspec[0:FR, :, :], ps[0:FR, 6:8, :]).then_inc(k_copied, 1)

            def correlation(g):
                act.wait_ge(corr_ready, g + 1)
                nc.scalar.copy(unsorted[:, :, :], ps[:, 0, :].rearrange("p (s t) -> p s t", t=P)).then_inc(corr_copied, 1)

            def exponentials(g):
                act.wait_ge(shifted, g + 1)
                nc.scalar.activation(ranked[:, :, :], ranked[:, :, :], ACT.Exp).then_inc(exp_ready, 1)

            def output(g):
                act.wait_ge(oT_ready, g + 1)
                nc.scalar.copy(oT[:, :, :], ps[:, 1, :].rearrange("p (s t) -> p s t", t=P)).then_inc(oT_copied, 1)

            spectra(0)
            correlation(0)
            with act.Fori(0, PAIRS - 1) as g:
                spectra(g + 1)
                exponentials(g)
                correlation(g + 1)
                output(g)
            exponentials(PAIRS - 1)
            output(PAIRS - 1)

        @block.vector
        def _(dve):
            k.wait_weights(dve, stage)
            norm.open(dve)
            def mask_values(g):
                dve.wait_ge(v_projected, g + 1)
                dve.tensor_tensor(vb[:, :, :, :], ps[:, 3, :].rearrange("p (u c e) -> p u c e", c=C, e=P),
                                  bc(bc(w.blocks, 1, C), 1, PAIR), ALU.mult).then_inc(v_masked, 1)

            def product(g):
                ch = Chain(dve, product_chain, g, 4)
                dve.wait_ge(k_copied, g + 1)
                f = slice(0, FR)
                qc, qs, kc, ks = ps[f, 4, :], ps[f, 5, :], kspec[f, 0, :], kspec[f, 1, :]
                dve.tensor_tensor(t1[f], qc, kc, ALU.mult)
                ch(dve.tensor_tensor(t2[f], qs, ks, ALU.mult))
                dve.tensor_tensor(re[f], t1[f], t2[f], ALU.add).then_inc(product_ready, 1)
                dve.wait_ge(product_ready, 2 * g + 1)
                ch(dve.tensor_tensor(t1[f], qc, ks, ALU.mult))
                ch(dve.tensor_tensor(t2[f], qs, kc, ALU.mult))
                ch(dve.tensor_tensor(im[f], t1[f], t2[f], ALU.subtract))
                dve.tensor_copy(spare[f, 2 * ROUNDS:2 * ROUNDS + 1], im[f, 0:1]).then_inc(product_ready, 1)
                ch.end()

            def finish(g):
                chain = Chain(dve, norm_chain, g, norm.chained())
                dve.wait_ge(y_ready, g + 1)
                for u in range(PAIR):
                    norm.add(dve, chain, g, u, ps[:, 2, u * D:(u + 1) * D])
                norm.moments(dve, chain, g)

                def apply():
                    norm.apply(dve, chain, g)
                    chain.end()
                return apply

            def turn(g, before=None, more=True):
                chain = Chain(dve, dve_chain, g, 2 * ROUNDS - 1 + 3)
                dve.wait_ge(corr_copied, g + 1)
                if before is not None:
                    dve.wait_ge(oT_ready, before + 1)
                dve.tensor_copy(spare[:, 2 * ROUNDS - 1:2 * ROUNDS], unsorted[:, 0, 0:1])
                for r in range(ROUNDS):
                    for s in range(SL):
                        top = dve.max(ranked[:, s, 8 * r:8 * r + 8], unsorted[:, s, :])
                    chain(top)
                    dve.tensor_copy(spare[:, r:r + 1], ranked[:, SL - 1, 8 * r:8 * r + 1])
                    if r < ROUNDS - 1:
                        for s in range(SL):
                            left = dve.match_replace(unsorted[:, s, :], ranked[:, s, 8 * r:8 * r + 8],
                                                     unsorted[:, s, :], -3e38)
                        chain(left)
                        dve.tensor_copy(spare[:, ROUNDS + r:ROUNDS + r + 1], unsorted[:, SL - 1, 0:1])
                    if r == 2 and before is not None:
                        apply = finish(before)
                    if r == 4 and before is not None:
                        apply()
                        mask_values(g)
                    if r in (2, 4) and before is not None:
                        dve.tensor_copy(spare[:, 2 * ROUNDS + r:2 * ROUNDS + r + 1], ranked[:, 0, 0:1])
                chain(dve.tensor_copy(total, ranked[:, :, 0]))
                dve.tensor_tensor(ranked[:, :, :], ranked[:, :, :], bc(total, 2, P), ALU.subtract).then_inc(shifted, 1)
                if more:
                    product(g + 1)
                dve.wait_ge(exp_ready, g + 1)
                chain(dve.tensor_reduce(total, ranked[:, :, :], AX.X, ALU.add))
                chain(dve.reciprocal(total, total))
                dve.tensor_tensor(ranked[:, :, :], ranked[:, :, :], bc(total, 2, P), ALU.mult).then_inc(weights_ready, 1)
                chain.end()

            product(0)
            mask_values(0)
            turn(0)
            with dve.Fori(1, PAIRS - 1) as g:
                turn(g, g - 1)
            turn(PAIRS - 1, PAIRS - 2, False)
            finish(PAIRS - 1)()
    sem.release()

QMAX = 127.0
MAGIC = 1.5 * 2.0 ** 23
ABSMAX = bass.bass_isa.ReduceOp.absmax
SUM = bass.bass_isa.ReduceOp.add


def int8_ffn_stage(k):
    stage = "L1_ffn"
    nc, ps, w, A = k.nc, k.psum, k.begin(stage), k.arena
    sem = Semaphores(nc, stage)
    turned, norm = Turned(k, sem, k.X, 4), Norm(k, sem, k.X, k.X)
    IC = w.gate.shape[1]
    IP = w.down.shape[2] // IC
    ones_set, ident_ready = sem("ones_set"), sem("ident_ready")
    x_measured, x_max, clips = sem("x_measured"), sem("x_max"), sem("clips_ready")
    w_quantized, w_turned, wT_ready = sem("weights_quantized"), sem("weights_turned"), sem("weightsT_ready")
    scales_spread = sem("down_scales_spread")
    x_rounded, xq_ready = sem("x_rounded"), sem("xq_ready")
    up_ready, silu_ready, h_ready = sem("up_ready"), sem("silu_ready"), sem("h_ready")
    h_measured, h_max, h_rounded, hq_ready = sem("h_measured"), sem("h_max"), sem("h_rounded"), sem("hq_ready")
    y_ready, dve_chain, scale_ready = sem("y_ready"), sem("dve_chain"), sem("scale_ready")

    identb = A(P, dtype=BF16)
    ones = A(P)
    wmax, winv, wscale = A(3 * IC), A(3 * IC), A(3 * IC)
    wgT, wuT = A(C, IC * IP, dtype=BF16), A(C, IC * IP, dtype=BF16)
    wdT = A(IC, D, dtype=BF16)
    diag, down_scale = A(C, P), A(D)
    part, whole = A(4), A(4)
    sig, sx, sxi, sh, shi = A(2), A(1), A(1), A(1), A(1)
    sgate, sup = A(IC), A(IC)
    xr, xq = A(C, N), A(C, N, dtype=BF16)
    sg = A(2, N)
    h = A(IC, B * P)
    hw = h.rearrange("p a b -> p (a b)")
    wq = [hw[:, 0:IC * D // 2].bitcast(BF16).rearrange("p (a b) -> p a b", a=IC),
          hw[:, IC * D // 2:IC * D].bitcast(BF16).rearrange("p (a b) -> p a b", a=IC),
          hw[:, IC * D:IC * D + C * IC * IP // 2].bitcast(BF16).rearrange("p (a b) -> p a b", a=C)]
    hmax = A(TURNS)
    hq = A(IC, N, dtype=BF16)
    hr = k.Y.rearrange("p b d -> p (b d)").rearrange("p (a b) -> p a b", a=IC)
    wtmp = hr.rearrange("p a b -> p (a b)")[:, 0:IC * D].rearrange("p (a b) -> p a b", a=IC)

    def bank_bf16(b, n):
        return ps[:, b, :].bitcast(BF16)[:, 0:n]

    with nc.Block() as block:
        @block.sync
        def _(sp):
            k.prefetch(sp, stage)

        @block.gpsimd
        def _(pool):
            pool.memset(ones, 1.0).then_inc(ones_set, 1)
            pool.memset(part, 0.0).then_inc(ones_set, 1)
            turned.stage(pool, 0)
            pool.wait_ge(x_measured, 1)
            pool.partition_all_reduce(whole[:, 0:1], part[:, 0:1], P, ABSMAX).then_inc(x_max, 1)
            for g in range(TURNS - 1):
                turned.stage_next(pool, g)
            pool.wait_ge(h_measured, 1)
            pool.partition_all_reduce(whole[:, 1:2], part[:, 1:2], P, ABSMAX).then_inc(h_max, 1)
            with pool.Fori(0, TURNS) as g:
                norm.roots(pool, g)

        @block.tensor
        def _(pe):
            k.wait_weights(pe, stage)
            pe.wait_ge(ones_set, 2)
            pe.wait_ge(ident_ready, 1)
            for m in range(2):
                pe.wait_ge(w_quantized, m + 1)
                for c in range(C):
                    for i in range(IC):
                        mm = nc.tensor.transpose(bank_bf16(2 * m + c, IC * IP)[:, i * IP:(i + 1) * IP],
                                                 wq[m][0:IP, i, c * P:(c + 1) * P], identb[0:IP, 0:IP])
                mm.then_inc(w_turned, 1)
            pe.wait_ge(w_quantized, 3)
            for i in range(IC):
                for c in range(C):
                    mm = nc.tensor.transpose(bank_bf16(6 + i // 4, 4 * D)[0:IP, (i % 4) * D + c * P:(i % 4) * D + (c + 1) * P],
                                             wq[2][:, c, i * IP:(i + 1) * IP], identb[:, :])
            mm.then_inc(w_turned, 1)
            pe.wait_ge(wT_ready, 4)
            pe.wait_ge(scale_ready, 1)
            for c in range(C):
                mm = nc.tensor.matmul(ps[:, 6, c * P:(c + 1) * P], ones[:, :], diag[:, c, :], start=True, stop=True)
            mm.then_inc(scales_spread, 1)
            with pe.Fori(0, TURNS) as g:
                turned.turn(pe, g)
                pe.wait_ge(xq_ready, g + 1)
                for i in range(IC):
                    for part_, wT in enumerate((wgT, wuT)):
                        if i >= 2 and part_ == 0:
                            pe.wait_ge(h_ready, g * IC + i - 1)
                        for c in range(C):
                            mm = nc.tensor.matmul(ps[0:IP, 2 * (i % 2) + part_, :], wT[:, c, i * IP:(i + 1) * IP],
                                                  xq[:, c, :], start=(c == 0), stop=(c == C - 1))
                    mm.then_inc(up_ready, 1)
            pe.wait_ge(scale_ready, 2)
            with pe.Fori(0, TURNS) as g:
                pe.wait_ge(hq_ready, g + 1)
                for u in range(TILES):
                    norm.wait_added(pe, g * TILES + u - 1 if u >= 2 else g * TILES)
                    for i in range(IC):
                        mm = nc.tensor.matmul(ps[:, 4 + u % 2, 0:D], hq[0:IP, i, u * P:(u + 1) * P], wdT[0:IP, i, :],
                                              start=(i == 0), stop=(i == IC - 1))
                    mm.then_inc(y_ready, 1)

        @block.scalar
        def _(act):
            k.wait_weights(act, stage)
            nc.scalar.copy(identb[:, :], k.ident).then_inc(ident_ready, 1)
            nc.scalar.activation(sig, w.clip, ACT.Sigmoid).then_inc(clips, 1)
            for m, wT in enumerate((wgT, wuT)):
                act.wait_ge(w_turned, m + 1)
                for c in range(C):
                    a = nc.scalar.copy(wT[:, c, :], bank_bf16(2 * m + c, IC * IP))
                a.then_inc(wT_ready, 1)
            act.wait_ge(w_turned, 3)
            for b in range(2):
                nc.scalar.copy(wdT[0:IP, 4 * b:4 * b + 4, :], bank_bf16(6 + b, 4 * D)[0:IP, :].rearrange(
                    "p (i d) -> p i d", d=D)).then_inc(wT_ready, 1)
            act.wait_ge(scale_ready, 1)
            with act.Fori(0, TURNS) as g:
                act.wait_ge(x_rounded, g + 1)
                nc.scalar.activation(xq[:, :, :], xr[:, :, :], ACT.Copy, bias=-MAGIC).then_inc(xq_ready, 1)
                for i in range(IC):
                    act.wait_ge(up_ready, g * IC + i + 1)
                    nc.scalar.activation(sg[0:IP, i % 2, :], ps[0:IP, 2 * (i % 2), :], ACT.Silu,
                                         scale=sgate[0:IP, i:i + 1]).then_inc(silu_ready, 1)
            with act.Fori(0, TURNS) as g:
                act.wait_ge(h_rounded, g + 1)
                nc.scalar.activation(hq[0:IP, :, :], hr[0:IP, :, :], ACT.Copy, bias=-MAGIC).then_inc(hq_ready, 1)

        @block.vector
        def _(dve):
            k.wait_weights(dve, stage)
            chain = Chain(dve, dve_chain)
            norm.open(dve)
            dve.wait_ge(ones_set, 2)
            dve.tensor_reduce(part[:, 0:1], k.X.rearrange("p b d -> p (b d)"), AX.X, ALU.max,
                              apply_absolute_value=True).then_inc(x_measured, 1)
            rows = [(0, IP, w.gate[0:IP]), (IC, IP, w.up[0:IP]), (2 * IC, P, w.down)]
            for m, (at, n, a) in enumerate(rows):
                cols = a.shape[1]
                chain(dve.tensor_reduce(wmax[0:n, at:at + cols], a, AX.X, ALU.max, apply_absolute_value=True))
                chain(dve.tensor_scalar(wscale[0:n, at:at + cols], wmax[0:n, at:at + cols], 1.0 / QMAX, None, ALU.mult))
                chain(dve.reciprocal(winv[0:n, at:at + cols], wscale[0:n, at:at + cols]))
                tmp = (wtmp if m < 2 else hr.rearrange("p a b -> p (a b)")[:, 0:C * IC * IP].rearrange(
                    "p (a b) -> p a b", a=C))[0:n]
                chain(dve.tensor_tensor(tmp, a, bc(winv[0:n, at:at + cols], 2, a.shape[2]), ALU.mult))
                dve.tensor_scalar(wq[m][0:n], tmp, MAGIC, MAGIC, ALU.add, ALU.subtract).then_inc(w_quantized, 1)
                dve.wait_ge(w_quantized, m + 1)
            for c in range(C):
                chain(dve.tensor_scalar(diag[:, c, :], k.ident, wscale[:, 2 * IC + c:2 * IC + c + 1], None, ALU.mult))

            def scale_of(out, inverse, clip, largest):
                chain(dve.tensor_tensor(out, clip, largest, ALU.mult))
                chain(dve.tensor_scalar(out, out, 1.0 / QMAX, None, ALU.mult))
                chain(dve.reciprocal(inverse, out))

            dve.wait_ge(x_max, 1)
            dve.wait_ge(clips, 1)
            scale_of(sx, sxi, sig[:, 0:1], whole[:, 0:1])
            chain(dve.tensor_scalar(sgate[0:IP], wscale[0:IP, 0:IC], sx[0:IP], None, ALU.mult))
            dve.tensor_scalar(sup[0:IP], wscale[0:IP, IC:2 * IC], sx[0:IP], None, ALU.mult).then_inc(scale_ready, 1)
            dve.wait_ge(scale_ready, 1)
            base = chain.n
            per = 2 + 1
            with dve.Fori(0, TURNS) as g:
                c1 = Chain(dve, dve_chain, 0, 0)
                c1.base = base + g * per
                for c in range(C):
                    dve.wait_ge(turned.turned, g * C + c + 1)
                    c1(dve.tensor_scalar(xr[:, c, :], ps[:, 4 + c, :], sxi, MAGIC, ALU.mult, ALU.add))
                dve.tensor_scalar(xr[:, :, :], xr[:, :, :], MAGIC + QMAX, MAGIC - QMAX - 1.0, ALU.min, ALU.max
                                  ).then_inc(x_rounded, 1)
                for i in range(IC):
                    dve.wait_ge(silu_ready, g * IC + i + 1)
                    dve.scalar_tensor_tensor(out=h[0:IP, i, bass.ds(g * N, N)], in0=ps[0:IP, 2 * (i % 2) + 1, :],
                                             scalar=sup[0:IP, i:i + 1], in1=sg[0:IP, i % 2, :],
                                             op0=ALU.mult, op1=ALU.mult).then_inc(h_ready, 1)
                dve.wait_ge(h_ready, (g + 1) * IC)
                c1(dve.tensor_reduce(hmax[0:IP, bass.ds(g, 1)], h[0:IP, :, bass.ds(g * N, N)], AX.XY, ALU.max,
                                     apply_absolute_value=True))
                assert c1.n == per
            chain.n += TURNS * per
            dve.tensor_reduce(part[0:IP, 1:2], hmax[0:IP], AX.X, ALU.max).then_inc(h_measured, 1)
            dve.wait_ge(h_max, 1)
            scale_of(sh, shi, sig[:, 1:2], whole[:, 1:2])
            dve.wait_ge(scales_spread, 1)
            dve.tensor_scalar(down_scale, ps[:, 6, 0:D], sh, None, ALU.mult).then_inc(scale_ready, 1)
            dve.wait_ge(scale_ready, 2)
            base2 = chain.n
            with dve.Fori(0, TURNS) as g:
                per2 = 1 + TILES + norm.chained()
                c2 = Chain(dve, dve_chain, 0, 0)
                c2.base = base2 + g * per2
                norm.wait_added(dve, g * TILES)
                c2(dve.tensor_scalar(hr[0:IP, :, :], h[0:IP, :, bass.ds(g * N, N)], shi[0:IP], MAGIC, ALU.mult, ALU.add))
                dve.tensor_scalar(hr[0:IP, :, :], hr[0:IP, :, :], MAGIC + QMAX, MAGIC - QMAX - 1.0, ALU.min, ALU.max
                                  ).then_inc(h_rounded, 1)
                for u in range(TILES):
                    dve.wait_ge(y_ready, g * TILES + u + 1)
                    y = norm.r[:, u, :]
                    c2(dve.tensor_tensor(y, ps[:, 4 + u % 2, 0:D], down_scale, ALU.mult))
                    norm.add(dve, c2, g, u, y)
                norm.moments(dve, c2, g)
                norm.apply(dve, c2, g)
                assert c2.n == per2
    sem.release()


def ternary_ffn_stage(k):
    stage = "L2_ffn"
    nc, ps, w, A = k.nc, k.psum, k.begin(stage), k.arena
    sem = Semaphores(nc, stage)
    norm = Norm(k, sem, k.X, k.X)
    F = w.gate.shape[2]
    FC = F // P
    ident_ready, w_summed, w_sums = sem("ident_ready"), sem("weights_summed"), sem("weight_sums_ready")
    w_rounded, w_ready = sem("weights_rounded"), sem("weights_ready")
    x_quantized, x_turned, xT_ready = sem("x_quantized"), sem("x_turned"), sem("xT_ready")
    up_ready, silu_ready, h_ready, h_rounded = sem("up_ready"), sem("silu_ready"), sem("h_ready"), sem("h_rounded")
    hq_ready, h_turned, hT_ready = sem("hq_ready"), sem("h_turned"), sem("hT_ready")
    y_ready, dve_chain = sem("y_ready"), sem("dve_chain")

    identb = A(P, dtype=BF16)
    sums, means, wmul = A(3), A(3), A(3)
    mags = A(C * F)
    wr = [A(C * F), A(C * F)]
    wt = [A(C, F, dtype=BF16), A(C, F, dtype=BF16), A(FC, D, dtype=BF16)]
    xm, xmul, xunit = A(TILES), A(TILES), A(TILES)
    gunit, uunit = A(TILES), A(TILES)
    xr, xq = A(TILES, D), A(TILES, D, dtype=BF16)
    xT = A(C, N, dtype=BF16)
    sg, hb = A(F), A(2, F)
    hm, hmul, hunit = A(2), A(2), A(2)
    hq, hT = A(2, F, dtype=BF16), A(2, FC, P, dtype=BF16)
    flat = [w.gate.rearrange("p c f -> p (c f)"), w.up.rearrange("p c f -> p (c f)"), w.down.rearrange("p c f -> p (c f)")]
    x_psum = ps[:, 4, :].bitcast(BF16).rearrange("p (c n) -> p c n", c=C)
    h_psum = ps[:, 5, :].bitcast(BF16).rearrange("p (f t) -> p f t", t=P)

    with nc.Block() as block:
        @block.sync
        def _(sp):
            k.prefetch(sp, stage)

        @block.gpsimd
        def _(pool):
            pool.wait_ge(w_summed, 3)
            pool.partition_all_reduce(means[:, :], sums[:, :], P, SUM).then_inc(w_sums, 1)
            with pool.Fori(0, TURNS) as g:
                norm.roots(pool, g)

        @block.tensor
        def _(pe):
            pe.wait_ge(ident_ready, 1)
            pe.wait_ge(w_ready, 3)
            with pe.Fori(0, TURNS) as g:
                pe.wait_ge(x_quantized, g + 1)
                for c in range(C):
                    for u in range(TILES):
                        mm = nc.tensor.transpose(x_psum[:, c, u * P:(u + 1) * P], xq[:, u, c * P:(c + 1) * P], identb)
                mm.then_inc(x_turned, 1)
                pe.wait_ge(xT_ready, g + 1)

                def down(u):
                    n = g * TILES + u
                    pe.wait_ge(hq_ready, n + 1)
                    for f in range(FC):
                        mm = nc.tensor.transpose(h_psum[:, f, :], hq[:, u % 2, f * P:(f + 1) * P], identb)
                    mm.then_inc(h_turned, 1)
                    pe.wait_ge(hT_ready, n + 1)
                    for f in range(FC):
                        mm = nc.tensor.matmul(ps[:, 6 + u % 2, 0:D], hT[:, u % 2, f, :], wt[2][:, f, :],
                                              start=(f == 0), stop=(f == FC - 1))
                    mm.then_inc(y_ready, 1)

                for u in range(TILES):
                    if u:
                        pe.wait_ge(h_ready, g * TILES + u)
                    for m in range(2):
                        for b in range(F // N):
                            for c in range(C):
                                mm = nc.tensor.matmul(ps[:, 2 * m + b, :], xT[:, c, u * P:(u + 1) * P],
                                                      wt[m][:, c, b * N:(b + 1) * N], start=(c == 0), stop=(c == C - 1))
                    mm.then_inc(up_ready, 1)
                    if u:
                        if u >= 3:
                            norm.wait_added(pe, g * TILES + u - 2)
                        down(u - 1)
                norm.wait_added(pe, g * TILES + TILES - 2)
                down(TILES - 1)

        @block.scalar
        def _(act):
            k.wait_weights(act, stage)
            nc.scalar.copy(identb[:, :], k.ident).then_inc(ident_ready, 1)
            for m in range(3):
                if m:
                    act.wait_ge(w_summed, m)
                nc.scalar.activation(mags, flat[m], ACT.Abs, accum_out=sums[:, m:m + 1]).then_inc(w_summed, 1)
            for m in range(3):
                act.wait_ge(w_rounded, m + 1)
                nc.scalar.activation(wt[m].rearrange("p c f -> p (c f)"), wr[m % 2], ACT.Copy, bias=-MAGIC
                                     ).then_inc(w_ready, 1)
            with act.Fori(0, TURNS) as g:
                act.wait_ge(x_turned, g + 1)
                nc.scalar.copy(xT[:, :, :], x_psum).then_inc(xT_ready, 1)

                def finish(u):
                    n = g * TILES + u
                    act.wait_ge(h_rounded, n + 1)
                    nc.scalar.activation(hq[:, u % 2, :], hb[:, u % 2, :], ACT.Copy, bias=-MAGIC).then_inc(hq_ready, 1)
                    act.wait_ge(h_turned, n + 1)
                    nc.scalar.copy(hT[:, u % 2, :, :], h_psum).then_inc(hT_ready, 1)

                for u in range(TILES):
                    act.wait_ge(up_ready, g * TILES + u + 1)
                    if u:
                        act.wait_ge(h_ready, g * TILES + u)
                    nc.scalar.activation(sg, ps[:, 0:2, :].rearrange("p a b -> p (a b)"), ACT.Silu,
                                         scale=gunit[:, u:u + 1]).then_inc(silu_ready, 1)
                    if u:
                        finish(u - 1)
                finish(TILES - 1)

        @block.vector
        def _(dve):
            k.wait_weights(dve, stage)
            norm.open(dve)
            chain = Chain(dve, dve_chain)
            dve.wait_ge(w_sums, 1)
            chain(dve.tensor_scalar(means, means, 1.0 / (C * P * F), 1e-5, ALU.mult, ALU.max))
            chain(dve.reciprocal(wmul, means))
            for m in range(3):
                if m == 2:
                    dve.wait_ge(w_ready, 1)
                chain(dve.tensor_scalar(wr[m % 2], flat[m], wmul[:, m:m + 1], MAGIC, ALU.mult, ALU.add))
                dve.tensor_scalar(wr[m % 2], wr[m % 2], MAGIC + 1.0, MAGIC - 1.0, ALU.min, ALU.max
                                  ).then_inc(w_rounded, 1)
            base = chain.n
            per = 6 + TILES * 4 + norm.chained()
            with dve.Fori(0, TURNS) as g:
                ch = Chain(dve, dve_chain)
                ch.base = base + g * per
                x = k.X[:, bass.ds(g * TILES, TILES), :]
                ch(dve.tensor_reduce(xm, x, AX.X, ALU.max, apply_absolute_value=True))
                ch(dve.tensor_scalar(xunit, xm, 1e-5, 1.0 / QMAX, ALU.max, ALU.mult))
                ch(dve.reciprocal(xmul, xunit))
                ch(dve.tensor_scalar(gunit, xunit, means[:, 0:1], None, ALU.mult))
                ch(dve.tensor_scalar(uunit, xunit, means[:, 1:2], None, ALU.mult))
                ch(dve.tensor_tensor(xr[:, :, :], x, bc(xmul, 2, D), ALU.mult))
                dve.tensor_scalar(xq[:, :, :], xr[:, :, :], MAGIC, MAGIC, ALU.add, ALU.subtract).then_inc(x_quantized, 1)

                def hidden(u):
                    n = g * TILES + u
                    b = hb[:, u % 2, :]
                    dve.wait_ge(silu_ready, n + 1)
                    dve.scalar_tensor_tensor(out=b, in0=ps[:, 2:4, :].rearrange("p a b -> p (a b)"),
                                             scalar=uunit[:, u:u + 1], in1=sg, op0=ALU.mult, op1=ALU.mult
                                             ).then_inc(h_ready, 1)
                    dve.wait_ge(h_ready, n + 1)
                    q = slice(u % 2, u % 2 + 1)
                    ch(dve.tensor_reduce(hm[:, q], b, AX.X, ALU.max, apply_absolute_value=True))
                    ch(dve.tensor_scalar(hunit[:, q], hm[:, q], 1e-5, 1.0 / QMAX, ALU.max, ALU.mult))
                    ch(dve.reciprocal(hmul[:, q], hunit[:, q]))
                    ch(dve.tensor_scalar(hunit[:, q], hunit[:, q], means[:, 2:3], None, ALU.mult))
                    dve.tensor_scalar(b, b, hmul[:, q], MAGIC, ALU.mult, ALU.add).then_inc(h_rounded, 1)
                    dve.wait_ge(h_rounded, n + 1)

                def finish(u):
                    dve.wait_ge(y_ready, g * TILES + u + 1)
                    norm.add(dve, ch, g, u, ps[:, 6 + u % 2, 0:D], hunit[:, u % 2:u % 2 + 1])

                for u in range(TILES):
                    hidden(u)
                    if u:
                        finish(u - 1)
                finish(TILES - 1)
                norm.moments(dve, ch, g)
                norm.apply(dve, ch, g)
                assert ch.n == per, (ch.n, per)
    sem.release()


def wide_attention_stage(k):
    stage = "L3_attn"
    nc, ps, w, A = k.nc, k.psum, k.begin(stage), k.arena
    sem = Semaphores(nc, stage)
    turned, norm = Turned(k, sem, k.X, 4), Norm(k, sem, k.X, k.X)
    xT = turned.xT
    ones_set, qk_projected, qk_ready = sem("ones_set"), sem("qk_projected"), sem("qk_ready")
    v_projected, v_ready, scores_ready, shifted = sem("v_projected"), sem("v_ready"), sem("scores_ready"), sem("shifted")
    probs_ready, probs_turned, probsT_ready = sem("probs_ready"), sem("probs_turned"), sem("probsT_ready")
    o_ready, dve_chain = sem("o_ready"), sem("dve_chain")
    qkT = A(2 * C, N)
    va = A(TILES, D + 1)
    pr, pT = A(TILES, P), A(TILES, P)
    mx, ri = A(TILES), A(TILES)
    s_psum = ps[:, 4, :].rearrange("p (u t) -> p u t", t=P)
    pT_psum = ps[:, 5, :].rearrange("p (u t) -> p u t", t=P)

    with nc.Block() as block:
        @block.sync
        def _(sp):
            k.prefetch(sp, stage)

        @block.gpsimd
        def _(pool):
            pool.memset(va[:, :, D:D + 1], 1.0).then_inc(ones_set, 1)
            turned.stage(pool, 0)
            with pool.Fori(0, TURNS - 1) as g:
                turned.stage_next(pool, g)
                norm.roots(pool, g)
            norm.roots(pool, TURNS - 1)

        @block.tensor
        def _(pe):
            k.wait_weights(pe, stage)
            pe.wait_ge(ones_set, 1)
            with pe.Fori(0, TURNS) as g:
                turned.turn(pe, g)
                pe.wait_ge(turned.ready, (g + 1) * C)
                norm.wait_added(pe, g * TILES)
                for p, (m, co) in enumerate([(w.wq, 0), (w.wq, 1), (w.wk, 0), (w.wk, 1)]):
                    for ci in range(C):
                        mm = nc.tensor.matmul(ps[:, p, :], m[:, ci, co * P:(co + 1) * P], xT[:, ci, :],
                                              start=(ci == 0), stop=(ci == C - 1))
                    mm.then_inc(qk_projected, 1)
                for u in range(TILES):
                    for ci in range(C):
                        mm = nc.tensor.matmul(ps[:, 6 + u // 2, (u % 2) * D:(u % 2 + 1) * D],
                                              xT[:, ci, u * P:(u + 1) * P], w.wv[:, ci, :],
                                              start=(ci == 0), stop=(ci == C - 1))
                    if u % 2:
                        mm.then_inc(v_projected, 1)
                pe.wait_ge(qk_ready, (g + 1) * 2 * C)
                for u in range(TILES):
                    for ci in range(C):
                        mm = nc.tensor.matmul(s_psum[:, u, :], qkT[:, ci, u * P:(u + 1) * P],
                                              qkT[:, C + ci, u * P:(u + 1) * P], start=(ci == 0), stop=(ci == C - 1))
                mm.then_inc(scores_ready, 1)
                pe.wait_ge(probs_ready, g + 1)
                for u in range(TILES):
                    mm = nc.tensor.transpose(pT_psum[:, u, :], pr[:, u, :], k.ident)
                mm.then_inc(probs_turned, 1)
                pe.wait_ge(probsT_ready, g + 1)
                pe.wait_ge(v_ready, (g + 1) * 2)
                for u in range(TILES):
                    nc.tensor.matmul(ps[:, u, 0:D + 1], pT[:, u, :], va[:, u, :], start=True, stop=True
                                     ).then_inc(o_ready, 1)

        @block.scalar
        def _(act):
            with act.Fori(0, TURNS) as g:
                turned.copy(act, g)
                for p in range(2 * C):
                    act.wait_ge(qk_projected, g * 2 * C + p + 1)
                    nc.scalar.copy(qkT[:, p, :], ps[:, p, :]).then_inc(qk_ready, 1)
                act.wait_ge(shifted, g + 1)
                nc.scalar.activation(pr[:, :, :], pr[:, :, :], ACT.Exp, scale=D ** -0.5).then_inc(probs_ready, 1)
                act.wait_ge(probs_turned, g + 1)
                nc.scalar.copy(pT[:, :, :], pT_psum).then_inc(probsT_ready, 1)

        @block.vector
        def _(dve):
            norm.open(dve)
            with dve.Fori(0, TURNS) as g:
                chain = Chain(dve, dve_chain, g, 1 + TILES + norm.chained())
                for i in range(2):
                    dve.wait_ge(v_projected, g * 2 + i + 1)
                    dve.tensor_copy(va[:, 2 * i:2 * i + 2, 0:D], ps[:, 6 + i, :].rearrange("p (u d) -> p u d", d=D)
                                    ).then_inc(v_ready, 1)
                dve.wait_ge(scores_ready, g + 1)
                chain(dve.tensor_reduce(mx, s_psum, AX.X, ALU.max))
                dve.tensor_tensor(pr[:, :, :], s_psum, bc(mx, 2, P), ALU.subtract).then_inc(shifted, 1)
                for u in range(TILES):
                    dve.wait_ge(o_ready, g * TILES + u + 1)
                    chain(dve.reciprocal(ri[:, u:u + 1], ps[:, u, D:D + 1]))
                    norm.add(dve, chain, g, u, ps[:, u, 0:D], ri[:, u:u + 1])
                norm.moments(dve, chain, g)
                norm.apply(dve, chain, g)
                chain.end()
    sem.release()


def relu_ffn_stage(k):
    stage = "L3_relu"
    nc, ps, w, A = k.nc, k.psum, k.begin(stage), k.arena
    sem = Semaphores(nc, stage)
    turned, norm = Turned(k, sem, k.Y, 4), Norm(k, sem, k.Y, k.Y, w.gain, w.shift)
    biased = Biased(k, sem, k.Y, w.b2)
    outer = Norm(k, lambda name: sem("outer_" + name), k.X, k.X)
    xT = turned.xT
    up_ready, h_ready, y_ready = sem("up_ready"), sem("h_ready"), sem("y_ready")
    dve_chain = sem("dve_chain")
    F = w.w1.shape[2]
    FC = F // P
    h = A(FC, N)

    with nc.Block() as block:
        @block.sync
        def _(sp):
            k.prefetch(sp, stage)

        @block.gpsimd
        def _(pool):
            turned.stage(pool, 0)
            k.wait_weights(pool, stage)
            biased.stage(pool, 0)
            for g in range(TURNS):
                if g + 1 < TURNS:
                    turned.stage_next(pool, g)
                norm.roots(pool, g)
                if g + 1 < TURNS:
                    biased.stage(pool, g + 1)
                outer.roots(pool, g)

        @block.tensor
        def _(pe):
            k.wait_weights(pe, stage)
            with pe.Fori(0, TURNS) as g:
                turned.turn(pe, g)
                pe.wait_ge(turned.ready, (g + 1) * C)
                for f in range(FC):
                    if f >= 4:
                        pe.wait_ge(h_ready, g * FC + f - 3)
                    for c in range(C):
                        mm = nc.tensor.matmul(ps[:, f % 4, :], w.w1[:, c, f * P:(f + 1) * P], xT[:, c, :],
                                              start=(c == 0), stop=(c == C - 1))
                    mm.then_inc(up_ready, 1)
                pe.wait_ge(h_ready, (g + 1) * FC)
                for u in range(TILES):
                    y = ps[:, 6 + u % 2, 0:D]
                    norm.wait_added(pe, g * TILES + u - 1 if u >= 2 else g * TILES)
                    for f in range(FC):
                        mm = nc.tensor.matmul(y, h[:, f, u * P:(u + 1) * P], w.w2[:, f, :], start=(f == 0),
                                              stop=(f == FC - 1))
                    mm.then_inc(y_ready, 1)

        @block.scalar
        def _(act):
            k.wait_weights(act, stage)
            with act.Fori(0, TURNS) as g:
                turned.copy(act, g)
                for f in range(FC):
                    act.wait_ge(up_ready, g * FC + f + 1)
                    nc.scalar.activation(h[:, f, :], ps[:, f % 4, :], ACT.Relu, bias=w.b1[:, f:f + 1]
                                         ).then_inc(h_ready, 1)

        @block.vector
        def _(dve):
            k.wait_weights(dve, stage)
            norm.open(dve)
            outer.open(dve)
            with dve.Fori(0, TURNS) as g:
                chain = Chain(dve, dve_chain, g, norm.chained() + outer.chained())
                for u in range(TILES):
                    dve.wait_ge(y_ready, g * TILES + u + 1)
                    norm.add(dve, chain, g, u, ps[:, 6 + u % 2, 0:D], x=biased.tile(dve, g, u))
                norm.moments(dve, chain, g)
                norm.apply(dve, chain, g)
                for u in range(TILES):
                    outer.add(dve, chain, g, u, k.Y[:, bass.ds(g * TILES + u, 1), :].rearrange("p a d -> p (a d)"))
                outer.moments(dve, chain, g)
                outer.apply(dve, chain, g)
                chain.end()
    sem.release()



def by_rows(a):
    a = np.asarray(a)
    return a.reshape(a.shape[0] // P, P, -1).transpose(1, 0, 2)


def col(b):
    return np.asarray(b).reshape(-1, P).T


def row(b):
    return np.broadcast_to(np.asarray(b).reshape(1, -1), (P, np.asarray(b).size))


def heads_mask():
    return (np.arange(P)[:, None] // DH == np.arange(HH)[None, :]).astype(np.float32)


def causal_mask(value):
    return np.where(np.tril(np.ones((P, P), bool)), 0.0, value).astype(np.float32)


def rope_tables():
    inv = (1.0 / 10000.0 ** (np.arange(0, DH, 2, dtype=np.float32) / DH)).astype(np.float32)
    f = np.arange(P, dtype=np.float32)[:, None] * inv[None, :]
    sin, cos = np.sin(f).T.astype(np.float32), np.cos(f).T.astype(np.float32)
    sin = np.stack([-sin, sin], 1).reshape(DH, P)
    return np.tile(np.repeat(cos, 2, 0), (HH, 1)), np.tile(sin, (HH, 1))


def swap_pairs(a):
    return np.asarray(a).reshape(-1, 2, *np.asarray(a).shape[1:])[:, ::-1].reshape(np.asarray(a).shape)


def pack_L1_attn(i):
    wq, wk, wv = np.split(np.asarray(i["L1_attn_w_qkv"]), 3, 0)
    bq, bk, bv = np.split(np.asarray(i["L1_attn_b_qkv"]), 3, 0)
    cos, sin = rope_tables()
    return dict(wq=by_rows(wq.T), wqs=by_rows(swap_pairs(wq).T), wk=by_rows(wk.T), wks=by_rows(swap_pairs(wk).T),
                wv=by_rows(wv.T), wo=by_rows(np.asarray(i["L1_attn_w_out"]).T), bq=col(bq), bqs=col(swap_pairs(bq)),
                bk=col(bk), bks=col(swap_pairs(bk)), bv=col(bv), bo=row(i["L1_attn_b_out"]), cos=cos, sin=sin,
                heads=heads_mask(), causal=causal_mask(-1e30))


def pack_L1_xattn(i):
    t = {n: by_rows(np.asarray(i["L1_xattn_W" + n]).T) for n in "qkvo"}
    return dict(wq=t["q"], wk=t["k"], wv=t["v"], wo=t["o"], bq=col(i["L1_xattn_bq"]), bk=col(i["L1_xattn_bk"]),
                bv=col(i["L1_xattn_bv"]), bo=row(i["L1_xattn_bo"]), heads=heads_mask())


def pack_L3(i, which):
    W = np.asarray(i[f"L3_xattn_Wq_{which}"]).transpose(1, 0, 2).reshape(D, D)
    b = np.asarray(i[f"L3_xattn_bq_{which}"]).reshape(-1)
    n = "1" if which == "self" else "2"
    out = dict(wq=by_rows(W), bq=col(b), bv_row=row(b), gain=row(i["L3_xattn_g" + n]),
               shift=row(i["L3_xattn_beta" + n]), heads=heads_mask())
    if which == "self":
        out["causal"] = causal_mask(-1e9)
    return out


PACKS = {
    "L1_attn": pack_L1_attn,
    "L1_xattn": pack_L1_xattn,
    "L3_self": lambda i: pack_L3(i, "self"),
    "L3_cross": lambda i: pack_L3(i, "cross"),
}
ALIASES = {"L3_self": dict(wk="wq", wv="wq", bk="bq"), "L3_cross": dict(wk="wq", wv="wq", bk="bq")}


def pack_L0_attn(i):
    a = {n: np.asarray(i["L0_attn_" + n]) for n in
         ("Wq", "Wk", "Wv", "Wg", "Wo", "Wbeta", "Wtg", "mode_logits", "log_decay", "omega_log_scale")}
    DK, M = 64, 8
    j, d = np.arange(P), np.arange(P)
    partner = np.where(d % DK < DK // 2, d + DK // 2, d - DK // 2)
    swap = np.zeros((P, P), np.float32)
    swap[partner, d] = np.where(d % DK < DK // 2, 1.0, -1.0)
    inv_freq = (1.0 / 10000.0 ** (np.arange(0, DK, 2, dtype=np.float32) / DK)).astype(np.float32)
    omega = a["omega_log_scale"].reshape(-1, 2, M)
    return dict(wq=by_rows(a["Wq"]), wk=by_rows(a["Wk"]), wv=by_rows(a["Wv"]), wg=by_rows(a["Wg"]), wo=by_rows(a["Wo"]),
                wbt=by_rows(np.concatenate([a["Wbeta"], a["Wtg"]], 1)), swap=swap,
                after=(j[:, None] > j[None, :]).astype(np.float32), incl=(j[:, None] <= j[None, :]).astype(np.float32),
                position=row(np.arange(P, dtype=np.float32)), inv_freq=inv_freq[d % (DK // 2)][:, None],
                omega=omega.transpose(1, 0, 2)[d // DK], log_decay=row(a["log_decay"].reshape(-1)),
                modes=np.broadcast_to(a["mode_logits"], (P, *a["mode_logits"].shape)))


PACKS["L0_attn"] = pack_L0_attn


def before_matrix(n):
    return np.broadcast_to(np.tril(np.ones((n, n), np.float32), -1), (P, n, n))


PACKS["L0_ffn"] = lambda i: dict(wg=by_rows(i["L0_ffn_Wg"]), bg=row(i["L0_ffn_bg"]), before=before_matrix(8),
                                 b2=np.concatenate([np.asarray(i["L0_ffn_b2"]), np.zeros((P - 8, D), np.float32)]))
PACKS["L3_ffn"] = lambda i: dict(wg=by_rows(np.asarray(i["L3_ffn_w_gate"]).T), before=before_matrix(16))


def flat_experts(*parts):
    return np.concatenate([np.asarray(p).reshape(*np.asarray(p).shape[:2], -1) for p in parts], 2)


def stream_L0(i):
    w1, w2 = np.asarray(i["L0_ffn_W1"]), np.asarray(i["L0_ffn_W2"])
    b1 = np.asarray(i["L0_ffn_b1"])
    E = w1.shape[0]
    return {"experts_L0_ffn": np.ascontiguousarray(flat_experts(
        w1.reshape(E, C, P, -1).transpose(0, 2, 1, 3), w2.reshape(E, -1, P, D).transpose(0, 2, 1, 3),
        b1.reshape(E, -1, P).transpose(0, 2, 1)))}


def stream_L3(i):
    up = [np.concatenate([np.asarray(i[f"L3_ffn_{n}_e"]), np.asarray(i[f"L3_ffn_{n}_s"]).reshape(-1, P, D)])
          for n in ("w1", "w3")]
    shared2 = np.asarray(i["L3_ffn_w2_s"]).reshape(D, -1, P).transpose(1, 0, 2)
    w2 = np.concatenate([np.asarray(i["L3_ffn_w2_e"]), shared2])
    E = w2.shape[0]
    return {"experts_L3_ffn": np.ascontiguousarray(flat_experts(
        *(a.transpose(0, 2, 1).reshape(E, C, P, P).transpose(0, 2, 1, 3) for a in up), w2.transpose(0, 2, 1)))}


STREAMS = {"L0_ffn": stream_L0, "L3_ffn": stream_L3}


def same_head():
    h = np.arange(P) // DH
    return (h[:, None] == h[None, :]).astype(np.float32)


def pack_L0_xattn(i):
    t = {n: by_rows(np.asarray(i["L0_xattn_W" + n]).T) for n in "qkvo"}
    return dict(wq=t["q"], wk=t["k"], wv=t["v"], wo=t["o"], bq=col(i["L0_xattn_bq"]), bk=row(i["L0_xattn_bk"]),
                bv=row(i["L0_xattn_bv"]), bo=row(i["L0_xattn_bo"]), blocks=same_head())


def pack_L2_recall(i):
    wkv = np.asarray(i["L2_xattn_Wkv"])
    return dict(wq=by_rows(np.asarray(i["L2_xattn_Wq"]).T),
                wkv=by_rows(np.concatenate([np.tile(wkv[:DH].T, (1, HH)), wkv[DH:].T], 1)),
                countdown=row(np.arange(P, 0, -1, dtype=np.float32)))


def pack_L2_xattn(i):
    return dict(wq=by_rows(np.asarray(i["L2_xattn_Wq"]).T), wo=by_rows(np.asarray(i["L2_xattn_Wc"]).T),
                heads=heads_mask())


def pack_L2_attn(i):
    f, t = np.arange(P)[:, None], np.arange(P)[None, :]
    angle = 2 * np.pi * ((f * t) % P) / P
    weight = np.where(f > P // 2, 0.0, np.where(f % (P // 2) == 0, 1.0, 2.0)) / P
    out = {"w" + n: by_rows(i["L2_attn_W" + n]) for n in "qkvo"}
    out.update({"b" + n: row(i["L2_attn_b" + n]) for n in "qkvo"})
    FR = P // 2 + 1
    return dict(out, dcos=np.cos(angle.T[:, :FR]).astype(np.float32), dsin=np.sin(angle.T[:, :FR]).astype(np.float32),
                icos=(weight * np.cos(angle)).astype(np.float32), isin=(-weight * np.sin(angle)).astype(np.float32),
                blocks=same_head())


PACKS.update(L0_xattn=pack_L0_xattn, L2_recall=pack_L2_recall, L2_xattn=pack_L2_xattn, L2_attn=pack_L2_attn)


def row_chunks(a, n):
    a = np.asarray(a).reshape(-1, n, a.shape[-1]).transpose(1, 0, 2)
    return np.concatenate([a, np.zeros((P - n, *a.shape[1:]), a.dtype)])


PACKS["L1_ffn"] = lambda i: dict(gate=row_chunks(i["L1_ffn_w_gate"], 88), up=row_chunks(i["L1_ffn_w_up"], 88),
                                 down=by_rows(i["L1_ffn_w_down"]),
                                 clip=np.concatenate([row(i["L1_ffn_clip_x"]), row(i["L1_ffn_clip_down"])], 1))
PACKS["L2_ffn"] = lambda i: dict(gate=by_rows(np.asarray(i["L2_ffn_w_gate"]).T), up=by_rows(np.asarray(i["L2_ffn_w_up"]).T),
                                 down=by_rows(np.asarray(i["L2_ffn_w_down"]).T))


PACKS["L3_attn"] = lambda i: {"w" + n: by_rows(np.asarray(i["L3_attn_W" + n]).T) for n in "qkv"}
PACKS["L3_relu"] = lambda i: dict(w1=by_rows(i["L3_xattn_w1"]), w2=by_rows(i["L3_xattn_w2"]), b1=col(i["L3_xattn_b1"]),
                                  b2=row(i["L3_xattn_b2"]), gain=row(i["L3_xattn_g3"]), shift=row(i["L3_xattn_beta3"]))


class Weights(dict):
    __getattr__ = dict.__getitem__


class Kernel:

    def __init__(self, nc, ctx, dram, shapes, stages):
        self.nc, self.dram, self.shapes, self.stages = nc, dram, shapes, stages

        def sb(name, words):
            return ctx.enter_context(nc.sbuf_tensor(name, [P, words], F32))

        self.X = sb("X", B * D)[:, :].rearrange("p (b d) -> p b d", d=D)
        self.Y = sb("Y", B * D)[:, :].rearrange("p (b d) -> p b d", d=D)
        self.ident = sb("ident", P)[:, :]
        self.eps = sb("eps", TILES)[:, :]
        self.minus_half = sb("minus_half", TILES)[:, :]
        self.regions = [sb(f"weights_{i}", REGION) for i in range(2)]
        self.arena = Arena(sb("arena", ARENA), ARENA)
        self.psum = ctx.enter_context(nc.psum_tensor("psum", [P, BANKS, N], F32))
        self.arrived = {s: nc.alloc_semaphore(f"{s}_weights_arrived") for s in stages}
        self.const_arrived = nc.alloc_semaphore("constants_arrived")
        if "ctxT" in dram:
            self.ctxT = dram["ctxT"]
        if "maskb" in dram:
            self.maskb = dram["maskb"]

    def words(self, stage):
        return sum(n for _, n, _ in self.shapes[stage])

    def load(self, sp, stage):
        n = self.words(stage)
        if n:
            to = self.regions[self.stages.index(stage) % 2]
            sp.dma_start(to[:, 0:n], self.dram["w_" + stage]).then_inc(self.arrived[stage], 16)

    def next_region(self, stage):
        return self.regions[(self.stages.index(stage) + 1) % 2]

    def prefetch(self, sp, stage):
        at = self.stages.index(stage) + 1
        if at < len(self.stages):
            self.load(sp, self.stages[at])

    def wait_weights(self, eng, stage):
        eng.wait_ge(self.const_arrived, 16)
        if self.words(stage):
            eng.wait_ge(self.arrived[stage], 16)

    def begin(self, stage):
        self.arena.reset()
        w, at = Weights(), 0
        region = self.regions[self.stages.index(stage) % 2]
        for name, n, dims in self.shapes[stage]:
            ap = region[:, at:at + n]
            if len(dims) > 1:
                letters = "abcd"[:len(dims)]
                ap = ap.rearrange("p (%s) -> p %s" % (" ".join(letters), " ".join(letters)),
                                  **dict(zip(letters[1:], dims[1:])))
            w[name] = ap
            at += n
        for new, old in ALIASES.get(stage, {}).items():
            w[new] = w[old]
        return w


RUN = {
    "L0_attn": lambda k: delta_stage(k),
    "L0_xattn": lambda k: linear_attention_stage(k),
    "L0_ffn": lambda k: experts_stage(k, "L0_ffn"),
    "L1_attn": lambda k: attention_stage(k, "L1_attn", k.X, k.X, rope=True, mask="causal"),
    "L1_xattn": lambda k: attention_stage(k, "L1_xattn", k.X, k.X, cross=True, mask="batch"),
    "L1_ffn": lambda k: int8_ffn_stage(k),
    "L2_attn": lambda k: correlation_stage(k),
    "L2_recall": lambda k: recall_stage(k),
    "L2_xattn": lambda k: attention_stage(k, "L2_xattn", k.X, k.X, recalled=True),
    "L2_ffn": lambda k: ternary_ffn_stage(k),
    "L3_attn": lambda k: wide_attention_stage(k),
    "L3_self": lambda k: attention_stage(k, "L3_self", k.X, k.Y, mask="causal", affine=True, out_proj=False),
    "L3_cross": lambda k: attention_stage(k, "L3_cross", k.Y, k.Y, cross=True, affine=True, out_proj=False),
    "L3_relu": lambda k: relu_ffn_stage(k),
    "L3_ffn": lambda k: experts_stage(k, "L3_ffn"),
}
STAGES = list(RUN)
REGION = 7168
ARENA = 30528


def program(nc, dram, out, shapes, stages=STAGES):
    with ExitStack() as ctx:
        k = Kernel(nc, ctx, dram, shapes, stages)
        x_in = dram["x"]
        with nc.Block() as block:
            @block.gpsimd
            def _(pool):
                pool.memset(k.minus_half, -0.5)
                pool.memset(k.eps, LN_EPS)

            @block.sync
            def _(sp):
                sp.dma_start(k.X[:, :, :], x_in.rearrange("b t d -> t b d")).then_inc(k.const_arrived, 16)
                sp.dma_start(k.ident[:, :], dram["ident"]).then_inc(k.const_arrived, 16)
                k.load(sp, stages[0])
                sp.wait_ge(k.const_arrived, 32)
        for s in stages:
            RUN[s](k)
        written = nc.alloc_semaphore("out_written")
        with nc.Block() as block:
            @block.sync
            def _(sp):
                sp.dma_start(out.rearrange("b t d -> t b d"), k.X[:, :, :]).then_inc(written, 16)
                sp.wait_ge(written, 16)


def lay_out(inputs, stages):
    arrays, shapes = {"x": np.ascontiguousarray(inputs["x"]), "ident": np.eye(P, dtype=np.float32)}, {}
    ctx = np.asarray(inputs["ctx_1024"])
    arrays["ctxT"] = np.ascontiguousarray(
        ctx.reshape(TURNS, TILES, P, C, P).transpose(0, 4, 3, 1, 2).reshape(TURNS, P, C, N))
    arrays["maskb"] = np.ascontiguousarray(
        np.asarray(inputs["mask_BxSxS2_ff0"]).reshape(TURNS, TILES, P, P).transpose(0, 2, 1, 3))
    arrays["padding"] = np.ascontiguousarray(np.asarray(inputs["mask_BxS2_bk1"]).T)
    for s in stages:
        packed = PACKS[s](inputs)
        shapes[s] = [(n, int(np.prod(a.shape[1:])), a.shape[1:]) for n, a in packed.items()]
        if packed:
            arrays["w_" + s] = np.ascontiguousarray(
                np.concatenate([np.asarray(a).reshape(P, -1) for a in packed.values()], 1))
    for s in stages:
        if s in STREAMS:
            arrays.update(STREAMS[s](inputs))
    return arrays, shapes


def kernel(**inputs):
    import numpy as _np
    import concourse.bacc as _bacc
    from concourse.bass_utils import run_bass_kernel_spmd as _run

    nc = _bacc.Bacc("TRN2", target_bir_lowering=False, num_devices=1)
    arrays, shapes = lay_out(inputs, STAGES)
    dram = {n: nc.dram_tensor(f"in_{n}", a.shape, mybir.dt.from_np(a.dtype), kind="ExternalInput").ap()
            for n, a in arrays.items()}
    out = nc.dram_tensor("out", (B, P, D), F32, kind="ExternalOutput").ap()
    program(nc, dram, out, shapes)
    r = _run(nc, [{f"in_{n}": a for n, a in arrays.items()}], core_ids=[0])
    return r.results[0]["out"]
```
